# Optimizing a Trainium2 kernel written in Bass

```python
import numpy as np
import jax
import jax.numpy as jnp

def _softmax(x, axis=-1):
    return jax.nn.softmax(x, axis=axis)

def _gelu(x):
    return jax.nn.gelu(x, approximate=True)

def _silu(x):
    return jax.nn.silu(x)

def _sigmoid(x):
    return jax.nn.sigmoid(x)

def _layernorm(x, axis=-1, eps=1e-05):
    m = jnp.mean(x, axis=axis, keepdims=True)
    v = jnp.var(x, axis=axis, keepdims=True)
    return (x - m) / jnp.sqrt(v + eps)

def _scatter_add(tgt, idx, src, axis=0):
    return tgt.at[idx].add(src)

def _segment_sum(src, seg, n):
    return jax.ops.segment_sum(src, seg, n)
kernel_name = 'mk_vit_tower_d1_tok_img2048_r4_d8a93a'

def setup_inputs(seed: int=0):
    np.random.seed(seed)
    _w = jnp.asarray

    def _rec_inputs():
        import jax
        import jax.numpy as jnp
        _rk = jax.random.key(seed)
        x = -0.0043416 + 0.998921 * jax.random.normal(jax.random.fold_in(_rk, 1), (64, 64, 64, 2), jnp.float32)
        return x
    x = _rec_inputs()

    def _L0_tok_setup():
        import jax, jax.numpy as jnp
        import numpy as np
        H, N, CH = (64, 64, 1)

        def _r2c(x):
            return x[..., 0] + 1j * x[..., 1]

        def _bilinear(dt, Ac, Bc):
            n = Ac.shape[-1]
            I = jnp.eye(n, dtype=Ac.dtype)
            half = (dt.astype(Ac.real.dtype) / 2)[:, None]
            A_back = I - half * Ac
            A_fwd = I + half * Ac
            dB = dt.astype(Ac.dtype) * jnp.linalg.solve(A_back, Bc[..., None])[..., 0]
            dA = jnp.linalg.solve(A_back, A_fwd)
            return (dA, dB)

        def _krylov(L, dA, dB):
            x = dB[..., None]
            A_ = dA
            while x.shape[-1] < L:
                x = jnp.concatenate([x, jnp.einsum('hnm,hml->hnl', A_, x)], axis=-1)
                A_ = A_ @ A_
            return x[..., :L]
        key = jax.random.key(seed)
        kA, kB, kC, kdt = jax.random.split(key, 4)
        M = jax.random.normal(kA, (H, N, N, 2), dtype=jnp.float32) / np.float32(np.sqrt(N))
        Mc = _r2c(M)
        Ac = 0.5 * (Mc - jnp.conjugate(jnp.swapaxes(Mc, -1, -2))) - 0.5 * jnp.eye(N, dtype=Mc.dtype)
        A = jnp.stack([Ac.real, Ac.imag], axis=-1)
        B = jax.random.normal(kB, (H, N, 2), dtype=jnp.float32)
        C = jax.random.normal(kC, (CH, H, N, 2), dtype=jnp.float32)
        log_dt = jax.random.uniform(kdt, (H, 1), dtype=jnp.float32, minval=np.float32(np.log(0.001)), maxval=np.float32(np.log(0.1)))
        return {'A': A, 'B': B, 'C': C, 'log_dt': log_dt, 'L': 512}
    _L0_tok_all = _L0_tok_setup()
    _L0_tok_in = {k: v for k, v in _L0_tok_all.items() if k in ('A', 'B', 'log_dt')}
    del _L0_tok_all

    def _L0_attn_setup():
        import jax, jax.numpy as jnp
        import numpy as np
        B, T, C = (4, 512, 512)
        N_HEAD = 16
        QK_HD = 128
        VO_HD = 128
        W_STD = 0.02
        key = jax.random.key(seed)
        ks = jax.random.split(key, 5)
        x = jax.random.normal(ks[0], (B, T, C), dtype=jnp.float32)
        Wq = jax.random.normal(ks[1], (N_HEAD * QK_HD, C), dtype=jnp.float32) * W_STD
        Wk = jax.random.normal(ks[2], (N_HEAD * QK_HD, C), dtype=jnp.float32) * W_STD
        Wv = jax.random.normal(ks[3], (N_HEAD * VO_HD, C), dtype=jnp.float32) * W_STD
        Wo = jax.random.normal(ks[4], (C, N_HEAD * VO_HD), dtype=jnp.float32) * W_STD
        return {'x': x, 'Wq': Wq, 'Wk': Wk, 'Wv': Wv, 'Wo': Wo}
    _L0_attn_all = _L0_attn_setup()
    _L0_attn_in = {k: v for k, v in _L0_attn_all.items() if k in ('Wq', 'Wk', 'Wv', 'Wo')}
    del _L0_attn_all

    def _L0_ffn_setup():
        import jax, jax.numpy as jnp
        import numpy as np
        B, S, D = (4, 512, 512)
        E = 8
        N_SHARE = 2
        N_ROUTED = E - N_SHARE
        H = 2048 // E
        key = jax.random.key(seed)
        ks = jax.random.split(key, 12)
        s = 0.02
        return {'x': jax.random.normal(ks[0], (B, S, D), jnp.float32), 'Wg': jax.random.normal(ks[1], (D, E), jnp.float32) * s, 'bg': jnp.zeros((E,), jnp.float32), 'Wgate': jax.random.normal(ks[2], (N_ROUTED, D, H), jnp.float32) * s, 'bgate': jnp.zeros((N_ROUTED, H), jnp.float32), 'Wup': jax.random.normal(ks[3], (N_ROUTED, D, H), jnp.float32) * s, 'bup': jnp.zeros((N_ROUTED, H), jnp.float32), 'Wdown': jax.random.normal(ks[4], (N_ROUTED, H, D), jnp.float32) * s, 'bdown': jnp.zeros((N_ROUTED, D), jnp.float32), 'Ws_up': jax.random.normal(ks[5], (D, N_SHARE * H), jnp.float32) * s, 'bs_up': jnp.zeros((N_SHARE * H,), jnp.float32), 'Ws_down': jax.random.normal(ks[6], (N_SHARE * H, D), jnp.float32) * s, 'bs_down': jnp.zeros((D,), jnp.float32)}
    _L0_ffn_all = _L0_ffn_setup()
    _L0_ffn_in = {k: v for k, v in _L0_ffn_all.items() if k in ('Wg', 'bg', 'Wgate', 'bgate', 'Wup', 'bup', 'Wdown', 'bdown', 'Ws_up', 'bs_up', 'Ws_down', 'bs_down')}
    del _L0_ffn_all
    return {'x': x, 'L0_tok_A': _L0_tok_in['A'], 'L0_tok_B': _L0_tok_in['B'], 'L0_tok_log_dt': _L0_tok_in['log_dt'], 'L0_attn_Wq': _L0_attn_in['Wq'], 'L0_attn_Wk': _L0_attn_in['Wk'], 'L0_attn_Wv': _L0_attn_in['Wv'], 'L0_attn_Wo': _L0_attn_in['Wo'], 'L0_ffn_Wg': _L0_ffn_in['Wg'], 'L0_ffn_bg': _L0_ffn_in['bg'], 'L0_ffn_Wgate': _L0_ffn_in['Wgate'], 'L0_ffn_bgate': _L0_ffn_in['bgate'], 'L0_ffn_Wup': _L0_ffn_in['Wup'], 'L0_ffn_bup': _L0_ffn_in['bup'], 'L0_ffn_Wdown': _L0_ffn_in['Wdown'], 'L0_ffn_bdown': _L0_ffn_in['bdown'], 'L0_ffn_Ws_up': _L0_ffn_in['Ws_up'], 'L0_ffn_bs_up': _L0_ffn_in['bs_up'], 'L0_ffn_Ws_down': _L0_ffn_in['Ws_down'], 'L0_ffn_bs_down': _L0_ffn_in['bs_down']}

def reference(x, L0_tok_A, L0_tok_B, L0_tok_log_dt, L0_attn_Wq, L0_attn_Wk, L0_attn_Wv, L0_attn_Wo, L0_ffn_Wg, L0_ffn_bg, L0_ffn_Wgate, L0_ffn_bgate, L0_ffn_Wup, L0_ffn_bup, L0_ffn_Wdown, L0_ffn_bdown, L0_ffn_Ws_up, L0_ffn_bs_up, L0_ffn_Ws_down, L0_ffn_bs_down):
    import jax
    import jax.numpy as jnp

    def _L0_tok_ref(A, B, C, log_dt, L):
        import jax, jax.numpy as jnp
        import numpy as np
        H, N, CH = (64, 64, 1)

        def _r2c(x):
            return x[..., 0] + 1j * x[..., 1]

        def _bilinear(dt, Ac, Bc):
            n = Ac.shape[-1]
            I = jnp.eye(n, dtype=Ac.dtype)
            half = (dt.astype(Ac.real.dtype) / 2)[:, None]
            A_back = I - half * Ac
            A_fwd = I + half * Ac
            dB = dt.astype(Ac.dtype) * jnp.linalg.solve(A_back, Bc[..., None])[..., 0]
            dA = jnp.linalg.solve(A_back, A_fwd)
            return (dA, dB)

        def _krylov(L, dA, dB):
            x = dB[..., None]
            A_ = dA
            while x.shape[-1] < L:
                x = jnp.concatenate([x, jnp.einsum('hnm,hml->hnl', A_, x)], axis=-1)
                A_ = A_ @ A_
            return x[..., :L]
        Ac, Bc, Cc = (_r2c(A), _r2c(B), _r2c(C))
        dt = jnp.exp(log_dt)
        dA, dB = _bilinear(dt, Ac, Bc)
        x = _krylov(L, dA, dB)
        k = jnp.einsum('chn,hnl->chl', Cc, x).real.astype(jnp.float32)
        return k

    def _L0_attn_ref(x, Wq, Wk, Wv, Wo):
        import jax, jax.numpy as jnp
        import numpy as np
        B, T, C = (4, 512, 512)
        N_HEAD = 16
        QK_HD = 128
        VO_HD = 128
        W_STD = 0.02
        b, t, c = x.shape
        q = (x @ Wq.T).reshape(b, t, N_HEAD, QK_HD).transpose(0, 2, 1, 3)
        k = (x @ Wk.T).reshape(b, t, N_HEAD, QK_HD).transpose(0, 2, 1, 3)
        v = (x @ Wv.T).reshape(b, t, N_HEAD, VO_HD).transpose(0, 2, 1, 3)
        scale = 1.0 / jnp.sqrt(jnp.asarray(QK_HD, dtype=x.dtype))
        att = jnp.einsum('bhqd,bhkd->bhqk', q, k) * scale
        causal = jnp.tril(jnp.ones((t, t), dtype=bool))
        att = jnp.where(causal, att, jnp.asarray(-jnp.inf, dtype=att.dtype))
        att = jax.nn.softmax(att, axis=-1)
        y = jnp.einsum('bhqk,bhkd->bhqd', att, v)
        y = y.transpose(0, 2, 1, 3).reshape(b, t, N_HEAD * VO_HD)
        return y @ Wo.T

    def _L0_ffn_ref(x, Wg, bg, Wgate, bgate, Wup, bup, Wdown, bdown, Ws_up, bs_up, Ws_down, bs_down):
        import jax, jax.numpy as jnp
        import numpy as np
        B, S, D = (4, 512, 512)
        E = 8
        N_SHARE = 2
        N_ROUTED = E - N_SHARE
        H = 2048 // E
        b, s, d = x.shape
        T = b * s
        n = Wgate.shape[0]
        xf = x.reshape(T, d)
        gate = xf @ Wg + bg
        vals, ids = jax.lax.top_k(gate, n)
        rows = jnp.arange(T)[:, None]
        masked = jnp.full_like(gate, -jnp.inf).at[rows, ids].set(vals)
        probs = jax.nn.softmax(masked, axis=-1)
        routed_mask = (ids[:, :, None] == jnp.arange(n)).any(axis=1)
        w = probs[:, :n] * routed_mask
        g = jnp.einsum('td,ndh->tnh', xf, Wgate) + bgate
        u = jnp.einsum('td,ndh->tnh', xf, Wup) + bup
        h = jax.nn.silu(g) * u
        eo = jnp.einsum('tnh,nhd->tnd', h, Wdown) + bdown
        routed_out = jnp.einsum('tnd,tn->td', eo, w)
        share = jax.nn.silu(xf @ Ws_up + bs_up) @ Ws_down + bs_down
        return (routed_out + share).reshape(b, s, d)
    h = _L0_tok_ref(L0_tok_A, L0_tok_B, x, L0_tok_log_dt, 512)
    h = h + _L0_attn_ref(_layernorm(h, axis=-1), L0_attn_Wq, L0_attn_Wk, L0_attn_Wv, L0_attn_Wo)
    h = h + _L0_ffn_ref(_layernorm(h, axis=-1), L0_ffn_Wg, L0_ffn_bg, L0_ffn_Wgate, L0_ffn_bgate, L0_ffn_Wup, L0_ffn_bup, L0_ffn_Wdown, L0_ffn_bdown, L0_ffn_Ws_up, L0_ffn_bs_up, L0_ffn_Ws_down, L0_ffn_bs_down)
    return h

_drawn_inputs = setup_inputs


def setup_inputs(seed=0):
    import zlib

    import numpy as np

    out = dict(_drawn_inputs(seed))
    spreads = {'L0_ffn_bg': (0.0, 0.343),
     'L0_ffn_bgate': (0.0, 0.542),
     'L0_ffn_bup': (0.0, 0.553),
     'L0_ffn_bdown': (0.0, 0.1),
     'L0_ffn_bs_up': (0.0, 0.1),
     'L0_ffn_bs_down': (0.0, 0.1)}
    factors = {}
    for name, (base, spread) in spreads.items():
        noise = np.random.default_rng([zlib.crc32(name.encode()), seed]).standard_normal(out[name].shape)
        drawn = base * np.exp(spread * noise) if base else spread * noise
        out[name] = jnp.asarray(drawn.astype(out[name].dtype))
    for name, factor in factors.items():
        out[name] = (out[name] * factor).astype(out[name].dtype)
    return out
```

```python
from contextlib import ExitStack

import numpy as np

import concourse.bass as bass
from concourse import mybir

f32 = mybir.dt.float32
f32r = mybir.dt.float32r
ALU = mybir.AluOpType
ACT = mybir.ActivationFunctionType
AX = mybir.AxisListType.X

P = 128
HD, NS, SEQ, CH = 64, 64, 512, 64
QH, GH = 16, 4
NQ, NG = HD // QH, QH // GH
INV = 10
DBL = 8
XC = 2 ** DBL
D, NHEAD, DH = 512, 16, 128
KC = D // P
TOK = CH * HD
HALVES = 2
TH = TOK // HALVES
TG = 512
NTG, TPG = TH // TG, TG // P
NT = TH // P
T = HD
NEXP, TOPK, HID = 8, 6, 256
NSH = 2
HC = HID // P
ITEMS = NHEAD + TOPK + NSH
SCALE = float(DH) ** -0.5
MASKED = -1e30
EPS = 1e-5
WCOLS = 2 * KC * HID + HC * D
ACOLS = 3 * KC * DH + D
SCOLS = KC * HID + HC * D


class Steps:

    def __init__(self, names):
        self.at = {n: i + 1 for i, n in enumerate(names)}
        self.n = len(names)

    def after(self, q, *name):
        return q * self.n + self.at[name]


def ssm_steps():
    G = range(NG)
    pe = [("G", g) for g in G]
    dve = [("B",)] + [("G", g) for g in G] + [("rowsum",), ("M",), ("Q",)]
    act = [("B",)] + [("G", g) for g in G]
    for k in range(INV):
        pe += [("N", k, g) for g in G]
        dve += [(x, k, g) for g in G for x in ("S", "N") if x == "N" or k < INV - 1]
        if k < INV - 1:
            act += [("N", k, g) for g in G]
    dve += [("P", g) for g in G]
    act += [("P", g) for g in G]
    pe += [("T", 0, g) for g in G] + [("b", g) for g in G]
    dve += [("T", 0, g) for g in G]
    dve += [(x, g) for g in G for x in ("b+", "b")]
    for j in range(DBL):
        pe += [("K", j, g) for g in G]
        dve += [("K", j, g) for g in G]
        act += [(x, j, g) for g in G for x in ("K", "X")]
        if j < DBL - 1:
            pe += [("T", j + 1, g) for g in G]
            dve += [("T", j + 1, g) for g in G]
    pe += [("Y", g) for g in G] + [("F", g) for g in G]
    dve += [("C",)] + [("F", g) for g in G]
    act += [("Y", g) for g in G] + [("F", g) for g in G]
    return Steps(pe), Steps(dve), Steps(act)


def ssm_program(nc, ins, hbuf, m, s):
    PE, DV, AC = ssm_steps()
    SR = m["zmat"]
    ET = m["zmat_t"]
    lo, hi = slice(0, 64), slice(64, 128)

    def grp(g):
        return slice(g * GH, (g + 1) * GH)

    def bank_a(g):
        return m["bank"][g][:, :]

    def bank_b(g):
        return m["bank"][NG + g][:, :]

    def a4(g, cols):
        return bank_a(g)[:, 0:GH * cols].rearrange("p (h c) -> p h c", h=GH)

    def b4(g, cols):
        return bank_b(g)[:, 0:GH * cols].rearrange("p (h c) -> p h c", h=GH)

    def heads(q):
        return bass.ds(q * QH, QH)

    def half_dt(q, cols, count=QH, at=0):
        return m["hdt"][:, bass.ds(q * QH + at, count)].unsqueeze(2).to_broadcast([P, count, cols])

    def sync(e):
        e.dma_start(m["hdt"][:, :], ins["log_dt"].partition_broadcast(P)).then_inc(s["small_in"][0], 16)
        e.dma_start(m["b_all"][:, :], ins["b"]).then_inc(s["small_in"][1], 16)
        with e.Fori(0, NQ) as q:
            for k, (dst, src) in enumerate(((m["a_all"], "a"), (m["at_all"], "at"), (m["c_all"], "c"))):
                e.dma_start(dst[:, heads(q), :], ins[src][:, heads(q), :]).then_inc(s["ssm_in"][k], 16)
            for k in range(3):
                e.wait_ge(s["ssm_in"][k], 16 * (q + 1))
            e.sem_inc(s["turn_sp"], 1)

    def store(e):
        with e.Fori(0, NQ) as q:
            e.wait_ge(s["dve"], DV.after(q, "F", NG - 1))
            e.wait_ge(s["act"], AC.after(q, "F", NG - 1))
            for blk in range(2):
                e.dma_start(hbuf[:, bass.ds(q * QH, QH), blk * XC:(blk + 1) * XC],
                            m["outb"][64 * blk:64 * blk + 64, :, :]).then_inc(s["rows_out"][blk], 16)
            for blk in range(2):
                e.wait_ge(s["rows_out"][blk], 16 * (q + 1))
            e.sem_inc(s["outb_free"], 1)

    def vector(e):
        v = nc.vector
        v.memset(m["sign"][0:64, :], 1.0).then_inc(s["const_v"], 1)
        v.memset(m["sign"][64:128, :], -1.0).then_inc(s["const_v"], 1)
        e.wait_ge(s["const_v"], 2)
        e.wait_ge(s["ident_ready"], 1)
        eye = m["ident"][:, 0:64].unsqueeze(1)
        with e.Fori(0, NQ) as q:
            e.wait_ge(s["ssm_in"][0], 16 * (q + 1))
            e.wait_ge(s["dt_ready"], 1)
            v.tensor_tensor(m["tmp"][:, :, :], m["a_all"][:, heads(q), :], half_dt(q, 64), ALU.mult).then_inc(s["link"], 1)
            e.wait_ge(s["link"], 3 * q + 1)
            v.tensor_tensor(SR[:, :, 0:64], eye.to_broadcast([P, QH, 64]), m["tmp"][:, :, :],
                            ALU.subtract).then_inc(s["dve"], 1)
            for g in range(NG):
                e.wait_ge(s["pe"], PE.after(q, "G", g))
                v.tensor_copy(SR[:, grp(g), 0:64], a4(g, 64)).then_inc(s["dve"], 1)
            e.wait_ge(s["act"], AC.after(q, "G", NG - 1))
            e.wait_ge(s["dve"], DV.after(q, "G", NG - 1))
            v.tensor_reduce(m["rowsum"][:, :], SR[:, :, 0:128], axis=AX, op=ALU.add,
                            apply_absolute_value=True).then_inc(s["dve"], 1)
            e.wait_ge(s["norm_ready"], q + 1)
            v.reciprocal(m["alpha"][:, :], m["norm"][:, :]).then_inc(s["link"], 1)
            e.wait_ge(s["link"], 3 * q + 2)
            v.tensor_tensor(SR[:, :, 0:128], SR[:, :, 0:128],
                            m["alpha"][:, :].unsqueeze(2).to_broadcast([P, QH, 128]), ALU.mult).then_inc(s["link"], 1)
            e.wait_ge(s["link"], 3 * q + 3)
            v.tensor_tensor(SR[:, :, 0:128], m["ident"][:, :].unsqueeze(1).to_broadcast([P, QH, 128]),
                            SR[:, :, 0:128], ALU.subtract).then_inc(s["dve"], 1)
            e.wait_ge(s["ssm_in"][1], 16 * (q + 1))
            v.scalar_tensor_tensor(m["tmp"][:, :, :], m["at_all"][:, heads(q), :], m["sign"][:, 0:1],
                                   half_dt(q, 64), ALU.mult, ALU.mult).then_inc(s["link2"], 1)
            e.wait_ge(s["link2"], 2 * q + 1)
            v.tensor_tensor(m["tmp"][:, :, :], eye.to_broadcast([P, QH, 64]), m["tmp"][:, :, :],
                            ALU.subtract).then_inc(s["link2"], 1)
            e.wait_ge(s["link2"], 2 * q + 2)
            v.tensor_tensor(SR[:, :, 128:192], m["tmp"][:, :, :],
                            m["alpha"][:, :].unsqueeze(2).to_broadcast([P, QH, 64]), ALU.mult).then_inc(s["dve"], 1)
            for k in range(INV):
                for g in range(NG):
                    e.wait_ge(s["pe"], PE.after(q, "N", k, g))
                    if k == INV - 1:
                        v.tensor_tensor(SR[:, grp(g), 128:192], SR[:, grp(g), 128:192], a4(g, 64),
                                        ALU.add).then_inc(s["dve"], 1)
                    else:
                        v.tensor_copy(SR[:, grp(g), 0:64], a4(g, 128)[:, :, 0:64]).then_inc(s["dve"], 1)
                        v.tensor_tensor(SR[:, grp(g), 128:192], SR[:, grp(g), 128:192],
                                        a4(g, 128)[:, :, 64:128], ALU.add).then_inc(s["dve"], 1)
            for g in range(NG):
                e.wait_ge(s["dve"], DV.after(q, "N", INV - 1, g))
                v.scalar_tensor_tensor(SR[:, grp(g), 0:64], SR[:, grp(g), 128:192], 2.0,
                                       eye.to_broadcast([P, GH, 64]), ALU.mult, ALU.subtract).then_inc(s["dve"], 1)

            def transposed(j, g):
                e.wait_ge(s["pe"], PE.after(q, "T", j, g))
                v.tensor_copy(ET[:, grp(g), :], b4(g, 128)).then_inc(s["dve"], 1)

            for g in range(NG):
                transposed(0, g)
            for g in range(NG):
                e.wait_ge(s["pe"], PE.after(q, "b", g))
                v.tensor_tensor(m["xk"][:, grp(g), 0:1], m["b_all"][:, bass.ds(q * QH + g * GH, GH)].unsqueeze(2),
                                a4(g, 1), ALU.add).then_inc(s["dve"], 1)
                e.wait_ge(s["dve"], DV.after(q, "b+", g))
                v.tensor_tensor(m["xk"][:, grp(g), 0:1], m["xk"][:, grp(g), 0:1], half_dt(q, 1, GH, g * GH),
                                ALU.mult).then_inc(s["dve"], 1)
            for j in range(DBL):
                for g in range(NG):
                    e.wait_ge(s["pe"], PE.after(q, "K", j, g))
                    v.tensor_copy(SR[:, grp(g), 0:64], a4(g, 64)).then_inc(s["dve"], 1)
                if j < DBL - 1:
                    for g in range(NG):
                        transposed(j + 1, g)
            e.wait_ge(s["ssm_in"][2], 16 * (q + 1))
            v.tensor_scalar(m["cy"][:, :, 0:64], m["c_all"][:, heads(q), :], m["sign"][:, 0:1], None,
                            ALU.mult).then_inc(s["dve"], 1)
            e.wait_ge(s["outb_free"], q + 1)
            for g in range(NG):
                e.wait_ge(s["pe"], PE.after(q, "F", g))
                v.tensor_copy(m["outb"][:, g * GH:g * GH + 2, :],
                              bank_a(g).rearrange("p (h c) -> p h c", h=2)).then_inc(s["dve"], 1)

    def scalar(e):
        c = nc.scalar
        e.wait_ge(s["small_in"][0], 16)
        c.activation(m["hdt"][:, :], m["hdt"][:, :], ACT.Exp).then_inc(s["link_a"], 1)
        e.wait_ge(s["link_a"], 1)
        c.activation(m["hdt"][:, :], m["hdt"][:, :], ACT.Copy, scale=0.5).then_inc(s["dt_ready"], 1)

        def rotate(z):
            c.activation(z[lo, :, 64:128], z[hi, :, 0:64], ACT.Copy, scale=-1.0)
            return c.activation(z[hi, :, 64:128], z[lo, :, 0:64], ACT.Copy)

        with e.Fori(0, NQ) as q:
            e.wait_ge(s["dve"], DV.after(q, "B"))
            rotate(SR[:, :, :]).then_inc(s["act"], 1)
            for g in range(NG):
                e.wait_ge(s["dve"], DV.after(q, "G", g))
                rotate(SR[:, grp(g), :]).then_inc(s["act"], 1)
            for k in range(INV - 1):
                for g in range(NG):
                    e.wait_ge(s["dve"], DV.after(q, "S", k, g))
                    rotate(SR[:, grp(g), :]).then_inc(s["act"], 1)
            for g in range(NG):
                e.wait_ge(s["dve"], DV.after(q, "P", g))
                rotate(SR[:, grp(g), :]).then_inc(s["act"], 1)
            for j in range(DBL):
                n = 2 ** j
                for g in range(NG):
                    e.wait_ge(s["dve"], DV.after(q, "K", j, g))
                    rotate(SR[:, grp(g), :]).then_inc(s["act"], 1)
                    c.activation(m["xk"][:, grp(g), n:2 * n], b4(g, n), ACT.Copy).then_inc(s["act"], 1)
            for g in range(NG):
                e.wait_ge(s["pe"], PE.after(q, "Y", g))
                c.activation(m["cy"][:, grp(g), 64:128], a4(g, 64), ACT.Copy).then_inc(s["act"], 1)
            e.wait_ge(s["outb_free"], q + 1)
            for g in range(NG):
                e.wait_ge(s["pe"], PE.after(q, "F", g))
                c.activation(m["outb"][:, g * GH + 2:g * GH + 4, :],
                             bank_b(g).rearrange("p (h c) -> p h c", h=2), ACT.Copy).then_inc(s["act"], 1)

    def gpsimd(e):
        with e.Fori(0, NQ) as q:
            e.wait_ge(s["dve"], DV.after(q, "rowsum"))
            e.sem_inc(s["turn_pool"], 1)
            nc.gpsimd.partition_all_reduce(m["norm"][:, :], m["rowsum"][:, :], P,
                                           bass.bass_isa.ReduceOp.max).then_inc(s["norm_ready"], 1)

    def tensor(e):
        mm = nc.tensor.matmul
        with e.Fori(0, NQ) as q:
            e.wait_ge(s["act"], AC.after(q, "B"))
            for g in range(NG):
                for i in range(GH):
                    h = g * GH + i
                    last = mm(a4(g, 64)[:, i, :], SR[:, h, 0:128], SR[:, h, 0:64], start=True, stop=True)
                last.then_inc(s["pe"], 1)
            for k in range(INV):
                for g in range(NG):
                    if k == 0:
                        e.wait_ge(s["dve"], DV.after(q, "Q"))
                    else:
                        e.wait_ge(s["dve"], DV.after(q, "N", k - 1, g))
                        e.wait_ge(s["act"], AC.after(q, "N", k - 1, g))
                    for i in range(GH):
                        h = g * GH + i
                        if k == INV - 1:
                            last = mm(a4(g, 64)[:, i, :], SR[:, h, 0:128], SR[:, h, 128:192], start=True, stop=True)
                        else:
                            sq = SR[:, h, :].rearrange("p (b c) -> p b c", b=3)[:, 0:3:2, :]
                            last = mm(a4(g, 128)[:, i, :], SR[:, h, 0:128], sq, start=True, stop=True)
                    last.then_inc(s["pe"], 1)

            def transpose(j, g):
                if j == 0:
                    e.wait_ge(s["act"], AC.after(q, "P", g))
                else:
                    e.wait_ge(s["dve"], DV.after(q, "K", j - 1, g))
                    e.wait_ge(s["act"], AC.after(q, "X", j - 1, g))
                for i in range(GH):
                    last = nc.tensor.transpose(b4(g, 128)[:, i, :], SR[:, g * GH + i, 0:128], m["ident"][:, :])
                last.then_inc(s["pe"], 1)

            for g in range(NG):
                transpose(0, g)
            e.wait_ge(s["small_in"][1], 16)
            for g in range(NG):
                e.wait_ge(s["dve"], DV.after(q, "T", 0, g))
                for i in range(GH):
                    h = g * GH + i
                    last = mm(a4(g, 1)[:, i, :], ET[:, h, :], m["b_all"][:, bass.ds(q * QH + h, 1)],
                              start=True, stop=True)
                last.then_inc(s["pe"], 1)
            for j in range(DBL):
                n = 2 ** j
                for g in range(NG):
                    e.wait_ge(s["dve"], DV.after(q, "b", g) if j == 0 else DV.after(q, "T", j, g))
                    for i in range(GH):
                        h = g * GH + i
                        mm(a4(g, 64)[:, i, :], ET[:, h, :], SR[:, h, 0:64], start=True, stop=True)
                        last = mm(b4(g, n)[:, i, :], ET[:, h, :], m["xk"][:, h, 0:n], start=True, stop=True)
                    last.then_inc(s["pe"], 1)
                if j < DBL - 1:
                    for g in range(NG):
                        transpose(j + 1, g)
            e.wait_ge(s["dve"], DV.after(q, "C"))
            for g in range(NG):
                e.wait_ge(s["act"], AC.after(q, "X", DBL - 1, g))
                for i in range(GH):
                    h = g * GH + i
                    last = mm(a4(g, 64)[:, i, :], SR[:, h, 0:128], m["cy"][:, h, 0:64], start=True, stop=True)
                last.then_inc(s["pe"], 1)
            for g in range(NG):
                e.wait_ge(s["act"], AC.after(q, "Y", g))
                for i in range(GH):
                    h = g * GH + i
                    bank = bank_a(g) if i < 2 else bank_b(g)
                    last = mm(bank[:, (i % 2) * XC:(i % 2 + 1) * XC], m["cy"][:, h, :], m["xk"][:, h, :],
                              start=True, stop=True)
                last.then_inc(s["pe"], 1)

    return dict(sync=sync, store=store, vector=vector, scalar=scalar, gpsimd=gpsimd, tensor=tensor)


def token_program(nc, ins, hbuf, wscr, out, m, s):
    HU, VU = NHEAD * NTG, (TOPK + NSH) * NTG
    BQ, BK, BV, BS, BT, BY, BO0, BO1 = (m["bank"][i][:, :] for i in range(8))
    BO = [BO0, BO1]
    BL = [BT, BY]
    BG, BU = [BQ, BV], [BK, BS]

    def tile_cols(t):
        return slice(t * P, (t + 1) * P)

    def group_cols(tg):
        return slice(tg * TG, (tg + 1) * TG)

    def pairs(bank):
        return bank.rearrange("p (i c) -> p i c", i=TPG)

    def w_proj(k, which):
        return slice((which * KC + k) * DH, (which * KC + k + 1) * DH)

    W_OUT = slice(3 * KC * DH, ACOLS)

    def w_hid(k, which, j):
        at = (which * KC + k) * HID + j * P
        return slice(at, at + P)

    def w_down(j, shared):
        at = (1 if shared else 2) * KC * HID + j * D
        return slice(at, at + D)

    def three(out_ap, hi, lo, rhi, rlo, start, stop):
        nc.tensor.matmul(out_ap, hi, rhi, start=start, stop=False)
        nc.tensor.matmul(out_ap, hi, rlo, start=False, stop=False)
        return nc.tensor.matmul(out_ap, lo, rhi, start=False, stop=stop)

    def split_hi(dst, src):
        return nc.scalar.activation(dst, src, ACT.Copy)

    def split_lo(dst, src, hi):
        return nc.vector.tensor_tensor(dst, src, hi.bitcast(f32), ALU.subtract)

    def pieces(cols):
        step = -(-cols // 3 // P) * P
        return [(a, min(a + step, cols)) for a in range(0, cols, step)]

    def item_hi(e, n, par, cols, k, first=False):
        a, b = pieces(cols)[k]
        e.wait_ge(s["raw_loaded"], 16 * (n + 1))
        if not first:
            e.wait_ge(s["o_done"], 16 * (n - 1) + 1)
        nc.scalar.activation(m["whi"][:, par, a:b], m["raw"][:, a:b], ACT.Copy).then_inc(s["w_hi"], 1)

    def item_lo(e, n, par, cols, bias):
        for k, (a, b) in enumerate(pieces(cols)):
            e.wait_ge(s["w_hi"], 3 * n + k + 1)
            last = nc.gpsimd.tensor_tensor(m["wlo"][:, par, a:b], m["raw"][:, a:b],
                                           m["whi"][:, par, a:b].bitcast(f32), ALU.subtract)
            if bias and k == 2:
                last = nc.gpsimd.tensor_copy(m["ebias"][:, par, 0:bias], m["raw"][:, cols:cols + bias])
        last.then_inc(s["w_ready"], 1)

    def dve_norm(e, hf, phase):
        v = nc.vector
        for tg in range(NTG):
            g = hf * 2 * NTG + phase * NTG + tg
            if phase == 0:
                e.wait_ge(s["acc_loaded"][tg], 16 * (hf + 1))
            else:
                e.wait_ge(s["o_added"], 4 * (hf * (HU + VU) + HU) + 2)
            for i in range(TPG):
                last = v.bn_stats(m["stats"][:, i, :], m["acc"][:, tg * TPG + i, :])
            last.then_inc(s["ln_stats"], 1)
            e.wait_ge(s["ln_stats"], g + 1)
            e.sem_inc(s["turn_dve"], 1)
            for i in range(TPG):
                last = v.bn_aggr(m["mean_var"][:, i, :], m["stats"][:, i, :])
            last.then_inc(s["ln_aggr"], 1)
            e.wait_ge(s["ln_rstd"], g + 1)

            def low(i):
                tile = g * TPG + i
                e.wait_ge(s["x_hi"], tile + 1)
                cols = tile_cols(tg * TPG + i)
                split_lo(m["xlo"][:, :, cols], pairs(BL[i % 2]), m["xhi"][:, :, cols]).then_inc(s["x_split"], 1)

            for i in range(TPG):
                e.wait_ge(s["xn_turned"], g * TPG + i + 1)
                v.tensor_scalar(m["xn"][:, i % 2, :], m["acc"][:, tg * TPG + i, :], m["mean_var"][:, i, 0:1],
                                m["rstd"][:, i:i + 1], ALU.subtract, ALU.mult).then_inc(s["xn_ready"], 1)
                if i:
                    low(i - 1)
            low(TPG - 1)

    def pool_norm(e, hf, phase):
        for tg in range(NTG):
            g = hf * 2 * NTG + phase * NTG + tg
            e.wait_ge(s["ln_aggr"], g + 1)
            e.sem_inc(s["turn_pool"], 1)
            nc.gpsimd.tensor_scalar(m["var_eps"][:, :], m["mean_var"][:, :, 1], EPS, None, ALU.add).then_inc(s["ln_eps"], 1)
            e.wait_ge(s["ln_eps"], g + 1)
            nc.gpsimd.tensor_tensor(m["rstd"][:, :], m["var_eps"][:, :], m["neg_half"][:, :], ALU.pow).then_inc(s["ln_rstd"], 1)

    def act_norm(e, hf, phase):
        for tg in range(NTG):
            for i in range(TPG):
                tile = (hf * 2 * NTG + phase * NTG + tg) * TPG + i
                e.wait_ge(s["xn_turned"], tile + 3)
                split_hi(m["xhi"][:, :, tile_cols(tg * TPG + i)], pairs(BL[i % 2])).then_inc(s["x_hi"], 1)

    def pe_norm(e, hf, phase):
        for tg in range(NTG):
            for i in range(TPG):
                tile = (hf * 2 * NTG + phase * NTG + tg) * TPG + i
                e.wait_ge(s["xn_ready"], tile + 1)
                e.wait_ge(s["x_split"], tile + 1)
                for k in range(KC):
                    last = nc.tensor.transpose(pairs(BL[i % 2])[:, k, :], m["xn"][:, i % 2, tile_cols(k)],
                                               m["ident"][:, :])
                last.then_inc(s["xn_turned"], 1)
            if phase == 1:
                e.wait_ge(s["x_split"], tile + 3)
                for i in range(TPG):
                    t = tg * TPG + i
                    for k in range(KC):
                        last = three(BO0[:, t * NEXP:(t + 1) * NEXP], m["xhi"][:, k, tile_cols(t)],
                                     m["xlo"][:, k, tile_cols(t)], m["wg_hi"][:, k, :], m["wg_lo"][:, k, :],
                                     k == 0, k == KC - 1)
                last.then_inc(s["gate_done"], 1)

    def pe_project(e, which, bank, free, done, u, n, hf, tg, par):
        if which == 0:
            e.wait_ge(s["w_ready"], n + 1)
            e.wait_ge(s["x_split"], hf * 2 * NT + (tg + 1) * TPG + 2)
        e.wait_ge(free, u + 1)
        for k in range(KC):
            w = w_proj(k, which)
            last = three(bank, m["whi"][:, par, w], m["wlo"][:, par, w], m["xhi"][:, k, group_cols(tg)],
                         m["xlo"][:, k, group_cols(tg)], k == 0, k == KC - 1)
        last.then_inc(done, 1)

    def pe_scores(e, u):
        e.wait_ge(s["q_split"], u + 2)
        e.wait_ge(s["k_split"], u + 2)
        e.wait_ge(s["s_read"], u + 1)
        for i in range(TPG):
            c = tile_cols(i)
            last = three(BS[:, c], m["qhi"][:, c], m["qlo"][:, c], m["khi"][:, c], m["klo"][:, c], True, True)
        last.then_inc(s["s_done"], 1)

    def pe_turn_v(e, u):
        e.wait_ge(s["vt_copied"], u + 1)
        for i in range(TPG):
            last = nc.tensor.transpose(BV[:, tile_cols(i)], m["vt"][:, tile_cols(i)], m["ident"][:, :])
        last.then_inc(s["v_turned"], 1)

    def pe_turn_p(e, u):
        e.wait_ge(s["p_ready"], u + 1)
        e.wait_ge(s["pt_split"], u + 1)
        for i in range(TPG):
            last = nc.tensor.transpose(BT[:, tile_cols(i)], m["prob"][:, i, :], m["ident"][:, :])
        last.then_inc(s["p_turned"], 1)

    def pe_mix(e, u):
        e.wait_ge(s["pt_split"], u + 2)
        e.wait_ge(s["v_split"], u + 2)
        e.wait_ge(s["y_split"], u + 1)
        for i in range(TPG):
            c = tile_cols(i)
            last = three(BY[:, c], m["vhi"][:, c], m["vlo"][:, c], m["pthi"][:, c], m["ptlo"][:, c], True, True)
        last.then_inc(s["y_done"], 1)

    def pe_out(e, u, w, par):
        e.wait_ge(s["y_split"], u + 2)
        for i in range(TPG):
            e.wait_ge(s["o_added"], 4 * w + i + 1)
            c = tile_cols(i)
            three(BO[i % 2], m["yhi"][:, c], m["ylo"][:, c], m["whi"][:, par, W_OUT], m["wlo"][:, par, W_OUT],
                  True, True).then_inc(s["o_done"], 1)

    def pe_attention(e, hf):
        def step(u, w, n, k, first=False, last=False):
            par, nxt, npar, ntg = k // NTG, u + 1, (k + 1) // NTG % 2, (k + 1) % NTG
            if first:
                nxt, npar, ntg = u, 0, 0
            nn = n + (1 if (k + 1) % NTG == 0 and not first else 0)
            if not last:
                pe_project(e, 0, BQ, s["q_split"], s["q_done"], nxt, nn, hf, ntg, npar)
                pe_project(e, 1, BK, s["k_split"], s["k_done"], nxt, nn, hf, ntg, npar)
            if not first:
                pe_turn_p(e, u)
            if not last:
                pe_project(e, 2, BV, s["v_split"], s["v_done"], nxt, nn, hf, ntg, npar)
            if not first:
                pe_mix(e, u)
            if not last:
                pe_scores(e, nxt)
                pe_turn_v(e, nxt)
            if not first:
                pe_out(e, u, w, par)

        u0, w0, n0 = hf * HU, hf * (HU + VU), hf * ITEMS
        step(u0, w0, n0, 0, first=True)
        with e.Fori(0, NHEAD // 2 - 1) as pair:
            for k in range(2 * NTG):
                step(u0 + pair * 8 + k, w0 + pair * 8 + k, n0 + pair * 2 + k // NTG, k)
        for k in range(2 * NTG):
            step(u0 + (HU - 8 + k), w0 + (HU - 8 + k), n0 + (NHEAD - 2 + k // NTG), k, last=k == 2 * NTG - 1)

    def act_attention(e, hf):
        def step(u, n, k, first=False, last=False):
            nxt = u if first else u + 1
            if not last:
                e.wait_ge(s["q_done"], nxt + 1)
                split_hi(m["qhi"][:, :], BQ).then_inc(s["q_hi"], 1)
                e.wait_ge(s["k_done"], nxt + 1)
                split_hi(m["khi"][:, :], BK).then_inc(s["k_hi"], 1)
            if not first:
                e.wait_ge(s["p_turned"], u + 1)
                split_hi(m["pthi"][:, :], BT).then_inc(s["pt_hi"], 1)
            if not last:
                e.wait_ge(s["v_done"], nxt + 1)
                nc.scalar.activation(m["vt"][:, :], BV, ACT.Copy).then_inc(s["vt_copied"], 1)
            if not first:
                e.wait_ge(s["y_done"], u + 1)
                split_hi(m["yhi"][:, :], BY).then_inc(s["y_hi"], 1)
            if not last:
                e.wait_ge(s["v_turned"], nxt + 1)
                split_hi(m["vhi"][:, :], BV).then_inc(s["v_hi"], 1)
                e.wait_ge(s["row_sub"], nxt + 1)
                nc.scalar.activation(m["sm"][:, :, :], m["sm"][:, :, :], ACT.Exp).then_inc(s["p_exp"], 1)
            if not first and k % NTG < 3:
                cols = WCOLS if last_pair and k >= NTG else ACOLS
                item_hi(e, n + 1, (k // NTG + 1) % 2, cols, k % NTG)

        u0, n0 = hf * HU, hf * ITEMS
        last_pair = False
        step(u0, n0, 0, first=True)
        with e.Fori(0, NHEAD // 2 - 1) as pair:
            for k in range(2 * NTG):
                step(u0 + pair * 8 + k, n0 + pair * 2 + k // NTG, k)
        last_pair = True
        for k in range(2 * NTG):
            step(u0 + (HU - 8 + k), n0 + (NHEAD - 2 + k // NTG), k, last=k == 2 * NTG - 1)

    def add_output(e, w, tg, i):
        t = tg * TPG + i
        e.wait_ge(s["o_done"], 4 * w + i + 2)
        nc.vector.tensor_tensor(m["acc"][:, t, :], m["acc"][:, t, :], BO[i % 2], ALU.add).then_inc(s["o_added"], 1)

    def dve_attention(e, hf):
        v = nc.vector
        rows = (slice(0, T), slice(T, P))

        def step(u, w, k, first=False, last=False):
            nxt, tg = (u if first else u + 1), k % NTG
            if not last:
                e.wait_ge(s["q_hi"], nxt + 1)
                split_lo(m["qlo"][:, :], BQ, m["qhi"][:, :]).then_inc(s["q_split"], 1)
                e.wait_ge(s["k_hi"], nxt + 1)
                split_lo(m["klo"][:, :], BK, m["khi"][:, :]).then_inc(s["k_split"], 1)
            if not first:
                e.wait_ge(s["pt_hi"], u + 1)
                split_lo(m["ptlo"][:, :], BT, m["pthi"][:, :]).then_inc(s["pt_split"], 1)
                e.wait_ge(s["y_hi"], u + 1)
                split_lo(m["ylo"][:, :], BY, m["yhi"][:, :]).then_inc(s["y_split"], 1)
            if not last:
                e.wait_ge(s["s_done"], nxt + 1)
                for r in rows:
                    got = v.scalar_tensor_tensor(m["sm"][r, :, :], pairs(BS)[r, :, r], SCALE,
                                                 m["mask"][r, :].unsqueeze(1).to_broadcast([T, TPG, T]),
                                                 ALU.mult, ALU.add)
                got.then_inc(s["s_read"], 1)
                e.wait_ge(s["s_read"], nxt + 2)
                v.tensor_reduce(m["rmax"][:, :], m["sm"][:, :, :], axis=AX, op=ALU.max).then_inc(s["row_max"], 1)
                e.wait_ge(s["row_max"], nxt + 1)
                v.tensor_tensor(m["sm"][:, :, :], m["sm"][:, :, :], m["rmax"][:, :].unsqueeze(2).to_broadcast([P, TPG, T]),
                                ALU.subtract).then_inc(s["row_sub"], 1)
            if not first:
                add_output(e, w, tg, 0)
            if not last:
                e.wait_ge(s["v_hi"], nxt + 1)
                split_lo(m["vlo"][:, :], BV, m["vhi"][:, :]).then_inc(s["v_split"], 1)
            if not first:
                add_output(e, w, tg, 1)
            if not last:
                e.wait_ge(s["p_exp"], nxt + 1)
                v.tensor_reduce(m["rsum"][:, :], m["sm"][:, :, :], axis=AX, op=ALU.add).then_inc(s["row_sum"], 1)
                e.wait_ge(s["row_sum"], nxt + 1)
                v.reciprocal(m["rinv"][:, :], m["rsum"][:, :]).then_inc(s["row_inv"], 1)
            if not first:
                add_output(e, w, tg, 2)
            if not last:
                e.wait_ge(s["row_inv"], nxt + 1)
                for r in rows:
                    got = v.tensor_tensor(m["prob"][r, :, r], m["sm"][r, :, :],
                                          m["rinv"][r, :].unsqueeze(2).to_broadcast([T, TPG, T]), ALU.mult)
                got.then_inc(s["p_ready"], 1)
            if not first:
                add_output(e, w, tg, 3)

        u0, w0 = hf * HU, hf * (HU + VU)
        for r, c in (rows, rows[::-1]):
            got = v.memset(m["prob"][r, :, c], 0.0)
        step(u0, w0, 0, first=True)
        with e.Fori(0, NHEAD // 2 - 1) as pair:
            for k in range(2 * NTG):
                step(u0 + pair * 8 + k, w0 + pair * 8 + k, k)
        for k in range(2 * NTG):
            step(u0 + (HU - 8 + k), w0 + (HU - 8 + k), k, last=k == 2 * NTG - 1)

    def dve_route(e, hf):
        v = nc.vector
        made = [0]
        LINKS = 18

        def link(op):
            made[0] += 1
            op.then_inc(s["route"], 1)
            e.wait_ge(s["route"], hf * LINKS + made[0])

        e.wait_ge(s["gate_done"], (hf + 1) * NTG)
        gate = m["gate"][:, :, :]
        by_e = gate.unsqueeze(3).to_broadcast([P, NT, NEXP, NEXP])
        by_j = gate.unsqueeze(2).to_broadcast([P, NT, NEXP, NEXP])
        link(v.tensor_tensor(gate, BO0[:, 0:NT * NEXP].rearrange("p (t x) -> p t x", t=NT),
                             m["bg"][:, :].unsqueeze(1).to_broadcast([P, NT, NEXP]), ALU.add))
        link(v.tensor_tensor(m["before"][:, :, :, :], by_j, by_e, ALU.is_gt))
        link(v.tensor_tensor(m["ties"][:, :, :, :], by_j, by_e, ALU.is_equal))
        link(v.tensor_tensor(m["ties"][:, :, :, :], m["ties"][:, :, :, :],
                             m["tri"][:, :, :].unsqueeze(1).to_broadcast([P, NT, NEXP, NEXP]), ALU.mult))
        link(v.tensor_tensor(m["before"][:, :, :, :], m["before"][:, :, :, :], m["ties"][:, :, :, :], ALU.add))
        link(v.tensor_reduce(m["keep"][:, :, :], m["before"][:, :, :, :], axis=AX, op=ALU.add))
        link(v.tensor_scalar(m["keep"][:, :, :], m["keep"][:, :, :], TOPK - 0.5, None, ALU.is_lt))
        link(v.tensor_reduce(m["gmax"][:, :], gate, axis=AX, op=ALU.max))
        link(v.tensor_tensor(gate, gate, m["gmax"][:, :].unsqueeze(2).to_broadcast([P, NT, NEXP]), ALU.subtract))
        e.wait_ge(s["gate_exp"], hf + 1)
        link(v.tensor_tensor(gate, gate, m["keep"][:, :, :], ALU.mult))
        link(v.tensor_reduce(m["gmax"][:, :], gate, axis=AX, op=ALU.add))
        link(v.reciprocal(m["gmax"][:, :], m["gmax"][:, :]))
        link(v.tensor_tensor(m["w8"][:, :, 0:TOPK], gate[:, :, 0:TOPK],
                             m["gmax"][:, :].unsqueeze(2).to_broadcast([P, NT, TOPK]), ALU.mult))
        link(v.tensor_copy(m["w8hi"][:, :, :], m["w8"][:, :, :]))
        link(v.tensor_copy(m["ws"][:, :, 0:NEXP], m["w8hi"][:, :, :].bitcast(f32)))
        link(v.tensor_tensor(m["ws"][:, :, 32:32 + NEXP], m["w8"][:, :, :], m["w8hi"][:, :, :].bitcast(f32), ALU.subtract))
        link(v.tensor_copy(m["ws"][:, :, 64:64 + NEXP], m["w8hi"][:, :, :].bitcast(f32)))
        link(v.tensor_copy(m["ws"][:, :, 96:96 + NEXP], m["w8"][:, :, :]))
        assert made[0] == LINKS
        for t in range(NT):
            e.wait_ge(s["bias_done"], hf * NT + t + 1)
            v.tensor_tensor(m["acc"][:, t, :], m["acc"][:, t, :], BL[t % 2], ALU.add).then_inc(s["bias_added"], 1)

    ROUTE_SUB, ROUTE_END = 9, 18

    def act_route(e, hf):
        e.wait_ge(s["route"], hf * ROUTE_END + ROUTE_SUB)
        nc.scalar.activation(m["gate"][:, :, :], m["gate"][:, :, :], ACT.Exp).then_inc(s["gate_exp"], 1)
        for tg in range(NTG):
            e.wait_ge(s["w_turned"], hf * NTG + tg + 1)
            nc.scalar.activation(m["w3t"][:, group_cols(tg)], BL[tg % 2], ACT.Copy)
            nc.scalar.activation(m["w8t"][96:128, group_cols(tg)], BL[tg % 2][96:128, :], ACT.Copy).then_inc(s["wt_ready"], 1)

    def pe_route(e, hf):
        e.wait_ge(s["route"], (hf + 1) * ROUTE_END)
        for tg in range(NTG):
            if tg >= 2:
                e.wait_ge(s["wt_ready"], hf * NTG + tg - 1)
            for i in range(TPG):
                last = nc.tensor.transpose(BL[tg % 2][:, tile_cols(i)], m["ws"][:, tg * TPG + i, :], m["ident"][:, :])
            last.then_inc(s["w_turned"], 1)
        e.wait_ge(s["wt_ready"], (hf + 1) * NTG)
        for t in range(NT):
            e.wait_ge(s["bias_added"], hf * NT + t + 1)
            nc.tensor.matmul(BL[t % 2], m["w3t"][:, tile_cols(t)], m["bd3"][:, :], start=True, stop=True)\
              .then_inc(s["bias_done"], 1)

    def pe_hidden(e, v, r, n, hf, tg, par, shared):
        e.wait_ge(s["w_ready"], n + 1)
        e.wait_ge(s["x_split"], hf * 2 * NT + NT + (tg + 1) * TPG + 2)
        for j in range(HC):
            for which, bank, done in ((0, BG[j], s["g_done"]), (1, BU[j], s["u_done"])):
                if which and shared:
                    continue
                if which:
                    e.wait_ge(s["u_used"], 2 * r + j + 1)
                else:
                    e.wait_ge(s["g_used"], 2 * v + j + 1)
                for k in range(KC):
                    c = w_hid(k, which, j)
                    last = three(bank, m["whi"][:, par, c], m["wlo"][:, par, c], m["xhi"][:, k, group_cols(tg)],
                                 m["xlo"][:, k, group_cols(tg)], k == 0, k == KC - 1)
                last.then_inc(done, 1)

    def pe_down(e, v, w, k8, par, shared):
        slot = k8 % 2
        e.wait_ge(s["hid_split"], 2 * v + 4)
        for i in range(TPG):
            e.wait_ge(s["o_added"], 4 * w + i + 1)
            c = tile_cols(i)
            for j in range(HC):
                d = w_down(j, shared)
                last = three(BO[i % 2], m["hhi"][:, slot, j, c], m["hlo"][:, slot, j, c], m["whi"][:, par, d],
                             m["wlo"][:, par, d], j == 0, j == HC - 1)
            last.then_inc(s["o_done"], 1)

    def pe_experts(e, hf):
        v0, w0, r0, n0 = hf * VU, hf * (HU + VU) + HU, hf * TOPK * NTG, hf * ITEMS + NHEAD

        def step(at, item, k, shared, next_shared, last=False):
            if not last:
                pe_hidden(e, v0 + at + 1, r0 + at + 1, n0 + item + (1 if k % NTG == NTG - 1 else 0), hf,
                          (k + 1) % NTG, (k + 1) // NTG % 2, next_shared)
            pe_down(e, v0 + at, w0 + at, k, k // NTG, shared)

        pe_hidden(e, v0, r0, n0, hf, 0, 0, False)
        pe_route(e, hf)
        with e.Fori(0, 2) as pair:
            for k in range(8):
                step(pair * 8 + k, pair * 2 + k // NTG, k, False, False)
        for k in range(8):
            step(16 + k, 4 + k // NTG, k, False, k == 7)
        for k in range(8):
            step(24 + k, 6 + k // NTG, k, True, True, last=k == 7)

    def act_experts(e, hf):
        v0, r0, n0 = hf * VU, hf * TOPK * NTG, hf * ITEMS + NHEAD

        def hidden(at, k, shared):
            par, slot = k // NTG, k % 2
            v, r = v0 + at, r0 + at
            for j in range(HC):
                e.wait_ge(s["g_done"], 2 * v + j + 1)
                e.wait_ge(s["hid_split"], 2 * v + j + 1)
                nc.scalar.activation(m["sg"][:, j, :], BG[j], ACT.Silu,
                                     bias=m["ebias"][:, par, j:j + 1]).then_inc(s["g_used"], 1)
            for j in range(HC):
                if shared:
                    e.wait_ge(s["g_used"], 2 * v + j + 3)
                else:
                    e.wait_ge(s["hd_ready"], 2 * r + j + 5)
                split_hi(m["hhi"][:, slot, j, :], m["sg"][:, j, :]).then_inc(s["hid_hi"], 1)

        def step(at, item, k, next_shared, cols, last=False):
            if not last:
                hidden(at + 1, (k + 1) % 8, next_shared)
            if k % NTG < 3:
                item_hi(e, n0 + item + 1, (k // NTG + 1) % 2, cols, k % NTG)

        hidden(0, 0, False)
        with e.Fori(0, 2) as pair:
            for k in range(8):
                step(pair * 8 + k, pair * 2 + k // NTG, k, False, WCOLS)
        for k in range(8):
            step(16 + k, 4 + k // NTG, k, k == 7, WCOLS if k < NTG else SCOLS)
        for k in range(8):
            step(24 + k, 6 + k // NTG, k, True, SCOLS if k < NTG else ACOLS, last=k == 7)

    def dve_experts(e, hf):
        vec = nc.vector
        v0, w0, r0 = hf * VU, hf * (HU + VU) + HU, hf * TOPK * NTG

        def hidden(at, half_at, k, shared):
            par, slot = k // NTG, k % 2
            v, r = v0 + at, r0 + at
            for j in range(HC if not shared else 0):
                e.wait_ge(s["g_used"], 2 * v + j + 3)
                e.wait_ge(s["u_done"], 2 * r + j + 1)
                vec.scalar_tensor_tensor(m["sg"][:, j, :], BU[j], m["ebias"][:, par, HC + j:HC + j + 1],
                                         m["sg"][:, j, :], ALU.add, ALU.mult).then_inc(s["u_used"], 1)
                e.wait_ge(s["u_used"], 2 * r + j + 3)
                e.wait_ge(s["wb_loaded"][slot], 16 * (hf * (TOPK * NTG // 2) + half_at + 1))
                vec.tensor_tensor(m["sg"][:, j, :], m["sg"][:, j, :], m["wb"][:, slot, :], ALU.mult).then_inc(s["hd_ready"], 1)
            for j in range(HC):
                e.wait_ge(s["hid_hi"], 2 * v + j + 1)
                split_lo(m["hlo"][:, slot, j, :], m["sg"][:, j, :], m["hhi"][:, slot, j, :]).then_inc(s["hid_split"], 1)

        def step(at, half_next, k, next_shared, last=False):
            if not last:
                hidden(at + 1, half_next, (k + 1) % 8, next_shared)
            for i in range(TPG):
                add_output(e, w0 + at, k % NTG, i)

        hidden(0, 0, 0, False)
        with e.Fori(0, 2) as pair:
            for k in range(8):
                step(pair * 8 + k, pair * 4 + (k + 1) // 2, k, False)
        for k in range(8):
            step(16 + k, 8 + (k + 1) // 2, k, k == 7)
        for k in range(8):
            step(24 + k, None, k, True, last=k == 7)

    def load_item(e, n, src, cols):
        e.wait_ge(s["w_ready"], n)
        e.dma_start(m["raw"][:, 0:cols], src).then_inc(s["raw_loaded"], 16)

    def load_acc(e, half, tg):
        t0 = half * NT + tg * TPG
        e.dma_start(m["acc"][:, tg * TPG:(tg + 1) * TPG, :],
                    tokens(hbuf)[:, t0:t0 + TPG, :]).then_inc(s["acc_loaded"][tg], 16)

    def tokens(dram):
        return dram.rearrange("c h l -> (c h) l").rearrange("(t p) l -> p t l", p=P)

    def sync(e):
        for half in range(HALVES):
            n0 = half * ITEMS
            if half == 0:
                for tg in range(NTG):
                    load_acc(e, 0, tg)
            with e.Fori(1, NHEAD) as head:
                load_item(e, n0 + head, ins["wattn"][bass.ds(head, 1), :, :].squeeze(0), ACOLS)
            load_item(e, n0 + NHEAD, ins["wexp"][0], WCOLS + 2 * HC)
            for tg in range(NTG):
                e.wait_ge(s["wt_ready"], half * NTG + tg + 1)
                e.dma_start(wscr[half, :, group_cols(tg)], m["w8t"][96:96 + NEXP, group_cols(tg)]).then_inc(s["w_out"][tg], 16)
            for tg in range(NTG):
                e.wait_ge(s["w_out"][tg], 16 * (half + 1))

            def weights_back(ex, tg):
                r = (half * TOPK + ex) * NTG + tg
                e.wait_ge(s["hd_ready"], 2 * r + 2)
                e.dma_start(m["wb"][:, tg % 2, :],
                            wscr[half, bass.ds(ex, 1), group_cols(tg)].squeeze(0).partition_broadcast(P))\
                 .then_inc(s["wb_loaded"][tg % 2], 16)

            with e.Fori(0, TOPK - 1) as ex:
                load_item(e, n0 + NHEAD + 1 + ex, ins["wexp"][bass.ds(ex + 1, 1), :, :].squeeze(0), WCOLS + 2 * HC)
                for tg in range(NTG):
                    weights_back(ex, tg)
            load_item(e, n0 + NHEAD + TOPK, ins["wsh"][0], SCOLS + HC)
            for tg in range(NTG):
                weights_back(TOPK - 1, tg)
            load_item(e, n0 + NHEAD + TOPK + 1, ins["wsh"][1], SCOLS + HC)
            load_item(e, n0 + ITEMS, ins["wattn"][0], ACOLS)
            for tg in range(NTG):
                w = half * (HU + VU) + HU + VU - NTG + tg
                e.wait_ge(s["o_added"], 4 * (w + 1) + 2)
                e.dma_start(tokens(out)[:, half * NT + tg * TPG:half * NT + (tg + 1) * TPG, :],
                            m["acc"][:, tg * TPG:(tg + 1) * TPG, :]).then_inc(s["out_stored"][tg], 16)
            for tg in range(NTG):
                e.wait_ge(s["out_stored"][tg], 16 * (half + 1))
                if half + 1 < HALVES:
                    load_acc(e, half + 1, tg)
        e.wait_ge(s["raw_loaded"], 16 * (HALVES * ITEMS + 1))

    def vector(e):
        with e.Fori(0, HALVES) as hf:
            dve_norm(e, hf, 0)
            dve_attention(e, hf)
            dve_norm(e, hf, 1)
            dve_route(e, hf)
            dve_experts(e, hf)

    def scalar(e):
        with e.Fori(0, HALVES) as hf:
            act_norm(e, hf, 0)
            act_attention(e, hf)
            act_norm(e, hf, 1)
            act_route(e, hf)
            act_experts(e, hf)

    def tensor(e):
        with e.Fori(0, HALVES) as hf:
            pe_norm(e, hf, 0)
            pe_attention(e, hf)
            pe_norm(e, hf, 1)
            pe_experts(e, hf)

    def gpsimd(e):
        with e.Fori(0, HALVES) as hf:
            n0 = hf * ITEMS
            pool_norm(e, hf, 0)
            with e.Fori(0, NHEAD // 2 - 1) as pair:
                for k in range(2):
                    item_lo(e, n0 + pair * 2 + k + 1, (k + 1) % 2, ACOLS, 0)
            item_lo(e, n0 + NHEAD - 1, 1, ACOLS, 0)
            item_lo(e, n0 + NHEAD, 0, WCOLS, 2 * HC)
            pool_norm(e, hf, 1)
            with e.Fori(0, 2) as pair:
                for k in range(2):
                    item_lo(e, n0 + NHEAD + pair * 2 + k + 1, (k + 1) % 2, WCOLS, 2 * HC)
            item_lo(e, n0 + NHEAD + TOPK - 1, 1, WCOLS, 2 * HC)
            for k in range(2):
                item_lo(e, n0 + NHEAD + TOPK + k, k, SCOLS, HC)
            item_lo(e, n0 + ITEMS, 0, ACOLS, 0)

    def first_item(e, engine):
        if engine == "scalar":
            for k in range(3):
                item_hi(e, 0, 0, ACOLS, k, first=True)
        else:
            item_lo(e, 0, 0, ACOLS, 0)

    return dict(sync=sync, vector=vector, scalar=scalar, tensor=tensor, gpsimd=gpsimd, first_item=first_item)


def program(nc, ins, out):
    hbuf = nc.dram_tensor("hidden_rows", [CH, HD, SEQ], f32, kind="Internal").ap()
    wscr = nc.dram_tensor("routed_weights", [HALVES, NEXP, TH], f32, kind="Internal").ap()

    buffers, sems = {}, {}
    with ExitStack() as ctx:
        buffers.update({n: ctx.enter_context(nc.sbuf_tensor(n, shape, dt)) for n, shape, dt in (
            ("whi", [P, 2, WCOLS], f32r), ("wlo", [P, 2, WCOLS], f32r), ("raw", [P, WCOLS + 2 * HC], f32),
            ("ebias", [P, 2, 2 * HC], f32), ("xn", [P, 2, D], f32),
            ("ident", [P, P], f32), ("mask", [P, T], f32), ("tri", [P, NEXP, NEXP], f32),
            ("neg_half", [P, TPG], f32), ("sign", [P, 1], f32),
            ("stats", [P, TPG, 6], f32), ("mean_var", [P, TPG, 2], f32), ("var_eps", [P, TPG], f32),
            ("rstd", [P, TPG], f32), ("wg_raw", [P, KC, NEXP], f32), ("wg_hi", [P, KC, NEXP], f32r),
            ("wg_lo", [P, KC, NEXP], f32r), ("bg", [P, NEXP], f32), ("bd3", [P, D], f32r),
            ("gate", [P, NT, NEXP], f32), ("keep", [P, NT, NEXP], f32), ("gmax", [P, NT], f32),
            ("w8", [P, NT, NEXP], f32), ("w8hi", [P, NT, NEXP], f32r),
            ("b_all", [P, HD], f32), ("hdt", [P, HD], f32), ("rowsum", [P, QH], f32),
            ("alpha", [P, QH], f32), ("norm", [P, QH], f32))})
        at = nc.sbuf_base
        size = 4 * (3 * NT * D + 10 * 1024)
        ctx.enter_context(nc.sbuf_tensor("arena", [P, size // 4], f32))

        def lay(offset, tensors):
            for n, shape, dt in tensors:
                buffers[n] = nc.alloc_sbuf_tensor_at(n, [P] + shape, dt, offset=at + offset)
                offset += -(-4 * int(np.prod(shape)) // 32) * 32
            assert offset <= size
            return offset

        lay(0, (("a_all", [HD, NS], f32), ("at_all", [HD, NS], f32), ("c_all", [HD, CH], f32),
                ("zmat", [QH, 3 * NS], f32), ("zmat_t", [QH, P], f32), ("xk", [QH, XC], f32),
                ("cy", [QH, P], f32), ("outb", [QH, XC], f32), ("tmp", [QH, NS], f32)))
        work = lay(0, (("acc", [NT, D], f32), ("xhi", [KC, TH], f32r), ("xlo", [KC, TH], f32r)))
        lay(work, [(n, [TG], f32r) for n in ("qhi", "qlo", "khi", "klo", "vhi", "vlo", "pthi", "ptlo", "yhi", "ylo")]
            + [("vt", [TG], f32), ("prob", [TPG, P], f32), ("sm", [TPG, T], f32),
               ("rmax", [TPG], f32), ("rsum", [TPG], f32), ("rinv", [TPG], f32)])
        after_hid = lay(work, (("sg", [HC, TG], f32), ("hhi", [2, HC, TG], f32r), ("hlo", [2, HC, TG], f32r),
                               ("wb", [2, TG], f32)))
        lay(work + 4 * HC * TG, (("before", [NT, NEXP, NEXP], f32), ("ties", [NT, NEXP, NEXP], f32),
                                 ("w8t", [TH], f32)))
        lay(work + 24 * 1024, (("w3t", [TH], f32r), ("ws", [NT, P], f32)))
        lay(work + 38 * 1024, (("bd_tmp", [D], f32r),))
        assert after_hid <= work + 24 * 1024
        buffers["bank"] = [ctx.enter_context(nc.psum_tensor(f"bank{i}", [P, 512], f32)) for i in range(8)]

        sems.update({n: ctx.enter_context(nc.semaphore(n)) for n in (
            "const_v", "link", "link2", "link_a", "dt_ready", "dve", "act", "pe", "norm_ready", "outb_free",
            "turn_sp", "turn_pool", "turn_dve", "zeroed", "ident_ready", "consts_ready", "w8_ones", "bd_loaded", "wg_loaded",
            "bg_loaded", "bd_hi", "router_ready",
            "raw_loaded", "w_hi", "w_ready", "ln_stats", "ln_aggr", "ln_eps", "ln_rstd", "xn_ready", "xn_turned",
            "x_hi", "x_split", "gate_done", "gate_exp", "route", "w_turned", "wt_ready", "bias_done", "bias_added",
            "q_done", "k_done", "v_done", "s_done", "y_done", "q_hi", "k_hi", "v_hi", "pt_hi", "y_hi",
            "q_split", "k_split", "v_split", "pt_split", "y_split", "s_read", "row_max", "row_sub", "p_exp",
            "row_sum", "row_inv", "p_ready", "p_turned", "vt_copied", "v_turned", "o_done", "o_added",
            "g_done", "u_done", "g_used", "u_used", "hd_ready", "hid_hi", "hid_split")})
        for n, k in (("small_in", 2), ("ssm_in", 3), ("rows_out", 2), ("acc_loaded", NTG), ("out_stored", NTG),
                     ("w_out", NTG), ("wb_loaded", 2), ("bd_part", 3)):
            sems[n] = [ctx.enter_context(nc.semaphore(f"{n}{i}")) for i in range(k)]

        m, s = buffers, sems
        ssm = ssm_program(nc, ins, hbuf, m, s)
        tok = token_program(nc, ins, hbuf, wscr, out, m, s)
        block = ctx.enter_context(nc.Block())

        @block.sync
        def _(e):
            ssm["sync"](e)
            e.dma_start(m["raw"][:, 0:ACOLS], ins["wattn"][0]).then_inc(s["raw_loaded"], 16)
            e.dma_start(m["wg_raw"][:, :, :], ins["wg"]).then_inc(s["wg_loaded"], 16)
            e.dma_start(m["bg"][:, :], ins["bg"].partition_broadcast(P)).then_inc(s["bg_loaded"], 16)
            e.wait_ge(s["zeroed"], 4)
            for k in range(3):
                e.dma_start(m["xn"][32 * k:32 * k + TOPK + 1, 0, :], ins["bdown"]).then_inc(s["bd_part"][k], 16)
            e.sem_inc(s["outb_free"], 1)
            ssm["store"](e)
            tok["sync"](e)

        @block.gpsimd
        def _(e):
            p = nc.gpsimd
            p.memset(m["ident"][:, :], 0.0).then_inc(s["zeroed"], 1)
            p.memset(m["mask"][:, :], 0.0).then_inc(s["zeroed"], 1)
            p.memset(m["tri"][:, :, :], 1.0).then_inc(s["zeroed"], 1)
            p.memset(m["xn"][:, 0, :], 0.0).then_inc(s["zeroed"], 1)
            p.memset(m["w8"][:, :, :], 0.0).then_inc(s["zeroed"], 1)
            e.wait_ge(s["zeroed"], 5)
            p.affine_select(out=m["ident"][:, :], in_=m["ident"][:, :], compare_op=ALU.not_equal, fill=1.0,
                            base=0, pattern=[[-1, P]], channel_multiplier=1).then_inc(s["ident_ready"], 1)
            e.wait_ge(s["ident_ready"], 1)
            for k, r in enumerate((slice(0, T), slice(T, P))):
                p.affine_select(out=m["mask"][r, :], in_=m["mask"][r, :], compare_op=ALU.is_ge, fill=MASKED,
                                base=0, pattern=[[-1, T]], channel_multiplier=1).then_inc(s["zeroed"], 1)
                e.wait_ge(s["zeroed"], 6 + k)
            p.affine_select(out=m["tri"][:, :, :], in_=m["tri"][:, :, :], compare_op=ALU.is_gt, fill=0.0,
                            base=0, pattern=[[1, NEXP], [-1, NEXP]], channel_multiplier=0)
            p.memset(m["neg_half"][:, :], -0.5)
            p.memset(m["w8"][:, :, TOPK:TOPK + 1], 1.0).then_inc(s["consts_ready"], 1)
            e.wait_ge(s["consts_ready"], 1)
            tok["first_item"](e, "gpsimd")
            ssm["gpsimd"](e)
            tok["gpsimd"](e)

        @block.vector
        def _(e):
            for sem, credit in ((s["q_split"], 1), (s["k_split"], 1), (s["v_split"], 1), (s["pt_split"], 1), (s["y_split"], 1),
                                (s["s_read"], 1), (s["x_split"], 2), (s["o_added"], 2), (s["u_used"], 2), (s["hid_split"], 2),
                                (s["hd_ready"], 4), (s["bias_added"], 2)):
                e.sem_inc(sem, credit)
            e.wait_ge(s["consts_ready"], 1)
            ssm["vector"](e)
            e.wait_ge(s["bd_hi"], 2)
            nc.vector.tensor_tensor(m["wg_lo"][:, :, :], m["wg_raw"][:, :, :], m["wg_hi"][:, :, :].bitcast(f32), ALU.subtract)
            nc.vector.tensor_tensor(m["bd3"][64:128, :], m["xn"][64:128, 0, :], m["bd_tmp"][64:128, :].bitcast(f32),
                                    ALU.subtract).then_inc(s["router_ready"], 1)
            e.wait_ge(s["router_ready"], 1)
            nc.vector.memset(m["ws"][:, :, :], 0.0)
            e.wait_ge(s["bg_loaded"], 16)
            tok["vector"](e)

        @block.scalar
        def _(e):
            e.sem_inc(s["g_used"], 2)
            tok["first_item"](e, "scalar")
            ssm["scalar"](e)
            e.wait_ge(s["wg_loaded"], 16)
            nc.scalar.activation(m["wg_hi"][:, :, :], m["wg_raw"][:, :, :], ACT.Copy).then_inc(s["bd_hi"], 1)
            for k in range(3):
                e.wait_ge(s["bd_part"][k], 16)
            nc.scalar.activation(m["bd3"][0:64, :], m["xn"][0:64, 0, :], ACT.Copy)
            nc.scalar.activation(m["bd_tmp"][64:128, :], m["xn"][64:128, 0, :], ACT.Copy).then_inc(s["bd_hi"], 1)
            tok["scalar"](e)

        @block.tensor
        def _(e):
            e.sem_inc(s["o_done"], 1)
            e.sem_inc(s["xn_turned"], 2)
            e.wait_ge(s["ident_ready"], 1)
            ssm["tensor"](e)
            e.wait_ge(s["router_ready"], 1)
            tok["tensor"](e)
    return nc


def kernel(x, L0_tok_A, L0_tok_B, L0_tok_log_dt, L0_attn_Wq, L0_attn_Wk, L0_attn_Wv, L0_attn_Wo, L0_ffn_Wg,
           L0_ffn_bg, L0_ffn_Wgate, L0_ffn_bgate, L0_ffn_Wup, L0_ffn_bup, L0_ffn_Wdown, L0_ffn_bdown,
           L0_ffn_Ws_up, L0_ffn_bs_up, L0_ffn_Ws_down, L0_ffn_bs_down):
    import concourse.bacc as bacc
    from concourse.bass_utils import run_bass_kernel_spmd

    def proj(w):
        return np.asarray(w).reshape(NHEAD, DH, KC, P).transpose(0, 3, 2, 1).reshape(NHEAD, P, KC * DH)

    def up(w):
        return np.asarray(w).reshape(-1, KC, P, HID).transpose(0, 2, 1, 3).reshape(-1, P, KC * HID)

    def down(w):
        return np.asarray(w).reshape(-1, HC, P, D).transpose(0, 2, 1, 3).reshape(-1, P, HC * D)

    def bias(b):
        return np.asarray(b).reshape(-1, HC, P).transpose(0, 2, 1)

    a, b = np.asarray(L0_tok_A), np.asarray(L0_tok_B)
    wo = np.asarray(L0_attn_Wo).reshape(D, NHEAD, DH).transpose(1, 2, 0)
    ws_up = np.asarray(L0_ffn_Ws_up).reshape(D, NSH, HID).transpose(1, 0, 2)
    arrays = {
        "a": a.transpose(3, 1, 0, 2).reshape(P, HD, NS),
        "at": a.transpose(3, 2, 0, 1).reshape(P, HD, NS),
        "b": b.transpose(2, 1, 0).reshape(P, HD),
        "c": np.asarray(x).transpose(3, 2, 1, 0).reshape(P, HD, CH),
        "log_dt": np.asarray(L0_tok_log_dt).reshape(HD),
        "wattn": np.concatenate([proj(L0_attn_Wq), proj(L0_attn_Wk), proj(L0_attn_Wv), wo], axis=2),
        "wexp": np.concatenate([up(L0_ffn_Wgate), up(L0_ffn_Wup), down(L0_ffn_Wdown), bias(L0_ffn_bgate),
                                bias(L0_ffn_bup)], axis=2),
        "wsh": np.concatenate([up(ws_up), down(L0_ffn_Ws_down), bias(L0_ffn_bs_up)], axis=2),
        "wg": np.asarray(L0_ffn_Wg).reshape(KC, P, NEXP).transpose(1, 0, 2),
        "bg": np.asarray(L0_ffn_bg),
        "bdown": np.concatenate([np.asarray(L0_ffn_bdown), np.asarray(L0_ffn_bs_down)[None]], axis=0),
    }
    arrays = {n: np.ascontiguousarray(v) for n, v in arrays.items()}
    nc = bacc.Bacc("TRN2", target_bir_lowering=False, num_devices=1)
    ins = {n: nc.dram_tensor(f"in_{n}", v.shape, mybir.dt.from_np(v.dtype), kind="ExternalInput").ap()
           for n, v in arrays.items()}
    out = nc.dram_tensor("out", [CH, HD, D], f32, kind="ExternalOutput").ap()
    program(nc, ins, out)
    result = run_bass_kernel_spmd(nc, [{f"in_{n}": v for n, v in arrays.items()}], core_ids=[0])
    return result.results[0]["out"]
```

```python
from contextlib import ExitStack

import numpy as np

import concourse.bass as bass
from concourse import mybir

f32 = mybir.dt.float32
f32r = mybir.dt.float32r
ALU = mybir.AluOpType
ACT = mybir.ActivationFunctionType
AX = mybir.AxisListType.X

P = 128
HD, NS, SEQ, CH = 64, 64, 512, 64
QH, GH = 16, 4
NQ, NG = HD // QH, QH // GH
INV = 10
DBL = 8
XC = 2 ** DBL
D, NHEAD, DH = 512, 16, 128
KC = D // P
TOK = CH * HD
HALVES = 2
TH = TOK // HALVES
TG = 512
NTG, TPG = TH // TG, TG // P
NT = TH // P
T = HD
NEXP, TOPK, HID = 8, 6, 256
NSH = 2
HC = HID // P
ITEMS = NHEAD + TOPK + NSH
SCALE = float(DH) ** -0.5
MASKED = -1e30
EPS = 1e-5
WCOLS = 2 * KC * HID + HC * D
ACOLS = 3 * KC * DH + D
SCOLS = KC * HID + HC * D


class Steps:

    def __init__(self, names):
        self.at = {n: i + 1 for i, n in enumerate(names)}
        self.n = len(names)

    def after(self, q, *name):
        return q * self.n + self.at[name]


def ssm_steps():
    G = range(NG)
    pe = [("G", g) for g in G]
    dve = [("B", g) for g in G] + [("G", g) for g in G] + [("rowsum", g) for g in G]
    dve += [(x, g) for g in G for x in ("M", "Q")]
    act = [("B", g) for g in G] + [("G", g) for g in G]
    for k in range(INV):
        pe += [("N", k, g) for g in G]
        dve += [(x, k, g) for g in G for x in ("S", "N") if x == "N" or k < INV - 1]
        if k < INV - 1:
            act += [("N", k, g) for g in G]
    dve += [("P", g) for g in G]
    act += [("P", g) for g in G]
    pe += [("T", 0, g) for g in G] + [("b", g) for g in G]
    dve += [("T", 0, g) for g in G]
    dve += [(x, g) for g in G for x in ("b+", "b")]
    for j in range(DBL):
        pe += [("K", j, g) for g in G]
        dve += [("K", j, g) for g in G]
        act += [(x, j, g) for g in G for x in ("K", "X")]
        if j < DBL - 1:
            pe += [("T", j + 1, g) for g in G]
            dve += [("T", j + 1, g) for g in G]
    pe += [("Y", g) for g in G] + [("F", g) for g in G]
    dve += [("C",)] + [("F", g) for g in G]
    act += [("Y", g) for g in G] + [("F", g) for g in G]
    return Steps(pe), Steps(dve), Steps(act)


def ssm_program(nc, ins, hbuf, m, s):
    PE, DV, AC = ssm_steps()
    SR = m["zmat"]
    ET = m["zmat_t"]
    lo, hi = slice(0, 64), slice(64, 128)

    def grp(g):
        return slice(g * GH, (g + 1) * GH)

    def bank_a(g):
        return m["bank"][g][:, :]

    def bank_b(g):
        return m["bank"][NG + g][:, :]

    def a4(g, cols):
        return bank_a(g)[:, 0:GH * cols].rearrange("p (h c) -> p h c", h=GH)

    def b4(g, cols):
        return bank_b(g)[:, 0:GH * cols].rearrange("p (h c) -> p h c", h=GH)

    def heads(q):
        return bass.ds(q * QH, QH)

    def half_dt(q, cols, count=QH, at=0):
        return m["hdt"][:, bass.ds(q * QH + at, count)].unsqueeze(2).to_broadcast([P, count, cols])

    def sync(e, after_first):
        e.dma_start(m["hdt"][:, :], ins["log_dt"].partition_broadcast(P)).then_inc(s["small_in"][0], 16)
        e.dma_start(m["b_all"][:, 0:HD], ins["b"]).then_inc(s["small_in"][1], 16)
        def load(q):
            for k, (dst, src) in enumerate(((m["a_all"], "a"), (m["at_all"], "at"), (m["c_all"], "c"))):
                e.dma_start(dst[:, heads(q), :], ins[src][:, heads(q), :]).then_inc(s["ssm_in"][k], 16)

        load(0)
        after_first()
        with e.Fori(1, NQ) as q:
            for k in range(3):
                e.wait_ge(s["ssm_in"][k], 16 * q)
            e.sem_inc(s["turn_sp"], 1)
            load(q)

    def store(e):
        with e.Fori(0, NQ) as q:
            e.wait_ge(s["dve"], DV.after(q, "F", NG - 1))
            e.wait_ge(s["act"], AC.after(q, "F", NG - 1))
            for blk in range(2):
                e.dma_start(hbuf[:, bass.ds(q * QH, QH), blk * XC:(blk + 1) * XC],
                            m["outb"][64 * blk:64 * blk + 64, :, :]).then_inc(s["rows_out"][blk], 16)
            for blk in range(2):
                e.wait_ge(s["rows_out"][blk], 16 * (q + 1))
            e.sem_inc(s["outb_free"], 1)

    def vector(e):
        v = nc.vector
        v.memset(m["sign"][0:64, :], 1.0).then_inc(s["const_v"], 1)
        v.memset(m["sign"][64:128, :], -1.0).then_inc(s["const_v"], 1)
        v.memset(m["b_all"][:, HD:], 0.0)
        v.memset(m["cy"][:, :, 64:128], 0.0)
        e.wait_ge(s["const_v"], 2)
        e.wait_ge(s["ident_ready"], 1)
        eye = m["ident"][:, 0:64].unsqueeze(1)
        links = 4 + NG
        with e.Fori(0, NQ) as q:
            e.wait_ge(s["ssm_in"][0], 16 * (q + 1))
            e.wait_ge(s["dt_ready"], 1)
            v.tensor_tensor(m["tmp"][:, :, :], m["a_all"][:, heads(q), :], half_dt(q, 64), ALU.mult).then_inc(s["link"], 1)
            e.wait_ge(s["link"], links * q + 1)
            for g in range(NG):
                v.tensor_tensor(SR[:, grp(g), 0:64], eye.to_broadcast([P, GH, 64]), m["tmp"][:, grp(g), :],
                                ALU.subtract).then_inc(s["dve"], 1)
            e.wait_ge(s["ssm_in"][1], 16 * (q + 1))
            e.wait_ge(s["dve"], DV.after(q, "B", NG - 1))
            v.scalar_tensor_tensor(m["tmp"][:, :, :], m["at_all"][:, heads(q), :], m["sign"][:, 0:1],
                                   half_dt(q, 64), ALU.mult, ALU.mult).then_inc(s["link"], 1)
            e.wait_ge(s["link"], links * q + 2)
            v.tensor_tensor(m["tmp"][:, :, :], eye.to_broadcast([P, QH, 64]), m["tmp"][:, :, :],
                            ALU.subtract).then_inc(s["link"], 1)
            for g in range(NG):
                e.wait_ge(s["pe"], PE.after(q, "G", g))
                v.tensor_copy(SR[:, grp(g), 0:64], a4(g, 128)[:, :, 0:64]).then_inc(s["dve"], 1)
            for g in range(NG):
                e.wait_ge(s["act"], AC.after(q, "G", g))
                v.tensor_reduce(m["rowsum"][:, grp(g)], SR[:, grp(g), 0:128], axis=AX, op=ALU.add,
                                apply_absolute_value=True).then_inc(s["dve"], 1)
            e.wait_ge(s["norm_ready"], q + 1)
            v.reciprocal(m["alpha"][:, :], m["norm"][:, :]).then_inc(s["link"], 1)
            e.wait_ge(s["link"], links * q + 4)
            for g in range(NG):
                by_alpha = m["alpha"][:, grp(g)].unsqueeze(2)
                v.tensor_tensor(SR[:, grp(g), 0:128], SR[:, grp(g), 0:128], by_alpha.to_broadcast([P, GH, 128]),
                                ALU.mult).then_inc(s["link"], 1)
                e.wait_ge(s["link"], links * q + 5 + g)
                v.tensor_tensor(SR[:, grp(g), 0:128], m["ident"][:, :].unsqueeze(1).to_broadcast([P, GH, 128]),
                                SR[:, grp(g), 0:128], ALU.subtract).then_inc(s["dve"], 1)
                v.tensor_tensor(SR[:, grp(g), 128:192], m["tmp"][:, grp(g), :], by_alpha.to_broadcast([P, GH, 64]),
                                ALU.mult).then_inc(s["dve"], 1)
            for k in range(INV):
                for g in range(NG):
                    e.wait_ge(s["pe"], PE.after(q, "N", k, g))
                    if k == INV - 1:
                        v.tensor_tensor(SR[:, grp(g), 128:192], SR[:, grp(g), 128:192],
                                        a4(g, 128)[:, :, 64:128], ALU.add).then_inc(s["dve"], 1)
                    else:
                        v.tensor_copy(SR[:, grp(g), 0:64], a4(g, 128)[:, :, 0:64]).then_inc(s["dve"], 1)
                        v.tensor_tensor(SR[:, grp(g), 128:192], SR[:, grp(g), 128:192],
                                        a4(g, 128)[:, :, 64:128], ALU.add).then_inc(s["dve"], 1)
            for g in range(NG):
                e.wait_ge(s["dve"], DV.after(q, "N", INV - 1, g))
                v.scalar_tensor_tensor(SR[:, grp(g), 0:64], SR[:, grp(g), 128:192], 2.0,
                                       eye.to_broadcast([P, GH, 64]), ALU.mult, ALU.subtract).then_inc(s["dve"], 1)

            def transposed(j, g):
                e.wait_ge(s["pe"], PE.after(q, "T", j, g))
                v.tensor_copy(ET[:, grp(g), :], b4(g, 128)).then_inc(s["dve"], 1)

            for g in range(NG):
                transposed(0, g)
            for g in range(NG):
                e.wait_ge(s["pe"], PE.after(q, "b", g))
                v.tensor_tensor(SR[:, grp(g), 128:129], m["b_all"][:, bass.ds(q * QH + g * GH, GH)].unsqueeze(2),
                                a4(g, 128)[:, :, 0:1], ALU.add).then_inc(s["dve"], 1)
                e.wait_ge(s["dve"], DV.after(q, "b+", g))
                v.tensor_tensor(SR[:, grp(g), 128:129], SR[:, grp(g), 128:129], half_dt(q, 1, GH, g * GH),
                                ALU.mult).then_inc(s["dve"], 1)
            for j in range(DBL):
                for g in range(NG):
                    e.wait_ge(s["pe"], PE.after(q, "K", j, g))
                    v.tensor_copy(SR[:, grp(g), 0:64], a4(g, 128)[:, :, 0:64]).then_inc(s["dve"], 1)
                if j < DBL - 1:
                    for g in range(NG):
                        transposed(j + 1, g)
            e.wait_ge(s["ssm_in"][2], 16 * (q + 1))
            v.tensor_scalar(m["cy"][:, :, 0:64], m["c_all"][:, heads(q), :], m["sign"][:, 0:1], None,
                            ALU.mult).then_inc(s["dve"], 1)
            e.wait_ge(s["outb_free"], q + 1)
            for g in range(NG):
                e.wait_ge(s["pe"], PE.after(q, "F", g))
                v.tensor_copy(m["outb"][:, g * GH:g * GH + 2, :],
                              bank_a(g).rearrange("p (h c) -> p h c", h=2)).then_inc(s["dve"], 1)

    def scalar(e, beside_inverse):
        c = nc.scalar
        e.wait_ge(s["small_in"][0], 16)
        c.activation(m["hdt"][:, :], m["hdt"][:, :], ACT.Exp).then_inc(s["link_a"], 1)
        e.wait_ge(s["link_a"], 1)
        c.activation(m["hdt"][:, :], m["hdt"][:, :], ACT.Copy, scale=0.5).then_inc(s["dt_ready"], 1)

        def rotate(z):
            c.activation(z[lo, :, 64:128], z[hi, :, 0:64], ACT.Copy, scale=-1.0)
            return c.activation(z[hi, :, 64:128], z[lo, :, 0:64], ACT.Copy)

        with e.Fori(0, NQ) as q:
            for g in range(NG):
                e.wait_ge(s["dve"], DV.after(q, "B", g))
                rotate(SR[:, grp(g), :]).then_inc(s["act"], 1)
            for g in range(NG):
                e.wait_ge(s["dve"], DV.after(q, "G", g))
                rotate(SR[:, grp(g), :]).then_inc(s["act"], 1)
            beside_inverse(q)
            for k in range(INV - 1):
                for g in range(NG):
                    e.wait_ge(s["dve"], DV.after(q, "S", k, g))
                    rotate(SR[:, grp(g), :]).then_inc(s["act"], 1)
            for g in range(NG):
                e.wait_ge(s["dve"], DV.after(q, "P", g))
                rotate(SR[:, grp(g), :]).then_inc(s["act"], 1)
            for j in range(DBL):
                n = 2 ** j
                for g in range(NG):
                    e.wait_ge(s["dve"], DV.after(q, "K", j, g))
                    rotate(SR[:, grp(g), :]).then_inc(s["act"], 1)
                    if n < 64:
                        c.activation(SR[:, grp(g), 128 + n:128 + 2 * n], a4(g, 128)[:, :, 64:64 + n],
                                     ACT.Copy).then_inc(s["act"], 1)
                    elif n == 64:
                        c.activation(m["xk"][:, grp(g), 0:n], SR[:, grp(g), 128:192], ACT.Copy)
                        c.activation(m["xk"][:, grp(g), n:2 * n], a4(g, 128)[:, :, 64:128], ACT.Copy).then_inc(s["act"], 1)
                    else:
                        c.activation(m["xk"][:, grp(g), n:2 * n], b4(g, n), ACT.Copy).then_inc(s["act"], 1)
            for g in range(NG):
                e.wait_ge(s["pe"], PE.after(q, "Y", g))
                c.activation(m["cy"][:, grp(g), 64:128], a4(g, 128)[:, :, 0:64], ACT.Copy).then_inc(s["act"], 1)
            e.wait_ge(s["outb_free"], q + 1)
            for g in range(NG):
                e.wait_ge(s["pe"], PE.after(q, "F", g))
                c.activation(m["outb"][:, g * GH + 2:g * GH + 4, :],
                             bank_b(g).rearrange("p (h c) -> p h c", h=2), ACT.Copy).then_inc(s["act"], 1)

    def gpsimd(e, beside_inverse):
        with e.Fori(0, NQ) as q:
            e.wait_ge(s["dve"], DV.after(q, "rowsum", NG - 1))
            e.sem_inc(s["turn_pool"], 1)
            nc.gpsimd.partition_all_reduce(m["norm"][:, :], m["rowsum"][:, :], P,
                                           bass.bass_isa.ReduceOp.max).then_inc(s["norm_ready"], 1)
            beside_inverse(q)

    def tensor(e):
        mm = nc.tensor.matmul

        def s_and_third(h):
            return SR[:, h, :].rearrange("p (b c) -> p b c", b=3)[:, 0:3:2, :]

        with e.Fori(0, NQ) as q:
            for g in range(NG):
                e.wait_ge(s["act"], AC.after(q, "B", g))
                for i in range(GH):
                    h = g * GH + i
                    last = mm(a4(g, 128)[:, i, :], SR[:, h, 0:128], SR[:, h, 0:128], start=True, stop=True)
                last.then_inc(s["pe"], 1)
            for k in range(INV):
                for g in range(NG):
                    if k == 0:
                        e.wait_ge(s["dve"], DV.after(q, "Q", g))
                    else:
                        e.wait_ge(s["dve"], DV.after(q, "N", k - 1, g))
                        e.wait_ge(s["act"], AC.after(q, "N", k - 1, g))
                    for i in range(GH):
                        h = g * GH + i
                        last = mm(a4(g, 128)[:, i, :], SR[:, h, 0:128], s_and_third(h), start=True, stop=True)
                    last.then_inc(s["pe"], 1)

            def transpose(j, g):
                if j == 0:
                    e.wait_ge(s["act"], AC.after(q, "P", g))
                else:
                    e.wait_ge(s["dve"], DV.after(q, "K", j - 1, g))
                    e.wait_ge(s["act"], AC.after(q, "X", j - 1, g))
                for i in range(GH):
                    last = nc.tensor.transpose(b4(g, 128)[:, i, :], SR[:, g * GH + i, 0:128], m["ident"][:, :])
                last.then_inc(s["pe"], 1)

            for g in range(NG):
                transpose(0, g)
            e.wait_ge(s["small_in"][1], 16)
            for g in range(NG):
                e.wait_ge(s["dve"], DV.after(q, "T", 0, g))
                for i in range(GH):
                    h = g * GH + i
                    last = mm(a4(g, 128)[:, i, :], ET[:, h, :], m["b_all"][:, bass.ds(q * QH + h, P)],
                              start=True, stop=True)
                last.then_inc(s["pe"], 1)
            for j in range(DBL):
                n = 2 ** j
                for g in range(NG):
                    e.wait_ge(s["dve"], DV.after(q, "b", g) if j == 0 else DV.after(q, "T", j, g))
                    for i in range(GH):
                        h = g * GH + i
                        if n <= 64:
                            last = mm(a4(g, 128)[:, i, :], ET[:, h, :], s_and_third(h), start=True, stop=True)
                        else:
                            mm(a4(g, 128)[:, i, :], ET[:, h, :], SR[:, h, 0:128], start=True, stop=True)
                            last = mm(b4(g, n)[:, i, :], ET[:, h, :], m["xk"][:, h, 0:n], start=True, stop=True)
                    last.then_inc(s["pe"], 1)
                if j < DBL - 1:
                    for g in range(NG):
                        transpose(j + 1, g)
            e.wait_ge(s["dve"], DV.after(q, "C"))
            for g in range(NG):
                e.wait_ge(s["act"], AC.after(q, "X", DBL - 1, g))
                for i in range(GH):
                    h = g * GH + i
                    last = mm(a4(g, 128)[:, i, :], SR[:, h, 0:128], m["cy"][:, h, :], start=True, stop=True)
                last.then_inc(s["pe"], 1)
            for g in range(NG):
                e.wait_ge(s["act"], AC.after(q, "Y", g))
                for i in range(GH):
                    h = g * GH + i
                    bank = bank_a(g) if i < 2 else bank_b(g)
                    last = mm(bank[:, (i % 2) * XC:(i % 2 + 1) * XC], m["cy"][:, h, :], m["xk"][:, h, :],
                              start=True, stop=True)
                last.then_inc(s["pe"], 1)

    return dict(sync=sync, store=store, vector=vector, scalar=scalar, gpsimd=gpsimd, tensor=tensor)


def token_program(nc, ins, hbuf, wscr, out, m, s):
    HU, VU = NHEAD * NTG, (TOPK + NSH) * NTG
    BQ, BK, BV, BS, BT, BY, BO0, BO1 = (m["bank"][i][:, :] for i in range(8))
    BO = [BO0, BO1, BT, BY]
    BL = [BO0, BO1]
    BR = [BT, BY]
    BG, BU = [BQ, BV], [BK, BS]

    def tile_cols(t):
        return slice(t * P, (t + 1) * P)

    def group_cols(tg):
        return slice(tg * TG, (tg + 1) * TG)

    def pairs(bank):
        return bank.rearrange("p (i c) -> p i c", i=TPG)

    def w_proj(k, which):
        return slice((which * KC + k) * DH, (which * KC + k + 1) * DH)

    W_OUT = slice(3 * KC * DH, ACOLS)

    def w_hid(k, which, j):
        at = (which * KC + k) * HID + j * P
        return slice(at, at + P)

    def w_down(j, shared):
        at = (1 if shared else 2) * KC * HID + j * D
        return slice(at, at + D)

    def three(out_ap, hi, lo, rhi, rlo, start, stop):
        nc.tensor.matmul(out_ap, hi, rhi, start=start, stop=False)
        nc.tensor.matmul(out_ap, hi, rlo, start=False, stop=False)
        return nc.tensor.matmul(out_ap, lo, rhi, start=False, stop=stop)

    def split_hi(dst, src):
        return nc.scalar.activation(dst, src, ACT.Copy)

    def split_lo(dst, src, hi):
        return nc.vector.tensor_tensor(dst, src, hi.bitcast(f32), ALU.subtract)

    def pieces(cols):
        step = -(-cols // 3 // P) * P
        return [(a, min(a + step, cols)) for a in range(0, cols, step)]

    def item_hi(e, n, par, cols, k):
        a, b = pieces(cols)[k]
        e.wait_ge(s["raw_loaded"], 16 * (n + 1))
        e.wait_ge(s["o_done"], 16 * (n - 1) + 1)
        nc.scalar.activation(m["whi"][:, par, a:b], m["raw"][:, a:b], ACT.Copy).then_inc(s["w_hi"], 1)

    def item_lo(e, n, par, cols, bias, between=()):
        for k, (a, b) in enumerate(pieces(cols)):
            e.wait_ge(s["w_hi"], 3 * n + k + 1)
            last = nc.gpsimd.tensor_tensor(m["wlo"][:, par, a:b], m["raw"][:, a:b],
                                           m["whi"][:, par, a:b].bitcast(f32), ALU.subtract)
            if bias and k == 2:
                last = nc.gpsimd.tensor_copy(m["ebias"][:, par, 0:bias], m["raw"][:, cols:cols + bias])
            if k < len(between):
                between[k]()
        last.then_inc(s["w_ready"], 1)

    def norm_group(hf, phase, tg):
        return (hf * 2 + phase) * NTG + tg

    def dve_stats(e, hf, phase, tg):
        v, g = nc.vector, norm_group(hf, phase, tg)
        if phase == 0:
            e.wait_ge(s["acc_loaded"][tg], 16 * (hf + 1))
        else:
            e.wait_ge(s["o_added"], 4 * (hf * (HU + VU) + HU - NTG + tg + 1) + 4)
        for i in range(TPG):
            last = v.bn_stats(m["stats"][:, i, :], m["acc"][:, tg * TPG + i, :])
        last.then_inc(s["ln_stats"], 1)
        e.wait_ge(s["ln_stats"], g + 1)
        e.sem_inc(s["turn_dve"], 1)
        for i in range(TPG):
            last = v.bn_aggr(m["mean_var"][:, i, :], m["stats"][:, i, :])
        last.then_inc(s["ln_aggr"], 1)

    def dve_normalise(e, hf, phase, tg, i):
        g = norm_group(hf, phase, tg)
        if i == 0:
            e.wait_ge(s["ln_rstd"], g + 1)
            e.sem_inc(s["turn_dve"], 1)
        e.wait_ge(s["xn_turned"], g * TPG + i + 1)
        e.sem_inc(s["turn_dve"], 1)
        nc.vector.tensor_scalar(m["xn"][:, i % 2, :], m["acc"][:, tg * TPG + i, :], m["mean_var"][:, i, 0:1],
                                m["rstd"][:, i:i + 1], ALU.subtract, ALU.mult).then_inc(s["xn_ready"], 1)

    def dve_norm(e, hf, phase, tg, i):
        tile = norm_group(hf, phase, tg) * TPG + i
        e.wait_ge(s["x_hi"], tile + 1)
        cols = tile_cols(tg * TPG + i)
        split_lo(m["xlo"][:, :, cols], pairs(BL[i % 2]), m["xhi"][:, :, cols]).then_inc(s["x_split"], 1)

    def dve_norm_alone(e, hf, phase, tg):
        dve_normalise(e, hf, phase, tg, 0)
        if phase == 1:
            dve_gate(e, hf, tg - 1)
        for i in range(TPG):
            if i + 1 < TPG:
                dve_normalise(e, hf, phase, tg, i + 1)
            dve_norm(e, hf, phase, tg, i)

    def dve_gate(e, hf, tg):
        e.wait_ge(s["gate_turned"], hf * NTG + tg + 1)
        nc.vector.tensor_tensor(m["gate"][:, tg * TPG:(tg + 1) * TPG, :],
                                BO1[:, 0:TPG * NEXP].rearrange("p (t x) -> p t x", t=TPG),
                                m["bg"][:, :].unsqueeze(1).to_broadcast([P, TPG, NEXP]), ALU.add).then_inc(s["gate_read"], 1)

    def pool_norm(e, hf, phase, tg):
        p, g = nc.gpsimd, norm_group(hf, phase, tg)
        e.wait_ge(s["ln_aggr"], g + 1)
        e.sem_inc(s["turn_pool"], 1)
        p.tensor_scalar(m["var_eps"][:, :], m["mean_var"][:, :, 1], EPS, None, ALU.add).then_inc(s["ln_eps"], 1)
        e.wait_ge(s["ln_eps"], g + 1)
        p.tensor_tensor(m["rstd"][:, :], m["var_eps"][:, :], m["neg_half"][:, :], ALU.pow).then_inc(s["ln_rstd"], 1)

    def act_norm(e, hf, phase, tg, i):
        e.wait_ge(s["xn_turned"], norm_group(hf, phase, tg) * TPG + i + 3)
        split_hi(m["xhi"][:, :, tile_cols(tg * TPG + i)], pairs(BL[i % 2])).then_inc(s["x_hi"], 1)

    def pe_norm(e, hf, phase, tg, i):
        tile = norm_group(hf, phase, tg) * TPG + i
        e.wait_ge(s["xn_ready"], tile + 1)
        e.wait_ge(s["x_split"], tile + 1)
        for k in range(KC):
            last = nc.tensor.transpose(pairs(BL[i % 2])[:, k, :], m["xn"][:, i % 2, tile_cols(k)], m["ident"][:, :])
        last.then_inc(s["xn_turned"], 1)

    def pe_gate(e, hf, tg):
        e.wait_ge(s["x_split"], (norm_group(hf, 1, tg) + 1) * TPG + 2)
        for k in range(KC):
            last = three(BO0[0:NEXP, :], m["wg_hi"][:, k, :], m["wg_lo"][:, k, :], m["xhi"][:, k, group_cols(tg)],
                         m["xlo"][:, k, group_cols(tg)], k == 0, k == KC - 1)
        last.then_inc(s["gate_done"], 1)

    def act_gate(e, hf, tg):
        e.wait_ge(s["gate_done"], hf * NTG + tg + 1)
        nc.scalar.activation(m["gate_t"][0:NEXP, :], BO0[0:NEXP, :], ACT.Copy).then_inc(s["gate_copied"], 1)

    def pe_turn_gate(e, hf, tg):
        e.wait_ge(s["gate_copied"], hf * NTG + tg + 1)
        e.sem_inc(s["turn_pe"], 1)
        for i in range(TPG):
            last = nc.tensor.transpose(BO1[:, i * NEXP:(i + 1) * NEXP], m["gate_t"][0:NEXP, tile_cols(i)],
                                       m["ident"][0:NEXP, 0:NEXP])
        last.then_inc(s["gate_turned"], 1)

    def norms_beside(step):
        inside = {("start", 0): (0, 1), ("first", 0): (0, 2), ("first", 1): (0, 3)}
        inside.update({("last", 5 + tg): (1, tg) for tg in range(3)})
        after = {("start", 0): (0, 2), ("first", 0): (0, 3)}
        after.update({("last", 4 + tg): (1, tg) for tg in range(NTG)})
        return inside.get(step), after.get(step)

    def pe_project(e, which, bank, free, done, u, n, hf, tg, par):
        if which == 1:
            e.wait_ge(s["w_ready"], n + 1)
            e.wait_ge(s["x_split"], hf * 2 * NT + (tg + 1) * TPG + 2)
        e.wait_ge(free, u + 1)
        for k in range(KC):
            w = w_proj(k, which)
            last = three(bank, m["whi"][:, par, w], m["wlo"][:, par, w], m["xhi"][:, k, group_cols(tg)],
                         m["xlo"][:, k, group_cols(tg)], k == 0, k == KC - 1)
        last.then_inc(done, 1)

    def pe_scores(e, u):
        e.wait_ge(s["q_ready"], u + 2)
        e.wait_ge(s["k_ready"], u + 2)
        e.wait_ge(s["s_read"], u + 1)
        for i in range(TPG):
            c = tile_cols(i)
            last = nc.tensor.matmul(BS[:, c], m["qt"][:, c], m["kt"][:, c], start=True, stop=True)
        last.then_inc(s["s_done"], 1)

    def pe_turn_v(e, u):
        e.wait_ge(s["vt_copied"], u + 1)
        for i in range(TPG):
            last = nc.tensor.transpose(BV[:, tile_cols(i)], m["vt"][:, tile_cols(i)], m["ident"][:, :])
        last.then_inc(s["v_turned"], 1)

    def pe_turn_p(e, u, w):
        e.wait_ge(s["p_ready"], u + 1)
        e.wait_ge(s["o_added"], 4 * w + 3)
        for i in range(TPG):
            last = nc.tensor.transpose(BT[:, tile_cols(i)], m["prob"][:, i, :], m["ident"][:, :])
        last.then_inc(s["p_turned"], 1)

    def pe_mix(e, u, w):
        e.wait_ge(s["pt_ready"], u + 1)
        e.wait_ge(s["v_ready"], u + 2)
        e.wait_ge(s["o_added"], 4 * w + 4)
        for i in range(TPG):
            c = tile_cols(i)
            last = nc.tensor.matmul(BY[:, c], m["v"][:, c], m["pt"][:, c], start=True, stop=True)
        last.then_inc(s["y_done"], 1)

    def pe_out(e, u, w, par):
        e.wait_ge(s["y_split"], u + 1)
        for i in range(TPG):
            e.wait_ge(s["o_added"], 4 * w + i + 1)
            c = tile_cols(i)
            three(BO[i], m["yhi"][:, c], m["ylo"][:, c], m["whi"][:, par, W_OUT], m["wlo"][:, par, W_OUT],
                  True, True).then_inc(s["o_done"], 1)

    def over_heads(hf, step):
        step("start", 0, 0)
        for k in range(2 * NTG):
            step("first", 0, k)
        yield
        for k in range(2 * NTG):
            step("last", NHEAD // 2 - 1, k)

    def pe_attention(e, hf):
        def step(where, pair, k):
            first, last = where == "start", where == "last" and k == 2 * NTG - 1
            beside, _ = norms_beside((where, k))
            at = pair * 2 * NTG + k
            u, w = hf * HU + at, hf * (HU + VU) + at
            par, nxt, npar, ntg = k // NTG, u + 1, (k + 1) // NTG % 2, (k + 1) % NTG
            nn = hf * ITEMS + pair * 2 + (k + 1) // NTG
            if first:
                nxt, npar, ntg, nn = u, 0, 0, hf * ITEMS
            gates = beside[1] - 1 if beside and beside[0] == 1 and beside[1] else None
            if not last:
                pe_project(e, 1, BK, s["k_ready"], s["k_done"], nxt, nn, hf, ntg, npar)
            if not first:
                pe_turn_p(e, u, w)
            if gates is not None:
                pe_gate(e, hf, gates)
            if not last:
                pe_project(e, 0, BQ, s["q_ready"], s["q_done"], nxt, nn, hf, ntg, npar)
            if gates is not None:
                pe_turn_gate(e, hf, gates)
            if not first:
                pe_mix(e, u, w)
            if not last:
                pe_scores(e, nxt)
            if gates is not None:
                e.wait_ge(s["gate_read"], hf * NTG + gates + 1)
            if beside:
                pe_norm(e, hf, *beside, 0)
                pe_norm(e, hf, *beside, 1)
            if not last:
                pe_project(e, 2, BV, s["v_ready"], s["v_done"], nxt, nn, hf, ntg, npar)
            if beside:
                pe_norm(e, hf, *beside, 2)
                pe_norm(e, hf, *beside, 3)
                e.wait_ge(s["x_split"], (norm_group(hf, *beside) + 1) * TPG + 2)
            if not first:
                pe_out(e, u, w, par)
            if not last:
                pe_turn_v(e, nxt)

        units = over_heads(hf, step)
        next(units)
        with e.Fori(1, NHEAD // 2 - 1) as pair:
            for k in range(2 * NTG):
                step("", pair, k)
        for _ in units:
            pass

    def act_attention(e, hf):
        def step(where, pair, k):
            first, last = where == "start", where == "last" and k == 2 * NTG - 1
            beside, _ = norms_beside((where, k))
            u = hf * HU + pair * 2 * NTG + k
            nxt = u if first else u + 1
            gates = beside[1] - 1 if beside and beside[0] == 1 and beside[1] else None
            if not first:
                e.wait_ge(s["p_turned"], u + 1)
                nc.scalar.activation(m["pt"][:, :], BT, ACT.Copy).then_inc(s["pt_ready"], 1)
            if gates is not None:
                act_gate(e, hf, gates)
            if not first and k % NTG < 3:
                cols = WCOLS if where == "last" and k >= NTG else ACOLS
                item_hi(e, hf * ITEMS + pair * 2 + k // NTG + 1, (k // NTG + 1) % 2, cols, k % NTG)
            if not last:
                e.wait_ge(s["q_done"], nxt + 1)
                nc.scalar.activation(m["qt"][:, :], BQ, ACT.Copy).then_inc(s["q_ready"], 1)
            if not first:
                e.wait_ge(s["y_done"], u + 1)
                split_hi(m["yhi"][:, :], BY).then_inc(s["y_hi"], 1)
            if beside:
                act_norm(e, hf, *beside, 0)
                act_norm(e, hf, *beside, 1)
            if not last:
                e.wait_ge(s["row_sub"], nxt + 1)
                nc.scalar.activation(m["sm"][:, :, :], m["sm"][:, :, :], ACT.Exp).then_inc(s["p_exp"], 1)
                e.wait_ge(s["v_done"], nxt + 1)
                nc.scalar.activation(m["vt"][:, :], BV, ACT.Copy).then_inc(s["vt_copied"], 1)
            if beside:
                act_norm(e, hf, *beside, 2)
                act_norm(e, hf, *beside, 3)

        units = over_heads(hf, step)
        next(units)
        with e.Fori(1, NHEAD // 2 - 1) as pair:
            for k in range(2 * NTG):
                step("", pair, k)
        for _ in units:
            pass

    def add_output(e, w, tg, i):
        t = tg * TPG + i
        e.wait_ge(s["o_done"], 4 * w + i + 2)
        nc.vector.tensor_tensor(m["acc"][:, t, :], m["acc"][:, t, :], BO[i], ALU.add).then_inc(s["o_added"], 1)

    def dve_attention(e, hf):
        v = nc.vector
        rows = (slice(0, T), slice(T, P))

        def step(where, pair, k):
            first, last = where == "start", where == "last" and k == 2 * NTG - 1
            beside, after = norms_beside((where, k))
            at = pair * 2 * NTG + k
            u, w = hf * HU + at, hf * (HU + VU) + at
            nxt, tg = (u if first else u + 1), k % NTG
            gates = beside[1] - 1 if beside and beside[0] == 1 and beside[1] else None
            if not last:
                e.wait_ge(s["k_done"], nxt + 1)
                v.tensor_copy(m["kt"][:, :], BK).then_inc(s["k_ready"], 1)
            if beside:
                dve_normalise(e, hf, *beside, 0)
                dve_normalise(e, hf, *beside, 1)
            if gates is not None:
                dve_gate(e, hf, gates)
            if not first:
                e.wait_ge(s["y_hi"], u + 1)
                split_lo(m["ylo"][:, :], BY, m["yhi"][:, :]).then_inc(s["y_split"], 1)
            if not last:
                e.wait_ge(s["s_done"], nxt + 1)
                for r in rows:
                    got = v.scalar_tensor_tensor(m["sm"][r, :, :], pairs(BS)[r, :, r], SCALE,
                                                 m["mask"][r, :].unsqueeze(1).to_broadcast([T, TPG, T]),
                                                 ALU.mult, ALU.add)
                got.then_inc(s["s_read"], 1)
                e.wait_ge(s["s_read"], nxt + 2)
                v.tensor_reduce(m["rmax"][:, :], m["sm"][:, :, :], axis=AX, op=ALU.max).then_inc(s["row_max"], 1)
                e.wait_ge(s["row_max"], nxt + 1)
                v.tensor_tensor(m["sm"][:, :, :], m["sm"][:, :, :], m["rmax"][:, :].unsqueeze(2).to_broadcast([P, TPG, T]),
                                ALU.subtract).then_inc(s["row_sub"], 1)
            if beside:
                dve_norm(e, hf, *beside, 0)
                dve_norm(e, hf, *beside, 1)
                dve_normalise(e, hf, *beside, 2)
                dve_normalise(e, hf, *beside, 3)
            if not last:
                e.wait_ge(s["p_exp"], nxt + 1)
                v.tensor_reduce(m["rsum"][:, :], m["sm"][:, :, :], axis=AX, op=ALU.add).then_inc(s["row_sum"], 1)
                e.wait_ge(s["row_sum"], nxt + 1)
                v.reciprocal(m["rinv"][:, :], m["rsum"][:, :]).then_inc(s["row_inv"], 1)
                e.wait_ge(s["row_inv"], nxt + 1)
                if not first:
                    e.wait_ge(s["p_turned"], u + 1)
                for r in rows:
                    got = v.tensor_tensor(m["prob"][r, :, r], m["sm"][r, :, :],
                                          m["rinv"][r, :].unsqueeze(2).to_broadcast([T, TPG, T]), ALU.mult)
                got.then_inc(s["p_ready"], 1)
            if beside:
                dve_norm(e, hf, *beside, 2)
                dve_norm(e, hf, *beside, 3)
            if not first:
                for i in range(TPG):
                    add_output(e, w, tg, i)
            if not last:
                e.wait_ge(s["v_turned"], nxt + 1)
                v.tensor_copy(m["v"][:, :], BV).then_inc(s["v_ready"], 1)
            if after:
                dve_stats(e, hf, *after)

        for r, c in (rows, rows[::-1]):
            got = v.memset(m["prob"][r, :, c], 0.0)
        units = over_heads(hf, step)
        next(units)
        with e.Fori(1, NHEAD // 2 - 1) as pair:
            for k in range(2 * NTG):
                step("", pair, k)
        for _ in units:
            pass

    def dve_route(e, hf):
        v = nc.vector
        made = [0]

        def link(op):
            made[0] += 1
            op.then_inc(s["route"], 1)
            e.wait_ge(s["route"], hf * ROUTE_END + made[0])

        e.wait_ge(s["gate_read"], (hf + 1) * NTG)
        gate = m["gate"][:, :, :]
        by_e = gate.unsqueeze(3).to_broadcast([P, NT, NEXP, NEXP])
        by_j = gate.unsqueeze(2).to_broadcast([P, NT, NEXP, NEXP])
        link(v.tensor_tensor(m["before"][:, :, :, :], by_j, by_e, ALU.is_gt))
        link(v.tensor_tensor(m["ties"][:, :, :, :], by_j, by_e, ALU.is_equal))
        link(v.tensor_tensor(m["ties"][:, :, :, :], m["ties"][:, :, :, :],
                             m["tri"][:, :, :].unsqueeze(1).to_broadcast([P, NT, NEXP, NEXP]), ALU.mult))
        link(v.tensor_tensor(m["before"][:, :, :, :], m["before"][:, :, :, :], m["ties"][:, :, :, :], ALU.add))
        link(v.tensor_reduce(m["keep"][:, :, :], m["before"][:, :, :, :], axis=AX, op=ALU.add))
        link(v.tensor_scalar(m["keep"][:, :, :], m["keep"][:, :, :], TOPK - 0.5, None, ALU.is_lt))
        link(v.tensor_reduce(m["gmax"][:, :], gate, axis=AX, op=ALU.max))
        link(v.tensor_tensor(gate, gate, m["gmax"][:, :].unsqueeze(2).to_broadcast([P, NT, NEXP]), ALU.subtract))
        e.wait_ge(s["gate_exp"], hf + 1)
        link(v.tensor_tensor(gate, gate, m["keep"][:, :, :], ALU.mult))
        link(v.tensor_reduce(m["gmax"][:, :], gate, axis=AX, op=ALU.add))
        link(v.reciprocal(m["gmax"][:, :], m["gmax"][:, :]))
        link(v.tensor_tensor(m["w8"][:, :, 0:TOPK], gate[:, :, 0:TOPK],
                             m["gmax"][:, :].unsqueeze(2).to_broadcast([P, NT, TOPK]), ALU.mult))
        link(v.tensor_copy(m["w8hi"][:, :, :], m["w8"][:, :, :]))
        link(v.tensor_copy(m["ws"][:, :, 0:NEXP], m["w8hi"][:, :, :].bitcast(f32)))
        link(v.tensor_tensor(m["ws"][:, :, 32:32 + NEXP], m["w8"][:, :, :], m["w8hi"][:, :, :].bitcast(f32), ALU.subtract))
        link(v.tensor_copy(m["ws"][:, :, 64:64 + NEXP], m["w8hi"][:, :, :].bitcast(f32)))
        link(v.tensor_copy(m["ws"][:, :, 96:96 + NEXP], m["w8"][:, :, :]))
        assert made[0] == ROUTE_END

    ROUTE_SUB, ROUTE_END = 8, 17

    def act_route(e, hf):
        e.wait_ge(s["route"], hf * ROUTE_END + ROUTE_SUB)
        nc.scalar.activation(m["gate"][:, :, :], m["gate"][:, :, :], ACT.Exp).then_inc(s["gate_exp"], 1)
        for tg in range(NTG):
            e.wait_ge(s["w_turned"], hf * NTG + tg + 1)
            nc.scalar.activation(m["w3t"][:, group_cols(tg)], BR[tg % 2], ACT.Copy)
            nc.scalar.activation(m["w8t"][96:128, group_cols(tg)], BR[tg % 2][96:128, :], ACT.Copy).then_inc(s["wt_ready"], 1)

    def pe_route(e, hf):
        e.wait_ge(s["route"], (hf + 1) * ROUTE_END)
        for tg in range(NTG):
            if tg >= 2:
                e.wait_ge(s["wt_ready"], hf * NTG + tg - 1)
            for i in range(TPG):
                last = nc.tensor.transpose(BR[tg % 2][:, tile_cols(i)], m["ws"][:, tg * TPG + i, :], m["ident"][:, :])
            last.then_inc(s["w_turned"], 1)
        e.wait_ge(s["wt_ready"], (hf + 1) * NTG)
        e.sem_inc(s["turn_pe"], 1)

    def pe_hidden(e, v, r, n, hf, tg, par, shared):
        e.wait_ge(s["w_ready"], n + 1)
        e.wait_ge(s["x_split"], hf * 2 * NT + NT + (tg + 1) * TPG + 2)
        for j in range(HC):
            for which, bank, done in ((0, BG[j], s["g_done"]), (1, BU[j], s["u_done"])):
                if which and shared:
                    continue
                if which:
                    e.wait_ge(s["u_used"], 2 * r + j + 1)
                else:
                    e.wait_ge(s["g_used"], 2 * v + j + 1)
                for k in range(KC):
                    c = w_hid(k, which, j)
                    last = three(bank, m["whi"][:, par, c], m["wlo"][:, par, c], m["xhi"][:, k, group_cols(tg)],
                                 m["xlo"][:, k, group_cols(tg)], k == 0, k == KC - 1)
                last.then_inc(done, 1)

    def pe_down(e, v, w, k8, par, shared, bias=False):
        slot = k8 % 2
        e.wait_ge(s["hid_split"], 2 * v + 4)
        for i in range(TPG):
            e.wait_ge(s["o_added"], 4 * w + i + 1)
            c = tile_cols(i)
            if bias:
                nc.tensor.matmul(BO[i], m["w3t"][:, tile_cols(k8 % NTG * TPG + i)], m["bd3"][:, :], start=True, stop=False)
            for j in range(HC):
                d = w_down(j, shared)
                last = three(BO[i], m["hhi"][:, slot, j, c], m["hlo"][:, slot, j, c], m["whi"][:, par, d],
                             m["wlo"][:, par, d], j == 0 and not bias, j == HC - 1)
            last.then_inc(s["o_done"], 1)

    def pe_experts(e, hf):
        v0, w0, r0, n0 = hf * VU, hf * (HU + VU) + HU, hf * TOPK * NTG, hf * ITEMS + NHEAD

        def step(at, item, k, shared, next_shared, last=False):
            if not last:
                pe_hidden(e, v0 + at + 1, r0 + at + 1, n0 + item + (1 if k % NTG == NTG - 1 else 0), hf,
                          (k + 1) % NTG, (k + 1) // NTG % 2, next_shared)
            pe_down(e, v0 + at, w0 + at, k, k // NTG, shared, bias=shared and k >= NTG)

        pe_route(e, hf)
        with e.Fori(0, 2) as pair:
            for k in range(8):
                step(pair * 8 + k, pair * 2 + k // NTG, k, False, False)
        for k in range(8):
            step(16 + k, 4 + k // NTG, k, False, k == 7)
        for k in range(8):
            step(24 + k, 6 + k // NTG, k, True, True, last=k == 7)

    def act_experts(e, hf):
        v0, r0, n0 = hf * VU, hf * TOPK * NTG, hf * ITEMS + NHEAD

        def hidden(at, k, shared):
            par, slot = k // NTG, k % 2
            v, r = v0 + at, r0 + at
            for j in range(HC):
                e.wait_ge(s["g_done"], 2 * v + j + 1)
                e.wait_ge(s["hid_split"], 2 * v + j + 1)
                nc.scalar.activation(m["sg"][:, j, :], BG[j], ACT.Silu,
                                     bias=m["ebias"][:, par, j:j + 1]).then_inc(s["g_used"], 1)
            for j in range(HC):
                if shared:
                    e.wait_ge(s["g_used"], 2 * v + j + 3)
                else:
                    e.wait_ge(s["hd_ready"], 2 * r + j + 5)
                split_hi(m["hhi"][:, slot, j, :], m["sg"][:, j, :]).then_inc(s["hid_hi"], 1)

        def step(at, item, k, next_shared, cols, last=False):
            if not last:
                hidden(at + 1, (k + 1) % 8, next_shared)
            if k % NTG < 3:
                item_hi(e, n0 + item + 1, (k // NTG + 1) % 2, cols, k % NTG)

        hidden(0, 0, False)
        with e.Fori(0, 2) as pair:
            for k in range(8):
                step(pair * 8 + k, pair * 2 + k // NTG, k, False, WCOLS)
        for k in range(8):
            step(16 + k, 4 + k // NTG, k, k == 7, WCOLS if k < NTG else SCOLS)
        for k in range(8):
            step(24 + k, 6 + k // NTG, k, True, SCOLS if k < NTG else ACOLS, last=k == 7)

    def dve_experts(e, hf):
        vec = nc.vector
        v0, w0, r0 = hf * VU, hf * (HU + VU) + HU, hf * TOPK * NTG

        def hidden(at, half_at, k, shared):
            par, slot = k // NTG, k % 2
            v, r = v0 + at, r0 + at
            for j in range(HC if not shared else 0):
                e.wait_ge(s["g_used"], 2 * v + j + 3)
                e.wait_ge(s["u_done"], 2 * r + j + 1)
                vec.scalar_tensor_tensor(m["sg"][:, j, :], BU[j], m["ebias"][:, par, HC + j:HC + j + 1],
                                         m["sg"][:, j, :], ALU.add, ALU.mult).then_inc(s["u_used"], 1)
                e.wait_ge(s["u_used"], 2 * r + j + 3)
                e.wait_ge(s["wb_loaded"][slot], 16 * (hf * (TOPK * NTG // 2) + half_at + 1))
                vec.tensor_tensor(m["sg"][:, j, :], m["sg"][:, j, :], m["wb"][:, slot, :], ALU.mult).then_inc(s["hd_ready"], 1)
            for j in range(HC):
                e.wait_ge(s["hid_hi"], 2 * v + j + 1)
                split_lo(m["hlo"][:, slot, j, :], m["sg"][:, j, :], m["hhi"][:, slot, j, :]).then_inc(s["hid_split"], 1)

        def step(at, half_next, k, next_shared, last=False):
            if not last:
                hidden(at + 1, half_next, (k + 1) % 8, next_shared)
            for i in range(TPG):
                add_output(e, w0 + at, k % NTG, i)

        hidden(0, 0, 0, False)
        with e.Fori(0, 2) as pair:
            for k in range(8):
                step(pair * 8 + k, pair * 4 + (k + 1) // 2, k, False)
        for k in range(8):
            step(16 + k, 8 + (k + 1) // 2, k, k == 7)
        for k in range(8):
            step(24 + k, None, k, True, last=k == 7)

    def load_item(e, n, src, cols):
        e.wait_ge(s["w_ready"], n)
        e.dma_start(m["raw"][:, 0:cols], src).then_inc(s["raw_loaded"], 16)

    def load_acc(e, half, tg):
        t0 = half * NT + tg * TPG
        e.dma_start(m["acc"][:, tg * TPG:(tg + 1) * TPG, :],
                    tokens(hbuf)[:, t0:t0 + TPG, :]).then_inc(s["acc_loaded"][tg], 16)

    def tokens(dram):
        return dram.rearrange("c h l -> (c h) l").rearrange("(t p) l -> p t l", p=P)

    def sync(e):
        for half in range(HALVES):
            n0 = half * ITEMS
            if half == 0:
                for tg in range(NTG):
                    load_acc(e, 0, tg)
            with e.Fori(1, NHEAD) as head:
                load_item(e, n0 + head, ins["wattn"][bass.ds(head, 1), :, :].squeeze(0), ACOLS)
            load_item(e, n0 + NHEAD, ins["wexp"][0], WCOLS + 2 * HC)
            for tg in range(NTG):
                e.wait_ge(s["wt_ready"], half * NTG + tg + 1)
                e.dma_start(wscr[half, :, group_cols(tg)], m["w8t"][96:96 + NEXP, group_cols(tg)]).then_inc(s["w_out"][tg], 16)
            for tg in range(NTG):
                e.wait_ge(s["w_out"][tg], 16 * (half + 1))

            def weights_back(ex, tg):
                r = (half * TOPK + ex) * NTG + tg
                e.wait_ge(s["hd_ready"], 2 * r + 2)
                e.dma_start(m["wb"][:, tg % 2, :],
                            wscr[half, bass.ds(ex, 1), group_cols(tg)].squeeze(0).partition_broadcast(P))\
                 .then_inc(s["wb_loaded"][tg % 2], 16)

            with e.Fori(0, TOPK - 1) as ex:
                load_item(e, n0 + NHEAD + 1 + ex, ins["wexp"][bass.ds(ex + 1, 1), :, :].squeeze(0), WCOLS + 2 * HC)
                for tg in range(NTG):
                    weights_back(ex, tg)
            load_item(e, n0 + NHEAD + TOPK, ins["wsh"][0], SCOLS + HC)
            for tg in range(NTG):
                weights_back(TOPK - 1, tg)
            load_item(e, n0 + NHEAD + TOPK + 1, ins["wsh"][1], SCOLS + HC)
            load_item(e, n0 + ITEMS, ins["wattn"][0], ACOLS)
            def store_group(tg):
                w = half * (HU + VU) + HU + VU - NTG + tg
                e.wait_ge(s["o_added"], 4 * (w + 1) + 4)
                e.dma_start(tokens(out)[:, half * NT + tg * TPG:half * NT + (tg + 1) * TPG, :],
                            m["acc"][:, tg * TPG:(tg + 1) * TPG, :]).then_inc(s["out_stored"][tg], 16)

            def next_group(tg):
                e.wait_ge(s["out_stored"][tg], 16 * (half + 1))
                if half + 1 < HALVES:
                    load_acc(e, half + 1, tg)

            store_group(0)
            for tg in range(1, NTG):
                next_group(tg - 1)
                store_group(tg)
            next_group(NTG - 1)
        e.wait_ge(s["raw_loaded"], 16 * (HALVES * ITEMS + 1))

    def vector(e):
        with e.Fori(0, HALVES) as hf:
            dve_stats(e, hf, 0, 0)
            dve_norm_alone(e, hf, 0, 0)
            dve_stats(e, hf, 0, 1)
            dve_attention(e, hf)
            dve_norm_alone(e, hf, 1, NTG - 1)
            dve_gate(e, hf, NTG - 1)
            dve_route(e, hf)
            dve_experts(e, hf)

    def scalar(e):
        with e.Fori(0, HALVES) as hf:
            for i in range(TPG):
                act_norm(e, hf, 0, 0, i)
            act_attention(e, hf)
            act_gate(e, hf, NTG - 2)
            for i in range(TPG):
                act_norm(e, hf, 1, NTG - 1, i)
            act_gate(e, hf, NTG - 1)
            act_route(e, hf)
            act_experts(e, hf)

    def tensor(e):
        with e.Fori(0, HALVES) as hf:
            for i in range(TPG):
                pe_norm(e, hf, 0, 0, i)
            pe_attention(e, hf)
            e.wait_ge(s["o_added"], 4 * (hf * (HU + VU) + HU) + 2)
            pe_gate(e, hf, NTG - 2)
            pe_hidden(e, hf * VU, hf * TOPK * NTG, hf * ITEMS + NHEAD, hf, 0, 0, False)
            pe_turn_gate(e, hf, NTG - 2)
            e.wait_ge(s["gate_read"], hf * NTG + NTG - 1)
            for i in range(TPG):
                pe_norm(e, hf, 1, NTG - 1, i)
            pe_gate(e, hf, NTG - 1)
            pe_turn_gate(e, hf, NTG - 1)
            pe_experts(e, hf)

    def gpsimd(e):
        with e.Fori(0, HALVES) as hf:
            n0 = hf * ITEMS
            for tg in range(3):
                pool_norm(e, hf, 0, tg)
            item_lo(e, n0 + 1, 1, ACOLS, 0, between=[lambda: pool_norm(e, hf, 0, 3)])
            item_lo(e, n0 + 2, 0, ACOLS, 0)
            with e.Fori(1, NHEAD // 2 - 1) as pair:
                for k in range(2):
                    item_lo(e, n0 + pair * 2 + k + 1, (k + 1) % 2, ACOLS, 0)
            item_lo(e, n0 + NHEAD - 1, 1, ACOLS, 0)
            item_lo(e, n0 + NHEAD, 0, WCOLS, 2 * HC,
                    between=[lambda tg=tg: pool_norm(e, hf, 1, tg) for tg in range(2)])
            pool_norm(e, hf, 1, 2)
            pool_norm(e, hf, 1, 3)
            with e.Fori(0, 2) as pair:
                for k in range(2):
                    item_lo(e, n0 + NHEAD + pair * 2 + k + 1, (k + 1) % 2, WCOLS, 2 * HC)
            item_lo(e, n0 + NHEAD + TOPK - 1, 1, WCOLS, 2 * HC)
            for k in range(2):
                item_lo(e, n0 + NHEAD + TOPK + k, k, SCOLS, HC)
            item_lo(e, n0 + ITEMS, 0, ACOLS, 0)

    def first_item_hi(e, q):
        e.wait_ge(s["raw_loaded"], 16)
        part = bass.ds(q * (ACOLS // NQ), ACOLS // NQ)
        nc.scalar.activation(m["whi"][:, 0, part], m["raw"][:, part], ACT.Copy).then_inc(s["first_hi"], 1)

    def first_item_lo(e, q):
        part = bass.ds(q * (ACOLS // NQ), ACOLS // NQ)
        e.wait_ge(s["first_hi"], q + 1)
        nc.gpsimd.tensor_tensor(m["wlo"][:, 0, part], m["raw"][:, part], m["whi"][:, 0, part].bitcast(f32),
                                ALU.subtract).then_inc(s["first_lo"], 1)

    return dict(sync=sync, vector=vector, scalar=scalar, tensor=tensor, gpsimd=gpsimd,
                first_item_hi=first_item_hi, first_item_lo=first_item_lo)


def program(nc, ins, out):
    hbuf = nc.dram_tensor("hidden_rows", [CH, HD, SEQ], f32, kind="Internal").ap()
    wscr = nc.dram_tensor("routed_weights", [HALVES, NEXP, TH], f32, kind="Internal").ap()

    buffers, sems = {}, {}
    with ExitStack() as ctx:
        buffers.update({n: ctx.enter_context(nc.sbuf_tensor(n, shape, dt)) for n, shape, dt in (
            ("whi", [P, 2, WCOLS], f32r), ("wlo", [P, 2, WCOLS], f32r), ("raw", [P, WCOLS + 2 * HC], f32),
            ("ebias", [P, 2, 2 * HC], f32), ("xn", [P, 2, D], f32),
            ("ident", [P, P], f32), ("mask", [P, T], f32), ("tri", [P, NEXP, NEXP], f32),
            ("neg_half", [P, TPG], f32), ("sign", [P, 1], f32),
            ("stats", [P, TPG, 6], f32), ("mean_var", [P, TPG, 2], f32), ("var_eps", [P, TPG], f32),
            ("rstd", [P, TPG], f32), ("wg_raw", [P, KC, NEXP], f32), ("wg_hi", [P, KC, NEXP], f32r),
            ("wg_lo", [P, KC, NEXP], f32r), ("bg", [P, NEXP], f32), ("bd3", [P, D], f32r),
            ("gate", [P, NT, NEXP], f32), ("keep", [P, NT, NEXP], f32), ("gmax", [P, NT], f32),
            ("w8", [P, NT, NEXP], f32), ("w8hi", [P, NT, NEXP], f32r),
            ("b_all", [P, HD + P - 1], f32), ("hdt", [P, HD], f32), ("rowsum", [P, QH], f32),
            ("alpha", [P, QH], f32), ("norm", [P, QH], f32))})
        at = nc.sbuf_base
        size = 4 * (3 * NT * D + 10 * 1024)
        ctx.enter_context(nc.sbuf_tensor("arena", [P, size // 4], f32))

        def lay(offset, tensors):
            for n, shape, dt in tensors:
                buffers[n] = nc.alloc_sbuf_tensor_at(n, [P] + shape, dt, offset=at + offset)
                offset += -(-4 * int(np.prod(shape)) // 32) * 32
            assert offset <= size
            return offset

        lay(0, (("a_all", [HD, NS], f32), ("at_all", [HD, NS], f32), ("c_all", [HD, CH], f32),
                ("zmat", [QH, 3 * NS], f32), ("zmat_t", [QH, P], f32), ("xk", [QH, XC], f32),
                ("cy", [QH, P], f32), ("outb", [QH, XC], f32), ("tmp", [QH, NS], f32)))
        work = lay(0, (("acc", [NT, D], f32), ("xhi", [KC, TH], f32r), ("xlo", [KC, TH], f32r)))
        lay(work, [(n, [TG], f32) for n in ("qt", "kt", "vt", "v", "pt", "gate_t")]
            + [("yhi", [TG], f32r), ("ylo", [TG], f32r), ("prob", [TPG, P], f32), ("sm", [TPG, T], f32),
               ("rmax", [TPG], f32), ("rsum", [TPG], f32), ("rinv", [TPG], f32)])
        after_hid = lay(work, (("sg", [HC, TG], f32), ("hhi", [2, HC, TG], f32r), ("hlo", [2, HC, TG], f32r),
                               ("wb", [2, TG], f32)))
        lay(work + 4 * HC * TG, (("before", [NT, NEXP, NEXP], f32), ("ties", [NT, NEXP, NEXP], f32),
                                 ("w8t", [TH], f32)))
        lay(work + 24 * 1024, (("w3t", [TH], f32r), ("ws", [NT, P], f32)))
        lay(work + 38 * 1024, (("bd_tmp", [D], f32r),))
        assert after_hid <= work + 24 * 1024
        buffers["bank"] = [ctx.enter_context(nc.psum_tensor(f"bank{i}", [P, 512], f32)) for i in range(8)]

        sems.update({n: ctx.enter_context(nc.semaphore(n)) for n in (
            "const_v", "link", "link_a", "dt_ready", "dve", "act", "pe", "norm_ready", "outb_free",
            "turn_sp", "turn_pool", "turn_dve", "turn_pe", "zeroed", "ident_ready", "consts_ready", "w8_ones", "bd_loaded", "wg_loaded",
            "bg_loaded", "bd_hi", "router_ready",
            "raw_loaded", "first_hi", "first_lo", "w_hi", "w_ready", "ln_stats", "ln_aggr", "ln_eps", "ln_rstd", "xn_ready", "xn_turned",
            "x_hi", "x_split", "gate_done", "gate_copied", "gate_turned", "gate_exp", "route", "w_turned", "wt_ready", "gate_read",
            "q_done", "k_done", "v_done", "s_done", "y_done", "y_hi",
            "q_ready", "k_ready", "v_ready", "pt_ready", "y_split", "s_read", "row_max", "row_sub", "p_exp",
            "row_sum", "row_inv", "p_ready", "p_turned", "vt_copied", "v_turned", "o_done", "o_added",
            "g_done", "u_done", "g_used", "u_used", "hd_ready", "hid_hi", "hid_split")})
        for n, k in (("small_in", 2), ("ssm_in", 3), ("rows_out", 2), ("acc_loaded", NTG), ("out_stored", NTG),
                     ("w_out", NTG), ("wb_loaded", 2), ("bd_part", 3)):
            sems[n] = [ctx.enter_context(nc.semaphore(f"{n}{i}")) for i in range(k)]

        m, s = buffers, sems
        ssm = ssm_program(nc, ins, hbuf, m, s)
        tok = token_program(nc, ins, hbuf, wscr, out, m, s)
        block = ctx.enter_context(nc.Block())

        @block.sync
        def _(e):
            ssm["sync"](e, lambda: e.dma_start(m["raw"][:, 0:ACOLS], ins["wattn"][0]).then_inc(s["raw_loaded"], 16))
            e.dma_start(m["wg_raw"][:, :, :], ins["wg"]).then_inc(s["wg_loaded"], 16)
            e.dma_start(m["bg"][:, :], ins["bg"].partition_broadcast(P)).then_inc(s["bg_loaded"], 16)
            e.wait_ge(s["zeroed"], 4)
            for k in range(3):
                e.dma_start(m["xn"][32 * k:32 * k + TOPK + 1, 0, :], ins["bdown"]).then_inc(s["bd_part"][k], 16)
            e.sem_inc(s["outb_free"], 1)
            ssm["store"](e)
            tok["sync"](e)

        @block.gpsimd
        def _(e):
            p = nc.gpsimd
            p.memset(m["ident"][:, :], 0.0).then_inc(s["zeroed"], 1)
            p.memset(m["mask"][:, :], 0.0).then_inc(s["zeroed"], 1)
            p.memset(m["tri"][:, :, :], 1.0).then_inc(s["zeroed"], 1)
            p.memset(m["xn"][:, 0, :], 0.0).then_inc(s["zeroed"], 1)
            p.memset(m["w8"][:, :, :], 0.0).then_inc(s["zeroed"], 1)
            e.wait_ge(s["zeroed"], 5)
            p.affine_select(out=m["ident"][:, :], in_=m["ident"][:, :], compare_op=ALU.not_equal, fill=1.0,
                            base=0, pattern=[[-1, P]], channel_multiplier=1).then_inc(s["ident_ready"], 1)
            e.wait_ge(s["ident_ready"], 1)
            for k, r in enumerate((slice(0, T), slice(T, P))):
                p.affine_select(out=m["mask"][r, :], in_=m["mask"][r, :], compare_op=ALU.is_ge, fill=MASKED,
                                base=0, pattern=[[-1, T]], channel_multiplier=1).then_inc(s["zeroed"], 1)
                e.wait_ge(s["zeroed"], 6 + k)
            p.affine_select(out=m["tri"][:, :, :], in_=m["tri"][:, :, :], compare_op=ALU.is_gt, fill=0.0,
                            base=0, pattern=[[1, NEXP], [-1, NEXP]], channel_multiplier=0)
            p.memset(m["neg_half"][:, :], -0.5)
            p.memset(m["w8"][:, :, TOPK:TOPK + 1], 1.0).then_inc(s["consts_ready"], 1)
            e.wait_ge(s["consts_ready"], 1)
            ssm["gpsimd"](e, lambda q: tok["first_item_lo"](e, q))
            e.wait_ge(s["first_lo"], NQ)
            e.sem_inc(s["w_ready"], 1)
            tok["gpsimd"](e)

        @block.vector
        def _(e):
            for sem, credit in ((s["k_ready"], 1), (s["v_ready"], 1),
                                (s["s_read"], 1), (s["x_split"], 2), (s["o_added"], 4), (s["u_used"], 2), (s["hid_split"], 2),
                                (s["hd_ready"], 4)):
                e.sem_inc(sem, credit)
            e.wait_ge(s["consts_ready"], 1)
            ssm["vector"](e)
            e.wait_ge(s["bd_hi"], 2)
            nc.vector.tensor_tensor(m["wg_lo"][:, :, :], m["wg_raw"][:, :, :], m["wg_hi"][:, :, :].bitcast(f32), ALU.subtract)
            nc.vector.tensor_tensor(m["bd3"][64:128, :], m["xn"][64:128, 0, :], m["bd_tmp"][64:128, :].bitcast(f32),
                                    ALU.subtract).then_inc(s["router_ready"], 1)
            e.wait_ge(s["router_ready"], 1)
            nc.vector.memset(m["ws"][:, :, :], 0.0)
            e.wait_ge(s["bg_loaded"], 16)
            tok["vector"](e)

        @block.scalar
        def _(e):
            e.sem_inc(s["g_used"], 2)
            e.sem_inc(s["q_ready"], 1)
            e.sem_inc(s["w_hi"], 3)
            ssm["scalar"](e, lambda q: tok["first_item_hi"](e, q))
            e.wait_ge(s["wg_loaded"], 16)
            nc.scalar.activation(m["wg_hi"][:, :, :], m["wg_raw"][:, :, :], ACT.Copy).then_inc(s["bd_hi"], 1)
            for k in range(3):
                e.wait_ge(s["bd_part"][k], 16)
            nc.scalar.activation(m["bd3"][0:64, :], m["xn"][0:64, 0, :], ACT.Copy)
            nc.scalar.activation(m["bd_tmp"][64:128, :], m["xn"][64:128, 0, :], ACT.Copy).then_inc(s["bd_hi"], 1)
            tok["scalar"](e)

        @block.tensor
        def _(e):
            e.sem_inc(s["o_done"], 1)
            e.sem_inc(s["xn_turned"], 2)
            e.wait_ge(s["ident_ready"], 1)
            ssm["tensor"](e)
            e.wait_ge(s["router_ready"], 1)
            tok["tensor"](e)
    return nc


def kernel(x, L0_tok_A, L0_tok_B, L0_tok_log_dt, L0_attn_Wq, L0_attn_Wk, L0_attn_Wv, L0_attn_Wo, L0_ffn_Wg,
           L0_ffn_bg, L0_ffn_Wgate, L0_ffn_bgate, L0_ffn_Wup, L0_ffn_bup, L0_ffn_Wdown, L0_ffn_bdown,
           L0_ffn_Ws_up, L0_ffn_bs_up, L0_ffn_Ws_down, L0_ffn_bs_down):
    import concourse.bacc as bacc
    from concourse.bass_utils import run_bass_kernel_spmd

    def proj(w):
        return np.asarray(w).reshape(NHEAD, DH, KC, P).transpose(0, 3, 2, 1).reshape(NHEAD, P, KC * DH)

    def up(w):
        return np.asarray(w).reshape(-1, KC, P, HID).transpose(0, 2, 1, 3).reshape(-1, P, KC * HID)

    def down(w):
        return np.asarray(w).reshape(-1, HC, P, D).transpose(0, 2, 1, 3).reshape(-1, P, HC * D)

    def bias(b):
        return np.asarray(b).reshape(-1, HC, P).transpose(0, 2, 1)

    a, b = np.asarray(L0_tok_A), np.asarray(L0_tok_B)
    wo = np.asarray(L0_attn_Wo).reshape(D, NHEAD, DH).transpose(1, 2, 0)
    ws_up = np.asarray(L0_ffn_Ws_up).reshape(D, NSH, HID).transpose(1, 0, 2)
    arrays = {
        "a": a.transpose(3, 1, 0, 2).reshape(P, HD, NS),
        "at": a.transpose(3, 2, 0, 1).reshape(P, HD, NS),
        "b": b.transpose(2, 1, 0).reshape(P, HD),
        "c": np.asarray(x).transpose(3, 2, 1, 0).reshape(P, HD, CH),
        "log_dt": np.asarray(L0_tok_log_dt).reshape(HD),
        "wattn": np.concatenate([proj(L0_attn_Wq), proj(L0_attn_Wk), proj(L0_attn_Wv), wo], axis=2),
        "wexp": np.concatenate([up(L0_ffn_Wgate), up(L0_ffn_Wup), down(L0_ffn_Wdown), bias(L0_ffn_bgate),
                                bias(L0_ffn_bup)], axis=2),
        "wsh": np.concatenate([up(ws_up), down(L0_ffn_Ws_down), bias(L0_ffn_bs_up)], axis=2),
        "wg": np.asarray(L0_ffn_Wg).reshape(KC, P, NEXP).transpose(1, 0, 2),
        "bg": np.asarray(L0_ffn_bg),
        "bdown": np.concatenate([np.asarray(L0_ffn_bdown), np.asarray(L0_ffn_bs_down)[None]], axis=0),
    }
    arrays = {n: np.ascontiguousarray(v) for n, v in arrays.items()}
    nc = bacc.Bacc("TRN2", target_bir_lowering=False, num_devices=1)
    ins = {n: nc.dram_tensor(f"in_{n}", v.shape, mybir.dt.from_np(v.dtype), kind="ExternalInput").ap()
           for n, v in arrays.items()}
    out = nc.dram_tensor("out", [CH, HD, D], f32, kind="ExternalOutput").ap()
    program(nc, ins, out)
    result = run_bass_kernel_spmd(nc, [{f"in_{n}": v for n, v in arrays.items()}], core_ids=[0])
    return result.results[0]["out"]
```

```python
from contextlib import ExitStack

import numpy as np

import concourse.bass as bass
from concourse import mybir

f32 = mybir.dt.float32
f32r = mybir.dt.float32r
ALU = mybir.AluOpType
ACT = mybir.ActivationFunctionType
AX = mybir.AxisListType.X

P = 128
HD, NS, SEQ, CH = 64, 64, 512, 64
QH, GH = 16, 4
NQ, NG = HD // QH, QH // GH
INV = 10
DBL = 8
XC = 2 ** DBL
D, NHEAD, DH = 512, 16, 128
KC = D // P
TOK = CH * HD
HALVES = 2
TH = TOK // HALVES
TG = 512
NTG, TPG = TH // TG, TG // P
NT = TH // P
T = HD
NEXP, TOPK, HID = 8, 6, 256
NSH = 2
HC = HID // P
ITEMS = NHEAD + TOPK + NSH
SCALE = float(DH) ** -0.5
MASKED = -1e30
EPS = 1e-5
WCOLS = 2 * KC * HID + HC * D
ACOLS = 3 * KC * DH + D
SCOLS = KC * HID + HC * D


class Steps:

    def __init__(self, names):
        self.at = {n: i + 1 for i, n in enumerate(names)}
        self.n = len(names)

    def after(self, q, *name):
        return q * self.n + self.at[name]


def ssm_steps():
    G = range(NG)
    pe = [("G", g) for g in G]
    dve = [("G", g) for g in G] + [("rowsum", g) for g in G]
    dve += [(x, g) for g in G for x in ("M", "Q")]
    act = [("G", g) for g in G]
    for k in range(INV):
        pe += [("N", k, g) for g in G]
        dve += [(x, k, g) for g in G for x in ("S", "N") if x == "N" or k < INV - 1]
        if k < INV - 1:
            act += [("N", k, g) for g in G]
    dve += [("P", g) for g in G]
    act += [("P", g) for g in G]
    pe += [("T", 0, g) for g in G] + [("b", g) for g in G]
    dve += [("T", 0, g) for g in G]
    dve += [(x, g) for g in G for x in ("b+", "b")]
    for j in range(DBL):
        pe += [("K", j, g) for g in G]
        dve += [("K", j, g) for g in G]
        act += [(x, j, g) for g in G for x in ("K", "X")]
        if j < DBL - 1:
            pe += [("T", j + 1, g) for g in G]
            dve += [("T", j + 1, g) for g in G]
    pe += [("Y", g) for g in G] + [("F", g) for g in G]
    dve += [("C",)]
    act += [("Y", g) for g in G] + [("F", g) for g in G]
    return Steps(pe), Steps(dve), Steps(act)


def ssm_program(nc, ins, hbuf, m, s):
    PE, DV, AC = ssm_steps()
    SR = m["zmat"]
    ET = m["zmat_t"]
    lo, hi = slice(0, 64), slice(64, 128)
    AT = HD

    def grp(g):
        return slice(g * GH, (g + 1) * GH)

    def bank_a(g):
        return m["bank"][g][:, :]

    def bank_b(g):
        return m["bank"][NG + g][:, :]

    def a4(g, cols):
        return bank_a(g)[:, 0:GH * cols].rearrange("p (h c) -> p h c", h=GH)

    def b4(g, cols):
        return bank_b(g)[:, 0:GH * cols].rearrange("p (h c) -> p h c", h=GH)

    def heads(q):
        return bass.ds(q * QH, QH)

    def half_dt(q, cols, count=QH, at=0):
        return m["hdt"][:, bass.ds(q * QH + at, count)].unsqueeze(2).to_broadcast([P, count, cols])

    def sync(e, after_first):
        e.dma_start(m["hdt"][:, 0:HD], ins["log_dt"].partition_broadcast(P)).then_inc(s["small_in"][0], 16)
        e.dma_start(m["b_all"][:, 0:HD], ins["b"]).then_inc(s["small_in"][1], 16)
        def load(q):
            for k, (dst, src) in enumerate(((m["aat"][:, 0:AT, :], "a"), (m["aat"][:, AT:, :], "at"),
                                            (m["c_all"][:, :, :], "c"))):
                e.dma_start(dst[:, heads(q), :], ins[src][:, heads(q), :]).then_inc(s["ssm_in"][k], 16)

        load(0)
        after_first()
        with e.Fori(1, NQ) as q:
            for k in range(3):
                e.wait_ge(s["ssm_in"][k], 16 * q)
            e.sem_inc(s["turn_sp"], 1)
            load(q)
        e.wait_ge(s["ssm_in"][0], 16 * NQ)
        e.sem_inc(s["ssm_in"][0], 16)

    def store(e):
        with e.Fori(0, NQ) as q:
            for g in range(NG):
                e.wait_ge(s["out_copied"], NG * (q + 1) + g + 1)
                e.sem_inc(s["turn_sp"], 1)
                e.wait_ge(s["act"], AC.after(q, "F", g))
                e.sem_inc(s["turn_sp"], 1)
                for blk in range(2):
                    e.dma_start(hbuf[:, bass.ds(q * QH + g * GH, GH), blk * XC:(blk + 1) * XC],
                                m["outb"][64 * blk:64 * blk + 64, grp(g), :]).then_inc(s["rows_out"][2 * g + blk], 16)
            for k in range(2 * NG):
                e.wait_ge(s["rows_out"][k], 16 * (q + 1))
                e.sem_inc(s["turn_sp"], 1)
            e.sem_inc(s["outb_free"], 1)

    def vector(e):
        v = nc.vector
        v.memset(m["sign"][0:64, :], 1.0).then_inc(s["const_v"], 1)
        v.memset(m["sign"][64:128, :], -1.0).then_inc(s["const_v"], 1)
        v.memset(m["b_all"][:, HD:], 0.0)
        v.memset(m["hdt"][:, HD:], 0.0)
        v.memset(m["cy"][:, :, 64:128], 0.0)
        e.wait_ge(s["const_v"], 2)
        e.wait_ge(s["ident_ready"], 1)
        eye = m["ident"][:, 0:64].unsqueeze(1)
        links = 4 + NG

        def form_b(q, freed):
            e.wait_ge(s["ssm_in"][0], 16 * (q + 1))
            e.wait_ge(s["dt_ready"], 1)
            v.tensor_tensor(m["tmp"][:, :, :], m["aat"][:, heads(q), :], half_dt(q, 64), ALU.mult).then_inc(s["link"], 1)
            e.wait_ge(s["link"], links * q + 1)
            for g in range(NG):
                freed(g)
                v.tensor_tensor(SR[:, grp(g), 0:64], eye.to_broadcast([P, GH, 64]), m["tmp"][:, grp(g), :],
                                ALU.subtract).then_inc(s["b_formed"], 1)

        form_b(0, lambda g: None)
        with e.Fori(0, NQ) as q:
            e.wait_ge(s["ssm_in"][1], 16 * (q + 1))
            e.wait_ge(s["b_formed"], NG * (q + 1))
            v.scalar_tensor_tensor(m["tmp"][:, :, :], m["aat"][:, bass.ds(q * QH + AT, QH), :], m["sign"][:, 0:1],
                                   half_dt(q, 64), ALU.mult, ALU.mult).then_inc(s["link"], 1)
            e.wait_ge(s["link"], links * q + 2)
            v.tensor_tensor(m["tmp"][:, :, :], eye.to_broadcast([P, QH, 64]), m["tmp"][:, :, :],
                            ALU.subtract).then_inc(s["link"], 1)
            for g in range(NG):
                e.wait_ge(s["pe"], PE.after(q, "G", g))
                v.tensor_copy(SR[:, grp(g), 0:64], a4(g, 128)[:, :, 0:64]).then_inc(s["dve"], 1)
            for g in range(NG):
                e.wait_ge(s["act"], AC.after(q, "G", g))
                v.tensor_reduce(m["rowsum"][:, grp(g)], SR[:, grp(g), 0:128], axis=AX, op=ALU.add,
                                apply_absolute_value=True).then_inc(s["dve"], 1)
            e.wait_ge(s["norm_ready"], q + 1)
            v.reciprocal(m["alpha"][:, :], m["norm"][:, :]).then_inc(s["link"], 1)
            e.wait_ge(s["link"], links * q + 4)
            for g in range(NG):
                by_alpha = m["alpha"][:, grp(g)].unsqueeze(2)
                v.tensor_tensor(SR[:, grp(g), 0:128], SR[:, grp(g), 0:128], by_alpha.to_broadcast([P, GH, 128]),
                                ALU.mult).then_inc(s["link"], 1)
                e.wait_ge(s["link"], links * q + 5 + g)
                v.tensor_tensor(SR[:, grp(g), 0:128], m["ident"][:, :].unsqueeze(1).to_broadcast([P, GH, 128]),
                                SR[:, grp(g), 0:128], ALU.subtract).then_inc(s["dve"], 1)
                v.tensor_tensor(SR[:, grp(g), 128:192], m["tmp"][:, grp(g), :], by_alpha.to_broadcast([P, GH, 64]),
                                ALU.mult).then_inc(s["dve"], 1)
            for k in range(INV):
                for g in range(NG):
                    e.wait_ge(s["pe"], PE.after(q, "N", k, g))
                    if k == INV - 1:
                        v.tensor_tensor(SR[:, grp(g), 128:192], SR[:, grp(g), 128:192],
                                        a4(g, 128)[:, :, 64:128], ALU.add).then_inc(s["dve"], 1)
                    else:
                        v.tensor_copy(SR[:, grp(g), 0:64], a4(g, 128)[:, :, 0:64]).then_inc(s["dve"], 1)
                        v.tensor_tensor(SR[:, grp(g), 128:192], SR[:, grp(g), 128:192],
                                        a4(g, 128)[:, :, 64:128], ALU.add).then_inc(s["dve"], 1)
            for g in range(NG):
                e.wait_ge(s["dve"], DV.after(q, "N", INV - 1, g))
                v.scalar_tensor_tensor(SR[:, grp(g), 0:64], SR[:, grp(g), 128:192], 2.0,
                                       eye.to_broadcast([P, GH, 64]), ALU.mult, ALU.subtract).then_inc(s["dve"], 1)

            def transposed(j, g):
                e.wait_ge(s["pe"], PE.after(q, "T", j, g))
                v.tensor_copy(ET[:, grp(g), :], b4(g, 128)).then_inc(s["dve"], 1)

            for g in range(NG):
                transposed(0, g)
            for g in range(NG):
                e.wait_ge(s["pe"], PE.after(q, "b", g))
                v.tensor_tensor(SR[:, grp(g), 128:129], m["b_all"][:, bass.ds(q * QH + g * GH, GH)].unsqueeze(2),
                                a4(g, 128)[:, :, 0:1], ALU.add).then_inc(s["dve"], 1)
                e.wait_ge(s["dve"], DV.after(q, "b+", g))
                v.tensor_tensor(SR[:, grp(g), 128:129], SR[:, grp(g), 128:129], half_dt(q, 1, GH, g * GH),
                                ALU.mult).then_inc(s["dve"], 1)
            for j in range(DBL):
                for g in range(NG):
                    e.wait_ge(s["pe"], PE.after(q, "K", j, g))
                    v.tensor_copy(SR[:, grp(g), 0:64], a4(g, 128)[:, :, 0:64]).then_inc(s["dve"], 1)
                if j < DBL - 1:
                    for g in range(NG):
                        transposed(j + 1, g)
            e.wait_ge(s["ssm_in"][2], 16 * (q + 1))
            v.tensor_scalar(m["cy"][:, :, 0:64], m["c_all"][:, heads(q), :], m["sign"][:, 0:1], None,
                            ALU.mult).then_inc(s["dve"], 1)
            form_b(q + 1, lambda g: e.wait_ge(s["pe"], PE.after(q, "Y", g)))
            e.wait_ge(s["outb_free"], q + 1)
            for g in range(NG):
                e.wait_ge(s["pe"], PE.after(q, "F", g))
                v.tensor_copy(m["outb"][:, g * GH:g * GH + 2, :],
                              bank_a(g).rearrange("p (h c) -> p h c", h=2)).then_inc(s["out_copied"], 1)

    def scalar(e, beside_inverse):
        c = nc.scalar
        e.wait_ge(s["small_in"][0], 16)
        c.activation(m["hdt"][:, 0:HD], m["hdt"][:, 0:HD], ACT.Exp).then_inc(s["link_a"], 1)
        e.wait_ge(s["link_a"], 1)
        c.activation(m["hdt"][:, 0:HD], m["hdt"][:, 0:HD], ACT.Copy, scale=0.5).then_inc(s["dt_ready"], 1)

        def rotate(z):
            c.activation(z[lo, :, 64:128], z[hi, :, 0:64], ACT.Copy, scale=-1.0)
            return c.activation(z[hi, :, 64:128], z[lo, :, 0:64], ACT.Copy)

        def turn_b(q):
            for g in range(NG):
                e.wait_ge(s["b_formed"], NG * q + g + 1)
                rotate(SR[:, grp(g), :]).then_inc(s["b_turned"], 1)

        turn_b(0)
        with e.Fori(0, NQ) as q:
            for g in range(NG):
                e.wait_ge(s["dve"], DV.after(q, "G", g))
                rotate(SR[:, grp(g), :]).then_inc(s["act"], 1)
            beside_inverse(q)
            for k in range(INV - 1):
                for g in range(NG):
                    e.wait_ge(s["dve"], DV.after(q, "S", k, g))
                    rotate(SR[:, grp(g), :]).then_inc(s["act"], 1)
            for g in range(NG):
                e.wait_ge(s["dve"], DV.after(q, "P", g))
                rotate(SR[:, grp(g), :]).then_inc(s["act"], 1)
            for j in range(DBL):
                n = 2 ** j
                for g in range(NG):
                    e.wait_ge(s["dve"], DV.after(q, "K", j, g))
                    rotate(SR[:, grp(g), :]).then_inc(s["act"], 1)
                    if n < 64:
                        c.activation(SR[:, grp(g), 128 + n:128 + 2 * n], a4(g, 128)[:, :, 64:64 + n],
                                     ACT.Copy).then_inc(s["act"], 1)
                    elif n == 64:
                        c.activation(m["xk"][:, grp(g), 0:n], SR[:, grp(g), 128:192], ACT.Copy)
                        c.activation(m["xk"][:, grp(g), n:2 * n], a4(g, 128)[:, :, 64:128], ACT.Copy).then_inc(s["act"], 1)
                    else:
                        c.activation(m["xk"][:, grp(g), n:2 * n], b4(g, n), ACT.Copy).then_inc(s["act"], 1)
            for g in range(NG):
                e.wait_ge(s["pe"], PE.after(q, "Y", g))
                c.activation(m["cy"][:, grp(g), 64:128], a4(g, 128)[:, :, 0:64], ACT.Copy).then_inc(s["act"], 1)
            turn_b(q + 1)
            e.wait_ge(s["outb_free"], q + 1)
            for g in range(NG):
                e.wait_ge(s["pe"], PE.after(q, "F", g))
                c.activation(m["outb"][:, g * GH + 2:g * GH + 4, :],
                             bank_b(g).rearrange("p (h c) -> p h c", h=2), ACT.Copy).then_inc(s["act"], 1)

    def gpsimd(e, beside_inverse):
        with e.Fori(0, NQ) as q:
            e.wait_ge(s["dve"], DV.after(q, "rowsum", NG - 1))
            e.sem_inc(s["turn_pool"], 1)
            nc.gpsimd.partition_all_reduce(m["norm"][:, :], m["rowsum"][:, :], P,
                                           bass.bass_isa.ReduceOp.max).then_inc(s["norm_ready"], 1)
            beside_inverse(q)

    def tensor(e):
        mm = nc.tensor.matmul

        def s_and_third(h):
            return SR[:, h, :].rearrange("p (b c) -> p b c", b=3)[:, 0:3:2, :]

        with e.Fori(0, NQ) as q:
            for g in range(NG):
                e.wait_ge(s["b_turned"], NG * q + g + 1)
                e.wait_ge(s["out_copied"], NG * q + g + 1)
                for i in range(GH):
                    h = g * GH + i
                    last = mm(a4(g, 128)[:, i, :], SR[:, h, 0:128], SR[:, h, 0:128], start=True, stop=True)
                last.then_inc(s["pe"], 1)
            for k in range(INV):
                for g in range(NG):
                    if k == 0:
                        e.wait_ge(s["dve"], DV.after(q, "Q", g))
                    else:
                        e.wait_ge(s["dve"], DV.after(q, "N", k - 1, g))
                        e.wait_ge(s["act"], AC.after(q, "N", k - 1, g))
                    for i in range(GH):
                        h = g * GH + i
                        last = mm(a4(g, 128)[:, i, :], SR[:, h, 0:128], s_and_third(h), start=True, stop=True)
                    last.then_inc(s["pe"], 1)

            def transpose(j, g):
                if j == 0:
                    e.wait_ge(s["act"], AC.after(q, "P", g))
                else:
                    e.wait_ge(s["dve"], DV.after(q, "K", j - 1, g))
                    e.wait_ge(s["act"], AC.after(q, "X", j - 1, g))
                for i in range(GH):
                    last = nc.tensor.transpose(b4(g, 128)[:, i, :], SR[:, g * GH + i, 0:128], m["ident"][:, :])
                last.then_inc(s["pe"], 1)

            for g in range(NG):
                transpose(0, g)
            e.wait_ge(s["small_in"][1], 16)
            for g in range(NG):
                e.wait_ge(s["dve"], DV.after(q, "T", 0, g))
                for i in range(GH):
                    h = g * GH + i
                    last = mm(a4(g, 128)[:, i, :], ET[:, h, :], m["b_all"][:, bass.ds(q * QH + h, P)],
                              start=True, stop=True)
                last.then_inc(s["pe"], 1)
            for j in range(DBL):
                n = 2 ** j
                for g in range(NG):
                    e.wait_ge(s["dve"], DV.after(q, "b", g) if j == 0 else DV.after(q, "T", j, g))
                    for i in range(GH):
                        h = g * GH + i
                        if n <= 64:
                            last = mm(a4(g, 128)[:, i, :], ET[:, h, :], s_and_third(h), start=True, stop=True)
                        else:
                            mm(a4(g, 128)[:, i, :], ET[:, h, :], SR[:, h, 0:128], start=True, stop=True)
                            last = mm(b4(g, n)[:, i, :], ET[:, h, :], m["xk"][:, h, 0:n], start=True, stop=True)
                    last.then_inc(s["pe"], 1)
                if j < DBL - 1:
                    for g in range(NG):
                        transpose(j + 1, g)
            e.wait_ge(s["dve"], DV.after(q, "C"))
            for g in range(NG):
                e.wait_ge(s["act"], AC.after(q, "X", DBL - 1, g))
                for i in range(GH):
                    h = g * GH + i
                    last = mm(a4(g, 128)[:, i, :], SR[:, h, 0:128], m["cy"][:, h, :], start=True, stop=True)
                last.then_inc(s["pe"], 1)
            for g in range(NG):
                e.wait_ge(s["act"], AC.after(q, "Y", g))
                for i in range(GH):
                    h = g * GH + i
                    bank = bank_a(g) if i < 2 else bank_b(g)
                    last = mm(bank[:, (i % 2) * XC:(i % 2 + 1) * XC], m["cy"][:, h, :], m["xk"][:, h, :],
                              start=True, stop=True)
                last.then_inc(s["pe"], 1)

    return dict(sync=sync, store=store, vector=vector, scalar=scalar, gpsimd=gpsimd, tensor=tensor)


def token_program(nc, ins, hbuf, wscr, out, m, s):
    HU, VU = NHEAD * NTG, (TOPK + NSH) * NTG
    BQ, BK, BV, BS, BT, BY, BO0, BO1 = (m["bank"][i][:, :] for i in range(8))
    BO = [BO0, BO1, BT, BY]
    BR = [BT, BY]
    BG, BU = [BQ, BV], [BK, BS]

    def tile_cols(t):
        return slice(t * P, (t + 1) * P)

    def group_cols(tg):
        return slice(tg * TG, (tg + 1) * TG)

    def pairs(bank):
        return bank.rearrange("p (i c) -> p i c", i=TPG)

    def w_proj(k, which):
        return slice((which * KC + k) * DH, (which * KC + k + 1) * DH)

    W_OUT = slice(3 * KC * DH, ACOLS)

    def w_hid(k, which, j):
        at = (which * KC + k) * HID + j * P
        return slice(at, at + P)

    def w_down(j, shared):
        at = (1 if shared else 2) * KC * HID + j * D
        return slice(at, at + D)

    def three(out_ap, hi, lo, rhi, rlo, start, stop):
        nc.tensor.matmul(out_ap, hi, rhi, start=start, stop=False)
        nc.tensor.matmul(out_ap, hi, rlo, start=False, stop=False)
        return nc.tensor.matmul(out_ap, lo, rhi, start=False, stop=stop)

    def split_hi(dst, src):
        return nc.scalar.activation(dst, src, ACT.Copy)

    def split_lo(dst, src, hi):
        return nc.vector.tensor_tensor(dst, src, hi.bitcast(f32), ALU.subtract)

    def pieces(cols):
        step = -(-cols // 3 // P) * P
        return [(a, min(a + step, cols)) for a in range(0, cols, step)]

    def item_hi(e, n, par, cols, k):
        a, b = pieces(cols)[k]
        e.wait_ge(s["raw_loaded"], 16 * (n + 1))
        e.wait_ge(s["o_done"], 16 * (n - 1) + 1)
        nc.scalar.activation(m["whi"][:, par, a:b], m["raw"][:, a:b], ACT.Copy).then_inc(s["w_hi"], 1)

    def item_lo(e, n, par, cols, bias, between=()):
        for k, (a, b) in enumerate(pieces(cols)):
            e.wait_ge(s["w_hi"], 3 * n + k + 1)
            last = nc.gpsimd.tensor_tensor(m["wlo"][:, par, a:b], m["raw"][:, a:b],
                                           m["whi"][:, par, a:b].bitcast(f32), ALU.subtract)
            if bias and k == 2:
                last = nc.gpsimd.tensor_copy(m["ebias"][:, par, 0:bias], m["raw"][:, cols:cols + bias])
            if k < len(between):
                between[k]()
        last.then_inc(s["w_ready"], 1)

    def norm_group(hf, phase, tg):
        return (hf * 2 + phase) * NTG + tg

    def norm_bank(phase, tg, i):
        if (phase, tg) == (0, 0):
            return BU[i % 2]
        return ([BO0, BO1, BO0, BO1] if (phase, tg) == (1, NTG - 1) else [BO0, BO1, BQ, BS])[i]

    def dve_stats(e, hf, phase, tg):
        v, g = nc.vector, norm_group(hf, phase, tg)
        if phase == 0:
            e.wait_ge(s["acc_loaded"][tg], 16 * (hf + 1))
        else:
            e.wait_ge(s["o_added"], 4 * (hf * (HU + VU) + HU - NTG + tg + 1) + 4)
        for i in range(TPG):
            last = v.bn_stats(m["stats"][:, i, :], m["acc"][:, tg * TPG + i, :])
        last.then_inc(s["ln_stats"], 1)
        e.wait_ge(s["ln_stats"], g + 1)
        e.sem_inc(s["turn_dve"], 1)
        for i in range(TPG):
            last = v.bn_aggr(m["mean_var"][:, i, :], m["stats"][:, i, :])
        last.then_inc(s["ln_aggr"], 1)

    def dve_normalise(e, hf, phase, tg, i):
        g = norm_group(hf, phase, tg)
        if i == 0:
            e.wait_ge(s["ln_rstd"], g + 1)
            e.sem_inc(s["turn_dve"], 1)
        e.wait_ge(s["xn_turned"], g * TPG + i + 1)
        e.sem_inc(s["turn_dve"], 1)
        nc.vector.tensor_scalar(m["xn"][:, i % 2, :], m["acc"][:, tg * TPG + i, :], m["mean_var"][:, i, 0:1],
                                m["rstd"][:, i:i + 1], ALU.subtract, ALU.mult).then_inc(s["xn_ready"], 1)

    def dve_norm(e, hf, phase, tg, i):
        tile = norm_group(hf, phase, tg) * TPG + i
        e.wait_ge(s["x_hi"], tile + 1)
        cols = tile_cols(tg * TPG + i)
        split_lo(m["xlo"][:, :, cols], pairs(norm_bank(phase, tg, i)), m["xhi"][:, :, cols]).then_inc(s["x_split"], 1)

    def dve_norm_alone(e, hf, phase, tg):
        dve_normalise(e, hf, phase, tg, 0)
        if phase == 1:
            dve_gate(e, hf, tg - 1)
        for i in range(TPG):
            if i + 1 < TPG:
                dve_normalise(e, hf, phase, tg, i + 1)
            dve_norm(e, hf, phase, tg, i)

    def dve_gate(e, hf, tg):
        e.wait_ge(s["gate_turned"], hf * NTG + tg + 1)
        nc.vector.tensor_tensor(m["gate"][:, tg * TPG:(tg + 1) * TPG, :],
                                BO1[:, 0:TPG * NEXP].rearrange("p (t x) -> p t x", t=TPG),
                                m["bg"][:, :].unsqueeze(1).to_broadcast([P, TPG, NEXP]), ALU.add).then_inc(s["gate_read"], 1)

    def pool_norm(e, hf, phase, tg):
        p, g = nc.gpsimd, norm_group(hf, phase, tg)
        e.wait_ge(s["ln_aggr"], g + 1)
        e.sem_inc(s["turn_pool"], 1)
        p.tensor_scalar(m["var_eps"][:, :], m["mean_var"][:, :, 1], EPS, None, ALU.add).then_inc(s["ln_eps"], 1)
        e.wait_ge(s["ln_eps"], g + 1)
        p.tensor_tensor(m["rstd"][:, :], m["var_eps"][:, :], m["neg_half"][:, :], ALU.pow).then_inc(s["ln_rstd"], 1)

    def act_norm(e, hf, phase, tg, i):
        e.wait_ge(s["xn_turned"], norm_group(hf, phase, tg) * TPG + i + 3)
        split_hi(m["xhi"][:, :, tile_cols(tg * TPG + i)], pairs(norm_bank(phase, tg, i))).then_inc(s["x_hi"], 1)

    def pe_norm(e, hf, phase, tg, i):
        tile = norm_group(hf, phase, tg) * TPG + i
        e.wait_ge(s["xn_ready"], tile + 1)
        e.wait_ge(s["x_split"], tile + 1)
        for k in range(KC):
            last = nc.tensor.transpose(pairs(norm_bank(phase, tg, i))[:, k, :], m["xn"][:, i % 2, tile_cols(k)], m["ident"][:, :])
        last.then_inc(s["xn_turned"], 1)

    def pe_gate(e, hf, tg):
        e.wait_ge(s["x_split"], (norm_group(hf, 1, tg) + 1) * TPG + 2)
        for k in range(KC):
            last = three(BO0[0:NEXP, :], m["wg_hi"][:, k, :], m["wg_lo"][:, k, :], m["xhi"][:, k, group_cols(tg)],
                         m["xlo"][:, k, group_cols(tg)], k == 0, k == KC - 1)
        last.then_inc(s["gate_done"], 1)

    def act_gate(e, hf, tg):
        e.wait_ge(s["gate_done"], hf * NTG + tg + 1)
        nc.scalar.activation(m["gate_t"][0:NEXP, :], BO0[0:NEXP, :], ACT.Copy).then_inc(s["gate_copied"], 1)

    def pe_turn_gate(e, hf, tg):
        e.wait_ge(s["gate_copied"], hf * NTG + tg + 1)
        e.sem_inc(s["turn_pe"], 1)
        for i in range(TPG):
            last = nc.tensor.transpose(BO1[:, i * NEXP:(i + 1) * NEXP], m["gate_t"][0:NEXP, tile_cols(i)],
                                       m["ident"][0:NEXP, 0:NEXP])
        last.then_inc(s["gate_turned"], 1)

    def norms_beside(step):
        inside = {("start", 0): (0, 1), ("first", 0): (0, 2), ("first", 1): (0, 3)}
        inside.update({("last", 5 + tg): (1, tg) for tg in range(3)})
        after = {("start", 0): (0, 2), ("first", 0): (0, 3)}
        after.update({("last", 4 + tg): (1, tg) for tg in range(NTG)})
        return inside.get(step), after.get(step)

    def pe_project(e, which, bank, free, done, u, n, hf, tg, par):
        if which == 1:
            e.wait_ge(s["w_ready"], n + 1)
            e.wait_ge(s["x_split"], hf * 2 * NT + (tg + 1) * TPG + 2)
        e.wait_ge(free, u + 1)
        for k in range(KC):
            w = w_proj(k, which)
            last = three(bank, m["whi"][:, par, w], m["wlo"][:, par, w], m["xhi"][:, k, group_cols(tg)],
                         m["xlo"][:, k, group_cols(tg)], k == 0, k == KC - 1)
        last.then_inc(done, 1)

    def pe_scores(e, u):
        e.wait_ge(s["q_ready"], u + 2)
        e.wait_ge(s["k_ready"], u + 2)
        e.wait_ge(s["s_read"], u + 1)
        for i in range(TPG):
            c = tile_cols(i)
            last = nc.tensor.matmul(BS[:, c], m["qt"][:, c], m["kt"][:, c], start=True, stop=True)
        last.then_inc(s["s_done"], 1)

    def pe_turn_v(e, u):
        e.wait_ge(s["vt_copied"], u + 1)
        for i in range(TPG):
            last = nc.tensor.transpose(BV[:, tile_cols(i)], m["vt"][:, tile_cols(i)], m["ident"][:, :])
        last.then_inc(s["v_turned"], 1)

    def pe_turn_p(e, u, w):
        e.wait_ge(s["p_ready"], u + 1)
        e.wait_ge(s["o_added"], 4 * w + 3)
        for i in range(TPG):
            last = nc.tensor.transpose(BT[:, tile_cols(i)], m["prob"][:, i, :], m["ident"][:, :])
        last.then_inc(s["p_turned"], 1)

    def pe_mix(e, u, w):
        e.wait_ge(s["pt_ready"], u + 1)
        e.wait_ge(s["v_ready"], u + 2)
        e.wait_ge(s["o_added"], 4 * w + 4)
        for i in range(TPG):
            c = tile_cols(i)
            last = nc.tensor.matmul(BY[:, c], m["v"][:, c], m["pt"][:, c], start=True, stop=True)
        last.then_inc(s["y_done"], 1)

    def pe_out(e, u, w, par):
        e.wait_ge(s["y_split"], u + 1)
        for i in range(TPG):
            e.wait_ge(s["o_added"], 4 * w + i + 1)
            c = tile_cols(i)
            three(BO[i], m["yhi"][:, c], m["ylo"][:, c], m["whi"][:, par, W_OUT], m["wlo"][:, par, W_OUT],
                  True, True).then_inc(s["o_done"], 1)

    def over_heads(hf, step):
        step("start", 0, 0)
        for k in range(2 * NTG):
            step("first", 0, k)
        yield
        for k in range(2 * NTG):
            step("last", NHEAD // 2 - 1, k)

    def pe_attention(e, hf):
        def step(where, pair, k):
            first, last = where == "start", where == "last" and k == 2 * NTG - 1
            beside, _ = norms_beside((where, k))
            at = pair * 2 * NTG + k
            u, w = hf * HU + at, hf * (HU + VU) + at
            par, nxt, npar, ntg = k // NTG, u + 1, (k + 1) // NTG % 2, (k + 1) % NTG
            nn = hf * ITEMS + pair * 2 + (k + 1) // NTG
            if first:
                nxt, npar, ntg, nn = u, 0, 0, hf * ITEMS
            gates = beside[1] - 1 if beside and beside[0] == 1 and beside[1] else None
            if not last:
                pe_project(e, 1, BK, s["k_ready"], s["k_done"], nxt, nn, hf, ntg, npar)
            if not first:
                pe_turn_p(e, u, w)
            if gates is not None:
                pe_gate(e, hf, gates)
            if not last:
                pe_project(e, 0, BQ, s["q_ready"], s["q_done"], nxt, nn, hf, ntg, npar)
            if gates is not None:
                pe_turn_gate(e, hf, gates)
            if not first:
                pe_mix(e, u, w)
            if not last:
                pe_scores(e, nxt)
            if gates is not None:
                e.wait_ge(s["gate_read"], hf * NTG + gates + 1)
            if beside:
                pe_norm(e, hf, *beside, 0)
                pe_norm(e, hf, *beside, 1)
            if not last:
                pe_project(e, 2, BV, s["v_ready"], s["v_done"], nxt, nn, hf, ntg, npar)
            if beside:
                pe_norm(e, hf, *beside, 2)
                pe_norm(e, hf, *beside, 3)
                e.wait_ge(s["x_split"], norm_group(hf, *beside) * TPG + 4)
            if not first:
                pe_out(e, u, w, par)
            if not last:
                pe_turn_v(e, nxt)

        units = over_heads(hf, step)
        next(units)
        with e.Fori(1, NHEAD // 2 - 1) as pair:
            for k in range(2 * NTG):
                step("", pair, k)
        for _ in units:
            pass

    def act_attention(e, hf):
        def step(where, pair, k):
            first, last = where == "start", where == "last" and k == 2 * NTG - 1
            beside, _ = norms_beside((where, k))
            u = hf * HU + pair * 2 * NTG + k
            nxt = u if first else u + 1
            gates = beside[1] - 1 if beside and beside[0] == 1 and beside[1] else None
            if not first:
                e.wait_ge(s["p_turned"], u + 1)
                nc.scalar.activation(m["pt"][:, :], BT, ACT.Copy).then_inc(s["pt_ready"], 1)
            if gates is not None:
                act_gate(e, hf, gates)
            if not first and k % NTG < 3:
                cols = WCOLS if where == "last" and k >= NTG else ACOLS
                item_hi(e, hf * ITEMS + pair * 2 + k // NTG + 1, (k // NTG + 1) % 2, cols, k % NTG)
            if not last:
                e.wait_ge(s["q_done"], nxt + 1)
                nc.scalar.activation(m["qt"][:, :], BQ, ACT.Copy).then_inc(s["q_ready"], 1)
            if not first:
                e.wait_ge(s["y_done"], u + 1)
                split_hi(m["yhi"][:, :], BY).then_inc(s["y_hi"], 1)
            if beside:
                act_norm(e, hf, *beside, 0)
                act_norm(e, hf, *beside, 1)
            if not last:
                e.wait_ge(s["row_sub"], nxt + 1)
                nc.scalar.activation(m["sm"][:, :, :], m["sm"][:, :, :], ACT.Exp).then_inc(s["p_exp"], 1)
                e.wait_ge(s["v_done"], nxt + 1)
                nc.scalar.activation(m["vt"][:, :], BV, ACT.Copy).then_inc(s["vt_copied"], 1)
            if beside:
                act_norm(e, hf, *beside, 2)
                act_norm(e, hf, *beside, 3)

        units = over_heads(hf, step)
        next(units)
        with e.Fori(1, NHEAD // 2 - 1) as pair:
            for k in range(2 * NTG):
                step("", pair, k)
        for _ in units:
            pass

    def add_output(e, w, tg, i):
        t = tg * TPG + i
        e.wait_ge(s["o_done"], 4 * w + i + 2)
        nc.vector.tensor_tensor(m["acc"][:, t, :], m["acc"][:, t, :], BO[i], ALU.add).then_inc(s["o_added"], 1)

    def dve_attention(e, hf):
        v = nc.vector
        rows = (slice(0, T), slice(T, P))

        def step(where, pair, k):
            first, last = where == "start", where == "last" and k == 2 * NTG - 1
            beside, after = norms_beside((where, k))
            at = pair * 2 * NTG + k
            u, w = hf * HU + at, hf * (HU + VU) + at
            nxt, tg = (u if first else u + 1), k % NTG
            gates = beside[1] - 1 if beside and beside[0] == 1 and beside[1] else None
            if not last:
                e.wait_ge(s["k_done"], nxt + 1)
                v.tensor_copy(m["kt"][:, :], BK).then_inc(s["k_ready"], 1)
            if beside:
                dve_normalise(e, hf, *beside, 0)
                dve_normalise(e, hf, *beside, 1)
            if gates is not None:
                dve_gate(e, hf, gates)
            if not first:
                e.wait_ge(s["y_hi"], u + 1)
                split_lo(m["ylo"][:, :], BY, m["yhi"][:, :]).then_inc(s["y_split"], 1)
            if not last:
                e.wait_ge(s["s_done"], nxt + 1)
                for r in rows:
                    got = v.scalar_tensor_tensor(m["sm"][r, :, :], pairs(BS)[r, :, r], SCALE,
                                                 m["mask"][r, :].unsqueeze(1).to_broadcast([T, TPG, T]),
                                                 ALU.mult, ALU.add)
                got.then_inc(s["s_read"], 1)
                e.wait_ge(s["s_read"], nxt + 2)
                v.tensor_reduce(m["rmax"][:, :], m["sm"][:, :, :], axis=AX, op=ALU.max).then_inc(s["row_max"], 1)
                e.wait_ge(s["row_max"], nxt + 1)
                v.tensor_tensor(m["sm"][:, :, :], m["sm"][:, :, :], m["rmax"][:, :].unsqueeze(2).to_broadcast([P, TPG, T]),
                                ALU.subtract).then_inc(s["row_sub"], 1)
            if beside:
                dve_norm(e, hf, *beside, 0)
                dve_norm(e, hf, *beside, 1)
                dve_normalise(e, hf, *beside, 2)
                dve_normalise(e, hf, *beside, 3)
            if not last:
                e.wait_ge(s["p_exp"], nxt + 1)
                v.tensor_reduce(m["rsum"][:, :], m["sm"][:, :, :], axis=AX, op=ALU.add).then_inc(s["row_sum"], 1)
                e.wait_ge(s["row_sum"], nxt + 1)
                v.reciprocal(m["rinv"][:, :], m["rsum"][:, :]).then_inc(s["row_inv"], 1)
                e.wait_ge(s["row_inv"], nxt + 1)
                if not first:
                    e.wait_ge(s["p_turned"], u + 1)
                for r in rows:
                    got = v.tensor_tensor(m["prob"][r, :, r], m["sm"][r, :, :],
                                          m["rinv"][r, :].unsqueeze(2).to_broadcast([T, TPG, T]), ALU.mult)
                got.then_inc(s["p_ready"], 1)
            if beside:
                dve_norm(e, hf, *beside, 2)
                dve_norm(e, hf, *beside, 3)
            if not first:
                for i in range(TPG):
                    add_output(e, w, tg, i)
            if not last:
                e.wait_ge(s["v_turned"], nxt + 1)
                v.tensor_copy(m["v"][:, :], BV).then_inc(s["v_ready"], 1)
            if after:
                dve_stats(e, hf, *after)

        for r, c in (rows, rows[::-1]):
            got = v.memset(m["prob"][r, :, c], 0.0)
        units = over_heads(hf, step)
        next(units)
        with e.Fori(1, NHEAD // 2 - 1) as pair:
            for k in range(2 * NTG):
                step("", pair, k)
        for _ in units:
            pass

    RT = NT // 2

    def dve_route(e, hf, part):
        tiles = slice(part * RT, (part + 1) * RT)
        v = nc.vector
        made = [0]

        def link(op):
            made[0] += 1
            op.then_inc(s["route"], 1)
            e.wait_ge(s["route"], (hf * 2 + part) * ROUTE_END + made[0])

        e.wait_ge(s["gate_read"], hf * NTG + 2 * (part + 1))
        gate = m["gate"][:, tiles, :]
        by_e = gate.unsqueeze(3).to_broadcast([P, RT, NEXP, NEXP])
        by_j = gate.unsqueeze(2).to_broadcast([P, RT, NEXP, NEXP])
        link(v.tensor_tensor(m["before"][:, :, :, :], by_j, by_e, ALU.is_gt))
        link(v.tensor_tensor(m["ties"][:, :, :, :], by_j, by_e, ALU.is_equal))
        link(v.tensor_tensor(m["ties"][:, :, :, :], m["ties"][:, :, :, :],
                             m["tri"][:, :, :].unsqueeze(1).to_broadcast([P, RT, NEXP, NEXP]), ALU.mult))
        link(v.tensor_tensor(m["before"][:, :, :, :], m["before"][:, :, :, :], m["ties"][:, :, :, :], ALU.add))
        link(v.tensor_reduce(m["keep"][:, tiles, :], m["before"][:, :, :, :], axis=AX, op=ALU.add))
        link(v.tensor_scalar(m["keep"][:, tiles, :], m["keep"][:, tiles, :], TOPK - 0.5, None, ALU.is_lt))
        link(v.tensor_reduce(m["gmax"][:, tiles], gate, axis=AX, op=ALU.max))
        link(v.tensor_tensor(gate, gate, m["gmax"][:, tiles].unsqueeze(2).to_broadcast([P, RT, NEXP]), ALU.subtract))
        e.wait_ge(s["gate_exp"], hf * 2 + part + 1)
        link(v.tensor_tensor(gate, gate, m["keep"][:, tiles, :], ALU.mult))
        link(v.tensor_reduce(m["gmax"][:, tiles], gate, axis=AX, op=ALU.add))
        link(v.reciprocal(m["gmax"][:, tiles], m["gmax"][:, tiles]))
        link(v.tensor_tensor(m["w8"][:, tiles, 0:TOPK], gate[:, :, 0:TOPK],
                             m["gmax"][:, tiles].unsqueeze(2).to_broadcast([P, RT, TOPK]), ALU.mult))
        link(v.tensor_copy(m["w8hi"][:, tiles, :], m["w8"][:, tiles, :]))
        e.wait_ge(s["w_turned"], hf * NTG + 2 * part + 1)
        link(v.tensor_copy(m["ws"][:, :, 0:NEXP], m["w8hi"][:, tiles, :].bitcast(f32)))
        link(v.tensor_tensor(m["ws"][:, :, 32:32 + NEXP], m["w8"][:, tiles, :], m["w8hi"][:, tiles, :].bitcast(f32), ALU.subtract))
        link(v.tensor_copy(m["ws"][:, :, 64:64 + NEXP], m["w8hi"][:, tiles, :].bitcast(f32)))
        link(v.tensor_copy(m["ws"][:, :, 96:96 + NEXP], m["w8"][:, tiles, :]))
        assert made[0] == ROUTE_END

    ROUTE_SUB, ROUTE_END = 8, 17

    def act_gate_exp(e, hf, part):
        tiles = slice(part * RT, (part + 1) * RT)
        e.wait_ge(s["route"], (hf * 2 + part) * ROUTE_END + ROUTE_SUB)
        nc.scalar.activation(m["gate"][:, tiles, :], m["gate"][:, tiles, :], ACT.Exp).then_inc(s["gate_exp"], 1)

    def act_weights(e, hf, tg):
        e.wait_ge(s["w_turned"], hf * NTG + tg + 2)
        if tg >= 2:
            e.wait_ge(s["w_out"][tg - 2], 16 * (hf + 1))
        nc.scalar.activation(m["w3t"][:, group_cols(tg)], BR[tg % 2], ACT.Copy)
        nc.scalar.activation(m["w8t"][96:128, tg % 2, :], BR[tg % 2][96:128, :], ACT.Copy).then_inc(s["wt_ready"], 1)

    def pe_turn_weights(e, hf, part):
        e.wait_ge(s["route"], (hf * 2 + part + 1) * ROUTE_END)
        for tg in (2 * part, 2 * part + 1):
            if part:
                e.wait_ge(s["wt_ready"], hf * NTG + tg - 1)
            else:
                e.sem_inc(s["turn_pe"], 1)
            for i in range(TPG):
                last = nc.tensor.transpose(BR[tg % 2][:, tile_cols(i)], m["ws"][:, (tg % 2) * TPG + i, :], m["ident"][:, :])
            last.then_inc(s["w_turned"], 1)

    def pe_hidden(e, v, r, n, hf, tg, par, shared, chunks=range(HC)):
        e.wait_ge(s["w_ready"], n + 1)
        e.wait_ge(s["x_split"], hf * 2 * NT + NT + (tg + 1) * TPG + 2)
        for j in chunks:
            for which, bank, done in ((0, BG[j], s["g_done"]), (1, BU[j], s["u_done"])):
                if which and shared:
                    continue
                if which:
                    e.wait_ge(s["u_used"], 2 * r + j + 1)
                else:
                    e.wait_ge(s["g_used"], 2 * v + j + 1)
                for k in range(KC):
                    c = w_hid(k, which, j)
                    last = three(bank, m["whi"][:, par, c], m["wlo"][:, par, c], m["xhi"][:, k, group_cols(tg)],
                                 m["xlo"][:, k, group_cols(tg)], k == 0, k == KC - 1)
                last.then_inc(done, 1)

    def pe_down(e, v, w, k8, par, shared, bias=False):
        slot = k8 % 2
        e.wait_ge(s["hid_split"], 2 * v + 4)
        for i in range(TPG):
            e.wait_ge(s["o_added"], 4 * w + i + 1)
            c = tile_cols(i)
            if bias:
                nc.tensor.matmul(BO[i], m["w3t"][:, tile_cols(k8 % NTG * TPG + i)], m["bd3"][:, :], start=True, stop=False)
            for j in range(HC):
                d = w_down(j, shared)
                last = three(BO[i], m["hhi"][:, slot, j, c], m["hlo"][:, slot, j, c], m["whi"][:, par, d],
                             m["wlo"][:, par, d], j == 0 and not bias, j == HC - 1)
            last.then_inc(s["o_done"], 1)

    def pe_experts(e, hf):
        v0, w0, r0, n0 = hf * VU, hf * (HU + VU) + HU, hf * TOPK * NTG, hf * ITEMS + NHEAD

        def step(at, item, k, shared, next_shared, norm=False, last=False):
            if not last:
                pe_hidden(e, v0 + at + 1, r0 + at + 1, n0 + item + (1 if k % NTG == NTG - 1 else 0), hf,
                          (k + 1) % NTG, (k + 1) // NTG % 2, next_shared)
            if norm:
                pe_norm(e, hf + 1, 0, 0, 0)
                pe_norm(e, hf + 1, 0, 0, 1)
            pe_down(e, v0 + at, w0 + at, k, k // NTG, shared, bias=shared and k >= NTG)
            if norm:
                pe_norm(e, hf + 1, 0, 0, 2)
                pe_norm(e, hf + 1, 0, 0, 3)

        with e.Fori(0, 2) as pair:
            for k in range(8):
                step(pair * 8 + k, pair * 2 + k // NTG, k, False, False)
        for k in range(8):
            step(16 + k, 4 + k // NTG, k, False, k == 7)
        for k in range(8):
            step(24 + k, 6 + k // NTG, k, True, True, norm=k == 6, last=k == 7)

    def act_experts(e, hf):
        v0, r0, n0 = hf * VU, hf * TOPK * NTG, hf * ITEMS + NHEAD

        def hidden(at, k, shared):
            silu(at, k)
            split(at, k, shared)

        def silu(at, k):
            par, v = k // NTG, v0 + at
            for j in range(HC):
                e.wait_ge(s["g_done"], 2 * v + j + 1)
                e.wait_ge(s["hid_split"], 2 * v + j + 1)
                nc.scalar.activation(m["sg"][:, j, :], BG[j], ACT.Silu,
                                     bias=m["ebias"][:, par, j:j + 1]).then_inc(s["g_used"], 1)

        def split(at, k, shared):
            slot, v, r = k % 2, v0 + at, r0 + at
            for j in range(HC):
                if shared:
                    e.wait_ge(s["g_used"], 2 * v + j + 3)
                else:
                    e.wait_ge(s["hd_ready"], 2 * r + j + 5)
                split_hi(m["hhi"][:, slot, j, :], m["sg"][:, j, :]).then_inc(s["hid_hi"], 1)

        def step(at, item, k, next_shared, cols, norm=False, last=False):
            if not last:
                hidden(at + 1, (k + 1) % 8, next_shared)
            if norm:
                for i in range(TPG):
                    act_norm(e, hf + 1, 0, 0, i)
            if k % NTG < 3:
                item_hi(e, n0 + item + 1, (k // NTG + 1) % 2, cols, k % NTG)

        silu(0, 0)
        for tg in (2, 3):
            act_weights(e, hf, tg)
        split(0, 0, False)
        with e.Fori(0, 2) as pair:
            for k in range(8):
                step(pair * 8 + k, pair * 2 + k // NTG, k, False, WCOLS)
        for k in range(8):
            step(16 + k, 4 + k // NTG, k, k == 7, WCOLS if k < NTG else SCOLS)
        for k in range(8):
            step(24 + k, 6 + k // NTG, k, True, SCOLS if k < NTG else ACOLS, norm=k == 6, last=k == 7)

    def dve_experts(e, hf):
        vec = nc.vector
        v0, w0, r0 = hf * VU, hf * (HU + VU) + HU, hf * TOPK * NTG

        def hidden(at, half_at, k, shared):
            par, slot = k // NTG, k % 2
            v, r = v0 + at, r0 + at
            for j in range(HC if not shared else 0):
                e.wait_ge(s["g_used"], 2 * v + j + 3)
                e.wait_ge(s["u_done"], 2 * r + j + 1)
                vec.scalar_tensor_tensor(m["sg"][:, j, :], BU[j], m["ebias"][:, par, HC + j:HC + j + 1],
                                         m["sg"][:, j, :], ALU.add, ALU.mult).then_inc(s["u_used"], 1)
                e.wait_ge(s["u_used"], 2 * r + j + 3)
                e.wait_ge(s["wb_loaded"][slot], 16 * (hf * (TOPK * NTG // 2) + half_at + 1))
                vec.tensor_tensor(m["sg"][:, j, :], m["sg"][:, j, :], m["wb"][:, slot, :], ALU.mult).then_inc(s["hd_ready"], 1)
            for j in range(HC):
                e.wait_ge(s["hid_hi"], 2 * v + j + 1)
                split_lo(m["hlo"][:, slot, j, :], m["sg"][:, j, :], m["hhi"][:, slot, j, :]).then_inc(s["hid_split"], 1)

        def step(at, half_next, k, next_shared, stats=False, norm=False, last=False):
            if not last:
                hidden(at + 1, half_next, (k + 1) % 8, next_shared)
            if norm:
                for i in range(2):
                    dve_normalise(e, hf + 1, 0, 0, i)
                for i in range(2):
                    dve_norm(e, hf + 1, 0, 0, i)
                    dve_normalise(e, hf + 1, 0, 0, i + 2)
            for i in range(TPG):
                add_output(e, w0 + at, k % NTG, i)
            if norm:
                for i in range(2, 4):
                    dve_norm(e, hf + 1, 0, 0, i)
            if stats:
                dve_stats(e, hf + 1, 0, 0)

        hidden(0, 0, 0, False)
        with e.Fori(0, 2) as pair:
            for k in range(8):
                step(pair * 8 + k, pair * 4 + (k + 1) // 2, k, False)
        for k in range(8):
            step(16 + k, 8 + (k + 1) // 2, k, k == 7)
        for k in range(8):
            step(24 + k, None, k, True, stats=k == 5, norm=k == 6, last=k == 7)

    def load_item(e, n, src, cols):
        e.wait_ge(s["w_ready"], n)
        e.dma_start(m["raw"][:, 0:cols], src).then_inc(s["raw_loaded"], 16)

    def load_acc(e, half, tg):
        t0 = half * NT + tg * TPG
        e.dma_start(m["acc"][:, tg * TPG:(tg + 1) * TPG, :],
                    tokens(hbuf)[:, t0:t0 + TPG, :]).then_inc(s["acc_loaded"][tg], 16)

    def tokens(dram):
        return dram.rearrange("c h l -> (c h) l").rearrange("(t p) l -> p t l", p=P)

    def sync(e):
        for half in range(HALVES):
            n0 = half * ITEMS
            if half == 0:
                for tg in range(NTG):
                    load_acc(e, 0, tg)
            with e.Fori(1, NHEAD) as head:
                load_item(e, n0 + head, ins["wattn"][bass.ds(head, 1), :, :].squeeze(0), ACOLS)
            load_item(e, n0 + NHEAD, ins["wexp"][0], WCOLS + 2 * HC)
            for tg in range(NTG):
                e.wait_ge(s["wt_ready"], half * NTG + tg + 1)
                e.dma_start(wscr[half, :, group_cols(tg)], m["w8t"][96:96 + NEXP, tg % 2, :]).then_inc(s["w_out"][tg], 16)
            for tg in range(NTG):
                e.wait_ge(s["w_out"][tg], 16 * (half + 1))

            def weights_back(ex, tg):
                r = (half * TOPK + ex) * NTG + tg
                e.wait_ge(s["hd_ready"], 2 * r + 2)
                e.dma_start(m["wb"][:, tg % 2, :],
                            wscr[half, bass.ds(ex, 1), group_cols(tg)].squeeze(0).partition_broadcast(P))\
                 .then_inc(s["wb_loaded"][tg % 2], 16)

            with e.Fori(0, TOPK - 1) as ex:
                load_item(e, n0 + NHEAD + 1 + ex, ins["wexp"][bass.ds(ex + 1, 1), :, :].squeeze(0), WCOLS + 2 * HC)
                for tg in range(NTG):
                    weights_back(ex, tg)
            load_item(e, n0 + NHEAD + TOPK, ins["wsh"][0], SCOLS + HC)
            for tg in range(NTG):
                weights_back(TOPK - 1, tg)
            load_item(e, n0 + NHEAD + TOPK + 1, ins["wsh"][1], SCOLS + HC)
            load_item(e, n0 + ITEMS, ins["wattn"][0], ACOLS)
            def store_group(tg):
                w = half * (HU + VU) + HU + VU - NTG + tg
                e.wait_ge(s["o_added"], 4 * (w + 1) + 4)
                e.dma_start(tokens(out)[:, half * NT + tg * TPG:half * NT + (tg + 1) * TPG, :],
                            m["acc"][:, tg * TPG:(tg + 1) * TPG, :]).then_inc(s["out_stored"][tg], 16)

            def next_group(tg):
                e.wait_ge(s["out_stored"][tg], 16 * (half + 1))
                if half + 1 < HALVES or tg == 0:
                    load_acc(e, (half + 1) % HALVES, tg)

            store_group(0)
            for tg in range(1, NTG):
                next_group(tg - 1)
                store_group(tg)
            next_group(NTG - 1)
        e.wait_ge(s["raw_loaded"], 16 * (HALVES * ITEMS + 1))
        e.wait_ge(s["acc_loaded"][0], 16 * (HALVES + 1))

    def vector(e):
        dve_stats(e, 0, 0, 0)
        dve_norm_alone(e, 0, 0, 0)
        with e.Fori(0, HALVES) as hf:
            dve_stats(e, hf, 0, 1)
            dve_attention(e, hf)
            dve_route(e, hf, 0)
            dve_norm_alone(e, hf, 1, NTG - 1)
            dve_gate(e, hf, NTG - 1)
            dve_route(e, hf, 1)
            dve_experts(e, hf)

    def scalar(e):
        for i in range(TPG):
            act_norm(e, 0, 0, 0, i)
        with e.Fori(0, HALVES) as hf:
            act_attention(e, hf)
            act_gate(e, hf, NTG - 2)
            act_gate_exp(e, hf, 0)
            for i in range(TPG):
                act_norm(e, hf, 1, NTG - 1, i)
            act_gate(e, hf, NTG - 1)
            for tg in (0, 1):
                act_weights(e, hf, tg)
            act_gate_exp(e, hf, 1)
            act_experts(e, hf)

    def tensor(e):
        for i in range(TPG):
            pe_norm(e, 0, 0, 0, i)
        with e.Fori(0, HALVES) as hf:
            pe_attention(e, hf)
            first = hf * VU, hf * TOPK * NTG, hf * ITEMS + NHEAD, hf, 0, 0, False
            e.wait_ge(s["o_added"], 4 * (hf * (HU + VU) + HU) + 2)
            pe_gate(e, hf, NTG - 2)
            pe_hidden(e, *first, chunks=[0])
            pe_turn_gate(e, hf, NTG - 2)
            e.wait_ge(s["gate_read"], hf * NTG + NTG - 1)
            for i in range(TPG):
                pe_norm(e, hf, 1, NTG - 1, i)
            pe_gate(e, hf, NTG - 1)
            pe_turn_gate(e, hf, NTG - 1)
            pe_turn_weights(e, hf, 0)
            pe_hidden(e, *first, chunks=[1])
            pe_turn_weights(e, hf, 1)
            e.wait_ge(s["wt_ready"], (hf + 1) * NTG)
            e.sem_inc(s["turn_pe"], 1)
            pe_experts(e, hf)

    def gpsimd(e):
        pool_norm(e, 0, 0, 0)
        with e.Fori(0, HALVES) as hf:
            n0 = hf * ITEMS
            for tg in range(1, 3):
                pool_norm(e, hf, 0, tg)
            item_lo(e, n0 + 1, 1, ACOLS, 0, between=[lambda: pool_norm(e, hf, 0, 3)])
            item_lo(e, n0 + 2, 0, ACOLS, 0)
            with e.Fori(1, NHEAD // 2 - 1) as pair:
                for k in range(2):
                    item_lo(e, n0 + pair * 2 + k + 1, (k + 1) % 2, ACOLS, 0)
            item_lo(e, n0 + NHEAD - 1, 1, ACOLS, 0)
            item_lo(e, n0 + NHEAD, 0, WCOLS, 2 * HC,
                    between=[lambda tg=tg: pool_norm(e, hf, 1, tg) for tg in range(2)])
            pool_norm(e, hf, 1, 2)
            pool_norm(e, hf, 1, 3)
            with e.Fori(0, 2) as pair:
                for k in range(2):
                    item_lo(e, n0 + NHEAD + pair * 2 + k + 1, (k + 1) % 2, WCOLS, 2 * HC)
            item_lo(e, n0 + NHEAD + TOPK - 1, 1, WCOLS, 2 * HC)
            for k in range(2):
                item_lo(e, n0 + NHEAD + TOPK + k, k, SCOLS, HC)
            item_lo(e, n0 + ITEMS, 0, ACOLS, 0,
                    between=[lambda: None, lambda: pool_norm(e, hf + 1, 0, 0)])

    def first_item_hi(e, q):
        e.wait_ge(s["raw_loaded"], 16)
        part = bass.ds(q * (ACOLS // NQ), ACOLS // NQ)
        nc.scalar.activation(m["whi"][:, 0, part], m["raw"][:, part], ACT.Copy).then_inc(s["first_hi"], 1)

    def first_item_lo(e, q):
        part = bass.ds(q * (ACOLS // NQ), ACOLS // NQ)
        e.wait_ge(s["first_hi"], q + 1)
        nc.gpsimd.tensor_tensor(m["wlo"][:, 0, part], m["raw"][:, part], m["whi"][:, 0, part].bitcast(f32),
                                ALU.subtract).then_inc(s["first_lo"], 1)

    return dict(sync=sync, vector=vector, scalar=scalar, tensor=tensor, gpsimd=gpsimd,
                first_item_hi=first_item_hi, first_item_lo=first_item_lo)


def program(nc, ins, out):
    hbuf = nc.dram_tensor("hidden_rows", [CH, HD, SEQ], f32, kind="Internal").ap()
    wscr = nc.dram_tensor("routed_weights", [HALVES, NEXP, TH], f32, kind="Internal").ap()

    buffers, sems = {}, {}
    with ExitStack() as ctx:
        buffers.update({n: ctx.enter_context(nc.sbuf_tensor(n, shape, dt)) for n, shape, dt in (
            ("whi", [P, 2, WCOLS], f32r), ("wlo", [P, 2, WCOLS], f32r), ("raw", [P, WCOLS + 2 * HC], f32),
            ("ebias", [P, 2, 2 * HC], f32), ("xn", [P, 2, D], f32),
            ("ident", [P, P], f32), ("mask", [P, T], f32), ("tri", [P, NEXP, NEXP], f32),
            ("neg_half", [P, TPG], f32), ("sign", [P, 1], f32),
            ("stats", [P, TPG, 6], f32), ("mean_var", [P, TPG, 2], f32), ("var_eps", [P, TPG], f32),
            ("rstd", [P, TPG], f32), ("wg_raw", [P, KC, NEXP], f32), ("wg_hi", [P, KC, NEXP], f32r),
            ("wg_lo", [P, KC, NEXP], f32r), ("bg", [P, NEXP], f32), ("bd3", [P, D], f32r),
            ("gate", [P, NT, NEXP], f32), ("keep", [P, NT, NEXP], f32), ("gmax", [P, NT], f32),
            ("w8", [P, NT, NEXP], f32), ("w8hi", [P, NT, NEXP], f32r),
            ("b_all", [P, HD + P - 1], f32), ("hdt", [P, HD + QH], f32), ("rowsum", [P, QH], f32),
            ("alpha", [P, QH], f32), ("norm", [P, QH], f32))})
        at = nc.sbuf_base
        size = 4 * (3 * NT * D + 10 * 1024)
        ctx.enter_context(nc.sbuf_tensor("arena", [P, size // 4], f32))

        def lay(offset, tensors):
            for n, shape, dt in tensors:
                buffers[n] = nc.alloc_sbuf_tensor_at(n, [P] + shape, dt, offset=at + offset)
                offset += -(-4 * int(np.prod(shape)) // 32) * 32
            assert offset <= size
            return offset

        lay(0, (("aat", [2 * HD, NS], f32), ("c_all", [HD, CH], f32),
                ("zmat", [QH, 3 * NS], f32), ("zmat_t", [QH, P], f32), ("xk", [QH, XC], f32),
                ("cy", [QH, P], f32), ("outb", [QH, XC], f32), ("tmp", [QH, NS], f32)))
        work = lay(0, (("acc", [NT, D], f32), ("xhi", [KC, TH], f32r), ("xlo", [KC, TH], f32r)))
        after_att = lay(work, [(n, [TG], f32) for n in ("qt", "kt", "vt", "v", "pt", "gate_t")]
            + [("yhi", [TG], f32r), ("ylo", [TG], f32r), ("prob", [TPG, P], f32), ("sm", [TPG, T], f32),
               ("rmax", [TPG], f32), ("rsum", [TPG], f32), ("rinv", [TPG], f32)])
        after_hid = lay(work, (("sg", [HC, TG], f32), ("hhi", [2, HC, TG], f32r), ("hlo", [2, HC, TG], f32r)))
        lay(work + 20 * 1024, (("before", [NT // 2, NEXP, NEXP], f32), ("ties", [NT // 2, NEXP, NEXP], f32),
                               ("w3t", [TH], f32r), ("ws", [NT // 2, P], f32), ("wb", [2, TG], f32)))
        lay(work + 38 * 1024, (("bd_tmp", [D], f32r),))
        assert max(after_att, after_hid) <= work + 20 * 1024
        buffers["w8t"] = buffers["xn"]
        buffers["bank"] = [ctx.enter_context(nc.psum_tensor(f"bank{i}", [P, 512], f32)) for i in range(8)]

        sems.update({n: ctx.enter_context(nc.semaphore(n)) for n in (
            "const_v", "link", "link_a", "dt_ready", "b_formed", "b_turned", "out_copied", "dve", "act", "pe", "norm_ready", "outb_free",
            "turn_sp", "turn_pool", "turn_dve", "turn_pe", "zeroed", "ident_ready", "consts_ready", "wg_loaded",
            "bg_loaded", "bd_hi", "router_ready",
            "raw_loaded", "first_hi", "first_lo", "w_hi", "w_ready", "ln_stats", "ln_aggr", "ln_eps", "ln_rstd", "xn_ready", "xn_turned",
            "x_hi", "x_split", "gate_done", "gate_copied", "gate_turned", "gate_exp", "route", "w_turned", "wt_ready", "gate_read",
            "q_done", "k_done", "v_done", "s_done", "y_done", "y_hi",
            "q_ready", "k_ready", "v_ready", "pt_ready", "y_split", "s_read", "row_max", "row_sub", "p_exp",
            "row_sum", "row_inv", "p_ready", "p_turned", "vt_copied", "v_turned", "o_done", "o_added",
            "g_done", "u_done", "g_used", "u_used", "hd_ready", "hid_hi", "hid_split")})
        for n, k in (("small_in", 2), ("ssm_in", 3), ("rows_out", 2 * NG), ("acc_loaded", NTG), ("out_stored", NTG),
                     ("w_out", NTG), ("wb_loaded", 2), ("bd_part", 3)):
            sems[n] = [ctx.enter_context(nc.semaphore(f"{n}{i}")) for i in range(k)]

        m, s = buffers, sems
        ssm = ssm_program(nc, ins, hbuf, m, s)
        tok = token_program(nc, ins, hbuf, wscr, out, m, s)
        block = ctx.enter_context(nc.Block())

        @block.sync
        def _(e):
            ssm["sync"](e, lambda: e.dma_start(m["raw"][:, 0:ACOLS], ins["wattn"][0]).then_inc(s["raw_loaded"], 16))
            e.dma_start(m["wg_raw"][:, :, :], ins["wg"]).then_inc(s["wg_loaded"], 16)
            e.dma_start(m["bg"][:, :], ins["bg"].partition_broadcast(P)).then_inc(s["bg_loaded"], 16)
            e.wait_ge(s["zeroed"], 4)
            for k in range(3):
                e.dma_start(m["xn"][32 * k:32 * k + TOPK + 1, 0, :], ins["bdown"]).then_inc(s["bd_part"][k], 16)
            e.sem_inc(s["outb_free"], 1)
            ssm["store"](e)
            tok["sync"](e)

        @block.gpsimd
        def _(e):
            p = nc.gpsimd
            p.memset(m["ident"][:, :], 0.0).then_inc(s["zeroed"], 1)
            p.memset(m["mask"][:, :], 0.0).then_inc(s["zeroed"], 1)
            p.memset(m["tri"][:, :, :], 1.0).then_inc(s["zeroed"], 1)
            p.memset(m["xn"][:, 0, :], 0.0).then_inc(s["zeroed"], 1)
            p.memset(m["w8"][:, :, :], 0.0).then_inc(s["zeroed"], 1)
            e.wait_ge(s["zeroed"], 5)
            p.affine_select(out=m["ident"][:, :], in_=m["ident"][:, :], compare_op=ALU.not_equal, fill=1.0,
                            base=0, pattern=[[-1, P]], channel_multiplier=1).then_inc(s["ident_ready"], 1)
            e.wait_ge(s["ident_ready"], 1)
            for k, r in enumerate((slice(0, T), slice(T, P))):
                p.affine_select(out=m["mask"][r, :], in_=m["mask"][r, :], compare_op=ALU.is_ge, fill=MASKED,
                                base=0, pattern=[[-1, T]], channel_multiplier=1).then_inc(s["zeroed"], 1)
                e.wait_ge(s["zeroed"], 6 + k)
            p.affine_select(out=m["tri"][:, :, :], in_=m["tri"][:, :, :], compare_op=ALU.is_gt, fill=0.0,
                            base=0, pattern=[[1, NEXP], [-1, NEXP]], channel_multiplier=0)
            p.memset(m["neg_half"][:, :], -0.5)
            p.memset(m["w8"][:, :, TOPK:TOPK + 1], 1.0).then_inc(s["consts_ready"], 1)
            e.wait_ge(s["consts_ready"], 1)
            ssm["gpsimd"](e, lambda q: tok["first_item_lo"](e, q))
            e.wait_ge(s["first_lo"], NQ)
            e.sem_inc(s["w_ready"], 1)
            tok["gpsimd"](e)

        @block.vector
        def _(e):
            for sem, credit in ((s["k_ready"], 1), (s["v_ready"], 1),
                                (s["s_read"], 1), (s["out_copied"], NG), (s["x_split"], 2), (s["o_added"], 4), (s["u_used"], 2), (s["hid_split"], 2),
                                (s["hd_ready"], 4)):
                e.sem_inc(sem, credit)
            e.wait_ge(s["consts_ready"], 1)
            ssm["vector"](e)
            e.wait_ge(s["bd_hi"], 2)
            nc.vector.tensor_tensor(m["wg_lo"][:, :, :], m["wg_raw"][:, :, :], m["wg_hi"][:, :, :].bitcast(f32), ALU.subtract)
            nc.vector.tensor_tensor(m["bd3"][64:128, :], m["xn"][64:128, 0, :], m["bd_tmp"][64:128, :].bitcast(f32),
                                    ALU.subtract).then_inc(s["router_ready"], 1)
            nc.vector.memset(m["ws"][:, :, :], 0.0)
            e.wait_ge(s["bg_loaded"], 16)
            tok["vector"](e)

        @block.scalar
        def _(e):
            e.sem_inc(s["g_used"], 2)
            e.sem_inc(s["q_ready"], 1)
            e.sem_inc(s["w_hi"], 3)
            ssm["scalar"](e, lambda q: tok["first_item_hi"](e, q))
            e.wait_ge(s["wg_loaded"], 16)
            nc.scalar.activation(m["wg_hi"][:, :, :], m["wg_raw"][:, :, :], ACT.Copy).then_inc(s["bd_hi"], 1)
            for k in range(3):
                e.wait_ge(s["bd_part"][k], 16)
            nc.scalar.activation(m["bd3"][0:64, :], m["xn"][0:64, 0, :], ACT.Copy)
            nc.scalar.activation(m["bd_tmp"][64:128, :], m["xn"][64:128, 0, :], ACT.Copy).then_inc(s["bd_hi"], 1)
            tok["scalar"](e)

        @block.tensor
        def _(e):
            e.sem_inc(s["o_done"], 1)
            e.sem_inc(s["xn_turned"], 2)
            e.sem_inc(s["w_turned"], 1)
            e.wait_ge(s["ident_ready"], 1)
            ssm["tensor"](e)
            e.wait_ge(s["router_ready"], 1)
            tok["tensor"](e)
    return nc


def kernel(x, L0_tok_A, L0_tok_B, L0_tok_log_dt, L0_attn_Wq, L0_attn_Wk, L0_attn_Wv, L0_attn_Wo, L0_ffn_Wg,
           L0_ffn_bg, L0_ffn_Wgate, L0_ffn_bgate, L0_ffn_Wup, L0_ffn_bup, L0_ffn_Wdown, L0_ffn_bdown,
           L0_ffn_Ws_up, L0_ffn_bs_up, L0_ffn_Ws_down, L0_ffn_bs_down):
    import concourse.bacc as bacc
    from concourse.bass_utils import run_bass_kernel_spmd

    def proj(w):
        return np.asarray(w).reshape(NHEAD, DH, KC, P).transpose(0, 3, 2, 1).reshape(NHEAD, P, KC * DH)

    def up(w):
        return np.asarray(w).reshape(-1, KC, P, HID).transpose(0, 2, 1, 3).reshape(-1, P, KC * HID)

    def down(w):
        return np.asarray(w).reshape(-1, HC, P, D).transpose(0, 2, 1, 3).reshape(-1, P, HC * D)

    def bias(b):
        return np.asarray(b).reshape(-1, HC, P).transpose(0, 2, 1)

    a, b = np.asarray(L0_tok_A), np.asarray(L0_tok_B)
    wo = np.asarray(L0_attn_Wo).reshape(D, NHEAD, DH).transpose(1, 2, 0)
    ws_up = np.asarray(L0_ffn_Ws_up).reshape(D, NSH, HID).transpose(1, 0, 2)
    arrays = {
        "a": a.transpose(3, 1, 0, 2).reshape(P, HD, NS),
        "at": a.transpose(3, 2, 0, 1).reshape(P, HD, NS),
        "b": b.transpose(2, 1, 0).reshape(P, HD),
        "c": np.asarray(x).transpose(3, 2, 1, 0).reshape(P, HD, CH),
        "log_dt": np.asarray(L0_tok_log_dt).reshape(HD),
        "wattn": np.concatenate([proj(L0_attn_Wq), proj(L0_attn_Wk), proj(L0_attn_Wv), wo], axis=2),
        "wexp": np.concatenate([up(L0_ffn_Wgate), up(L0_ffn_Wup), down(L0_ffn_Wdown), bias(L0_ffn_bgate),
                                bias(L0_ffn_bup)], axis=2),
        "wsh": np.concatenate([up(ws_up), down(L0_ffn_Ws_down), bias(L0_ffn_bs_up)], axis=2),
        "wg": np.asarray(L0_ffn_Wg).reshape(KC, P, NEXP).transpose(1, 0, 2),
        "bg": np.asarray(L0_ffn_bg),
        "bdown": np.concatenate([np.asarray(L0_ffn_bdown), np.asarray(L0_ffn_bs_down)[None]], axis=0),
    }
    arrays = {n: np.ascontiguousarray(v) for n, v in arrays.items()}
    nc = bacc.Bacc("TRN2", target_bir_lowering=False, num_devices=1)
    ins = {n: nc.dram_tensor(f"in_{n}", v.shape, mybir.dt.from_np(v.dtype), kind="ExternalInput").ap()
           for n, v in arrays.items()}
    out = nc.dram_tensor("out", [CH, HD, D], f32, kind="ExternalOutput").ap()
    program(nc, ins, out)
    result = run_bass_kernel_spmd(nc, [{f"in_{n}": v for n, v in arrays.items()}], core_ids=[0])
    return result.results[0]["out"]
```
